# Optimizing a Trainium2 kernel written in Bass

```python
import numpy as np
import jax
import jax.numpy as jnp

def _softmax(x, axis=-1):
    return jax.nn.softmax(x, axis=axis)

def _gelu(x):
    return jax.nn.gelu(x, approximate=True)

def _silu(x):
    return jax.nn.silu(x)

def _sigmoid(x):
    return jax.nn.sigmoid(x)

def _layernorm(x, axis=-1, eps=1e-05):
    m = jnp.mean(x, axis=axis, keepdims=True)
    v = jnp.var(x, axis=axis, keepdims=True)
    return (x - m) / jnp.sqrt(v + eps)

def _scatter_add(tgt, idx, src, axis=0):
    return tgt.at[idx].add(src)

def _segment_sum(src, seg, n):
    return jax.ops.segment_sum(src, seg, n)
kernel_name = 'mk_seq_preln_d2_jaxref_r4_506c82'

def setup_inputs(seed: int=0):
    np.random.seed(seed)
    _w = jnp.asarray

    def _L0_attn_setup():
        import jax, jax.numpy as jnp
        import numpy as np
        L, E, H = (4, 256, 16)
        HD = E // H
        EPS_LN = 1e-05

        def _layernorm(x, w, b):
            m = jnp.mean(x, axis=-1, keepdims=True)
            v = jnp.mean((x - m) ** 2, axis=-1, keepdims=True)
            return (x - m) / jnp.sqrt(v + EPS_LN) * w + b

        def _to_quaternion(x):
            p1 = jnp.diff(x, axis=1, prepend=x[:, :1])
            p2 = jnp.roll(x, 1, axis=2)
            p3 = jnp.cos(x)
            return jnp.stack([x, p1, p2, p3], axis=-1)

        def _hamilton(a, b):
            a0, a1, a2, a3 = (a[..., 0], a[..., 1], a[..., 2], a[..., 3])
            b0, b1, b2, b3 = (b[..., 0], b[..., 1], b[..., 2], b[..., 3])
            return jnp.stack([a0 * b0 - a1 * b1 - a2 * b2 - a3 * b3, a0 * b1 + a1 * b0 + a2 * b3 - a3 * b2, a0 * b2 - a1 * b3 + a2 * b0 + a3 * b1, a0 * b3 + a1 * b2 - a2 * b1 + a3 * b0], axis=-1)

        def _spectral_filter(S):
            ks = jnp.fft.fftfreq(S).astype(jnp.float32)[:, None, None]
            kh = jnp.fft.fftfreq(H).astype(jnp.float32)[None, :, None]
            kd = jnp.fft.fftfreq(HD).astype(jnp.float32)[None, None, :]
            km = jnp.sqrt(ks ** 2 + kh ** 2 + kd ** 2 + 1e-10)
            f = jnp.exp(1j * jnp.arctan(jnp.log(km + 1e-10)))
            return f[None, :, :, :, None].astype(jnp.complex64)

        def _modulation(S):
            lam = jnp.arange(S, dtype=jnp.float32) / S
            t = jnp.arange(S, dtype=jnp.float32) * 0.1
            probe = jnp.sin(t + lam)
            phase = t - 2.0 * lam + 0.5 * lam ** 2
            return (probe * jnp.cos(phase))[None, :, None, None]

        def _attention(x, aw, ab, pw, pb):
            B, S, _ = x.shape
            qkv = (x @ aw + ab).reshape(B, S, H, 3 * HD)
            q, k, v = jnp.split(qkv, 3, axis=-1)
            qk = _hamilton(_to_quaternion(q), _to_quaternion(k))
            qkv_p = _hamilton(qk, _to_quaternion(v))
            f = jnp.fft.fftn(qkv_p.astype(jnp.complex64), axes=(-3, -2))
            out = jnp.fft.ifftn(f * _spectral_filter(S), axes=(-3, -2)).real
            a = out[..., 0] * (1.0 + 0.1 * _modulation(S))
            return a.reshape(B, S, E) @ pw + pb

        def _layer(x, p):
            ln1w, ln1b, aw, ab, pw, pb, ln2w, ln2b, fw, fb, mw, mb = p
            x = x + _attention(_layernorm(x, ln1w, ln1b), aw, ab, pw, pb)
            h = _layernorm(x, ln2w, ln2b)
            h = jax.nn.gelu(h @ fw + fb, approximate=False) @ mw + mb
            return x + h
        key = jax.random.key(seed)
        ks = jax.random.split(key, 6)
        s = 0.02
        return {'x': jax.random.normal(ks[0], (2, 512, E), jnp.float32), 'ln1_w': jnp.ones((L, E), jnp.float32), 'ln1_b': jnp.zeros((L, E), jnp.float32), 'attn_w': jax.random.normal(ks[1], (L, E, 3 * E), jnp.float32) * s, 'attn_b': jnp.zeros((L, 3 * E), jnp.float32), 'aproj_w': jax.random.normal(ks[2], (L, E, E), jnp.float32) * s, 'aproj_b': jnp.zeros((L, E), jnp.float32), 'ln2_w': jnp.ones((L, E), jnp.float32), 'ln2_b': jnp.zeros((L, E), jnp.float32), 'fc_w': jax.random.normal(ks[3], (L, E, 4 * E), jnp.float32) * s, 'fc_b': jnp.zeros((L, 4 * E), jnp.float32), 'mproj_w': jax.random.normal(ks[4], (L, 4 * E, E), jnp.float32) * s, 'mproj_b': jnp.zeros((L, E), jnp.float32)}
    _L0_attn_in = _L0_attn_setup()

    def _L0_ffn_setup():
        import jax, jax.numpy as jnp
        import numpy as np
        B, S, H, E = (4, 512, 256, 8)
        key = jax.random.key(seed)
        k1, k2, k3 = jax.random.split(key, 3)
        scale_w = 1.0 / np.sqrt(H)
        return {'x': jax.random.normal(k1, (B, S, H), dtype=jnp.float32), 'router_w': jax.random.normal(k2, (H, E), dtype=jnp.float32) * scale_w, 'router_b': jnp.zeros((E,), dtype=jnp.float32), 'expert_w': jax.random.normal(k3, (E, H, H), dtype=jnp.float32) * scale_w, 'expert_b': jnp.zeros((E, H), dtype=jnp.float32)}
    _L0_ffn_in = _L0_ffn_setup()

    def _L1_attn_setup():
        import jax, jax.numpy as jnp
        import numpy as np
        EMBED = 256
        HEADS = 8
        D1 = 512
        HEAD_DIM = D1 // HEADS
        SEQ = 512
        BATCH = 4
        MAXL = 512
        EPS = 1e-08

        def simple_rms_norm(x, d):
            rms = jnp.linalg.norm(x, axis=-1, keepdims=True) * d ** (-0.5)
            return x / (rms + EPS)

        def toeplitz_causal(v, t_zero, t_pos):
            n = v.shape[2]
            t = jnp.concatenate([t_zero, t_pos[:, :n - 1]], axis=-1)
            m = 2 * n
            vf = jnp.fft.rfft(v, m, axis=2)
            tf = jnp.fft.rfft(t, m, axis=-1)
            y = jnp.fft.irfft(vf * tf[None, :, :, None], m, axis=2)
            return y[:, :, :n]
        key = jax.random.key(seed)
        ks = jax.random.split(key, 9)
        s = 0.02
        return {'x': jax.random.normal(ks[0], (SEQ, BATCH, EMBED), jnp.float32), 'u_w': jax.random.normal(ks[1], (D1, EMBED), jnp.float32) * s, 'u_b': jax.random.normal(ks[2], (D1,), jnp.float32) * s, 'v_w': jax.random.normal(ks[3], (D1, EMBED), jnp.float32) * s, 'v_b': jax.random.normal(ks[4], (D1,), jnp.float32) * s, 'o_w': jax.random.normal(ks[5], (EMBED, D1), jnp.float32) * s, 'o_b': jax.random.normal(ks[6], (EMBED,), jnp.float32) * s, 't_zero': jax.random.normal(ks[7], (HEADS, 1), jnp.float32), 't_pos': jax.random.normal(ks[8], (HEADS, MAXL - 1), jnp.float32)}
    _L1_attn_in = _L1_attn_setup()

    def _L1_ffn_setup():
        import jax, jax.numpy as jnp
        import numpy as np
        B, S, D, F, E = (4, 512, 256, 1024, 8)
        LN_EPS = 1e-05
        key = jax.random.key(seed)
        ks = jax.random.split(key, 6)
        sc = 0.02
        return {'x': jax.random.normal(ks[0], (B, S, D), dtype=jnp.float32), 'Wr': jax.random.normal(ks[1], (D, E), dtype=jnp.float32) * sc, 'br': jnp.zeros((E,), jnp.float32), 'ln_g': jnp.ones((D,), jnp.float32), 'ln_b': jnp.zeros((D,), jnp.float32), 'W1': jax.random.normal(ks[2], (E, D, F), dtype=jnp.float32) * sc, 'b1': jnp.zeros((E, F), jnp.float32), 'W2': jax.random.normal(ks[3], (E, F, D), dtype=jnp.float32) * sc, 'b2': jnp.zeros((E, D), jnp.float32)}
    _L1_ffn_in = _L1_ffn_setup()
    _d = {'L0_attn_x': _L0_attn_in['x'], 'L0_attn_ln1_w': _L0_attn_in['ln1_w'], 'L0_attn_ln1_b': _L0_attn_in['ln1_b'], 'L0_attn_attn_w': _L0_attn_in['attn_w'], 'L0_attn_attn_b': _L0_attn_in['attn_b'], 'L0_attn_aproj_w': _L0_attn_in['aproj_w'], 'L0_attn_aproj_b': _L0_attn_in['aproj_b'], 'L0_attn_ln2_w': _L0_attn_in['ln2_w'], 'L0_attn_ln2_b': _L0_attn_in['ln2_b'], 'L0_attn_fc_w': _L0_attn_in['fc_w'], 'L0_attn_fc_b': _L0_attn_in['fc_b'], 'L0_attn_mproj_w': _L0_attn_in['mproj_w'], 'L0_attn_mproj_b': _L0_attn_in['mproj_b'], 'L0_ffn_router_w': _L0_ffn_in['router_w'], 'L0_ffn_router_b': _L0_ffn_in['router_b'], 'L0_ffn_expert_w': _L0_ffn_in['expert_w'], 'L0_ffn_expert_b': _L0_ffn_in['expert_b'], 'L1_attn_u_w': _L1_attn_in['u_w'], 'L1_attn_u_b': _L1_attn_in['u_b'], 'L1_attn_v_w': _L1_attn_in['v_w'], 'L1_attn_v_b': _L1_attn_in['v_b'], 'L1_attn_o_w': _L1_attn_in['o_w'], 'L1_attn_o_b': _L1_attn_in['o_b'], 'L1_attn_t_zero': _L1_attn_in['t_zero'], 'L1_attn_t_pos': _L1_attn_in['t_pos'], 'L1_ffn_Wr': _L1_ffn_in['Wr'], 'L1_ffn_br': _L1_ffn_in['br'], 'L1_ffn_ln_g': _L1_ffn_in['ln_g'], 'L1_ffn_ln_b': _L1_ffn_in['ln_b'], 'L1_ffn_W1': _L1_ffn_in['W1'], 'L1_ffn_b1': _L1_ffn_in['b1'], 'L1_ffn_W2': _L1_ffn_in['W2'], 'L1_ffn_b2': _L1_ffn_in['b2']}
    _x0 = _d['L0_attn_x']
    _d['L0_attn_x'] = jax.random.normal(jax.random.fold_in(jax.random.key(seed), 1), (1, 4096, 256), dtype=_x0.dtype)
    del _x0
    return _d

def reference(L0_attn_x, L0_attn_ln1_w, L0_attn_ln1_b, L0_attn_attn_w, L0_attn_attn_b, L0_attn_aproj_w, L0_attn_aproj_b, L0_attn_ln2_w, L0_attn_ln2_b, L0_attn_fc_w, L0_attn_fc_b, L0_attn_mproj_w, L0_attn_mproj_b, L0_ffn_router_w, L0_ffn_router_b, L0_ffn_expert_w, L0_ffn_expert_b, L1_attn_u_w, L1_attn_u_b, L1_attn_v_w, L1_attn_v_b, L1_attn_o_w, L1_attn_o_b, L1_attn_t_zero, L1_attn_t_pos, L1_ffn_Wr, L1_ffn_br, L1_ffn_ln_g, L1_ffn_ln_b, L1_ffn_W1, L1_ffn_b1, L1_ffn_W2, L1_ffn_b2):

    def _L0_attn_ref(x, ln1_w, ln1_b, attn_w, attn_b, aproj_w, aproj_b, ln2_w, ln2_b, fc_w, fc_b, mproj_w, mproj_b):
        import jax, jax.numpy as jnp
        import numpy as np
        L, E, H = (4, 256, 16)
        HD = E // H
        EPS_LN = 1e-05

        def _layernorm(x, w, b):
            m = jnp.mean(x, axis=-1, keepdims=True)
            v = jnp.mean((x - m) ** 2, axis=-1, keepdims=True)
            return (x - m) / jnp.sqrt(v + EPS_LN) * w + b

        def _to_quaternion(x):
            p1 = jnp.diff(x, axis=1, prepend=x[:, :1])
            p2 = jnp.roll(x, 1, axis=2)
            p3 = jnp.cos(x)
            return jnp.stack([x, p1, p2, p3], axis=-1)

        def _hamilton(a, b):
            a0, a1, a2, a3 = (a[..., 0], a[..., 1], a[..., 2], a[..., 3])
            b0, b1, b2, b3 = (b[..., 0], b[..., 1], b[..., 2], b[..., 3])
            return jnp.stack([a0 * b0 - a1 * b1 - a2 * b2 - a3 * b3, a0 * b1 + a1 * b0 + a2 * b3 - a3 * b2, a0 * b2 - a1 * b3 + a2 * b0 + a3 * b1, a0 * b3 + a1 * b2 - a2 * b1 + a3 * b0], axis=-1)

        def _spectral_filter(S):
            ks = jnp.fft.fftfreq(S).astype(jnp.float32)[:, None, None]
            kh = jnp.fft.fftfreq(H).astype(jnp.float32)[None, :, None]
            kd = jnp.fft.fftfreq(HD).astype(jnp.float32)[None, None, :]
            km = jnp.sqrt(ks ** 2 + kh ** 2 + kd ** 2 + 1e-10)
            f = jnp.exp(1j * jnp.arctan(jnp.log(km + 1e-10)))
            return f[None, :, :, :, None].astype(jnp.complex64)

        def _modulation(S):
            lam = jnp.arange(S, dtype=jnp.float32) / S
            t = jnp.arange(S, dtype=jnp.float32) * 0.1
            probe = jnp.sin(t + lam)
            phase = t - 2.0 * lam + 0.5 * lam ** 2
            return (probe * jnp.cos(phase))[None, :, None, None]

        def _attention(x, aw, ab, pw, pb):
            B, S, _ = x.shape
            qkv = (x @ aw + ab).reshape(B, S, H, 3 * HD)
            q, k, v = jnp.split(qkv, 3, axis=-1)
            qk = _hamilton(_to_quaternion(q), _to_quaternion(k))
            qkv_p = _hamilton(qk, _to_quaternion(v))
            f = jnp.fft.fftn(qkv_p.astype(jnp.complex64), axes=(-3, -2))
            out = jnp.fft.ifftn(f * _spectral_filter(S), axes=(-3, -2)).real
            a = out[..., 0] * (1.0 + 0.1 * _modulation(S))
            return a.reshape(B, S, E) @ pw + pb

        def _layer(x, p):
            ln1w, ln1b, aw, ab, pw, pb, ln2w, ln2b, fw, fb, mw, mb = p
            x = x + _attention(_layernorm(x, ln1w, ln1b), aw, ab, pw, pb)
            h = _layernorm(x, ln2w, ln2b)
            h = jax.nn.gelu(h @ fw + fb, approximate=False) @ mw + mb
            return x + h
        for i in range(L):
            x = _layer(x, (ln1_w[i], ln1_b[i], attn_w[i], attn_b[i], aproj_w[i], aproj_b[i], ln2_w[i], ln2_b[i], fc_w[i], fc_b[i], mproj_w[i], mproj_b[i]))
        return x

    def _L0_ffn_ref(x, router_w, router_b, expert_w, expert_b):
        import jax, jax.numpy as jnp
        import numpy as np
        B, S, H, E = (4, 512, 256, 8)
        b, s, h = x.shape
        xt = x.reshape(b * s, h)
        logits = xt @ router_w + router_b
        probs = jax.nn.softmax(logits, axis=-1)
        gate = jnp.max(probs, axis=-1)
        idx = jnp.argmax(probs, axis=-1)
        out_all = jnp.einsum('th,ehd->ted', xt, expert_w) + expert_b[None, :, :]
        e_out = jnp.take_along_axis(out_all, idx[:, None, None], axis=1)[:, 0, :]
        y = gate[:, None] * e_out
        return y.reshape(b, s, h)

    def _L1_attn_ref(x, u_w, u_b, v_w, v_b, o_w, o_b, t_zero, t_pos):
        import jax, jax.numpy as jnp
        import numpy as np
        EMBED = 256
        HEADS = 8
        D1 = 512
        HEAD_DIM = D1 // HEADS
        SEQ = 512
        BATCH = 4
        MAXL = 512
        EPS = 1e-08

        def simple_rms_norm(x, d):
            rms = jnp.linalg.norm(x, axis=-1, keepdims=True) * d ** (-0.5)
            return x / (rms + EPS)

        def toeplitz_causal(v, t_zero, t_pos):
            n = v.shape[2]
            t = jnp.concatenate([t_zero, t_pos[:, :n - 1]], axis=-1)
            m = 2 * n
            vf = jnp.fft.rfft(v, m, axis=2)
            tf = jnp.fft.rfft(t, m, axis=-1)
            y = jnp.fft.irfft(vf * tf[None, :, :, None], m, axis=2)
            return y[:, :, :n]
        shortcut = x
        xn = simple_rms_norm(x, EMBED)
        u = jax.nn.silu(xn @ u_w.T + u_b)
        v = jax.nn.silu(xn @ v_w.T + v_b)
        n, b, _ = v.shape
        vh = v.reshape(n, b, HEADS, HEAD_DIM).transpose(1, 2, 0, 3)
        y = toeplitz_causal(vh, t_zero, t_pos)
        y = y.transpose(2, 0, 1, 3).reshape(n, b, D1)
        out = u * y
        out = out @ o_w.T + o_b + shortcut
        return out

    def _L1_ffn_ref(x, Wr, br, ln_g, ln_b, W1, b1, W2, b2):
        import jax, jax.numpy as jnp
        import numpy as np
        B, S, D, F, E = (4, 512, 256, 1024, 8)
        LN_EPS = 1e-05
        tokens_shape = x.shape[:-1]
        xt = x.reshape(-1, x.shape[-1])
        router_logits = xt @ Wr + br
        router_probs = jax.nn.softmax(router_logits, axis=-1)
        gates = jnp.max(router_probs, axis=-1, keepdims=True)
        idx = jnp.argmax(router_probs, axis=-1)
        onehot = jax.nn.one_hot(idx, E, dtype=xt.dtype)
        mu = jnp.mean(xt, axis=-1, keepdims=True)
        var = jnp.mean(jnp.square(xt - mu), axis=-1, keepdims=True)
        xn = (xt - mu) * jax.lax.rsqrt(var + LN_EPS) * ln_g + ln_b
        h = jnp.einsum('te,td,edf->tf', onehot, xn, W1) + b1[idx]
        h = jax.nn.relu(h)
        y = jnp.einsum('te,tf,efd->td', onehot, h, W2) + b2[idx]
        y = y * gates
        return y.reshape(tokens_shape + (y.shape[-1],))
    x = L0_attn_x
    x = x + _L0_attn_ref(_layernorm(x, axis=-1), L0_attn_ln1_w, L0_attn_ln1_b, L0_attn_attn_w, L0_attn_attn_b, L0_attn_aproj_w, L0_attn_aproj_b, L0_attn_ln2_w, L0_attn_ln2_b, L0_attn_fc_w, L0_attn_fc_b, L0_attn_mproj_w, L0_attn_mproj_b)
    x = x + _L0_ffn_ref(_layernorm(x, axis=-1), L0_ffn_router_w, L0_ffn_router_b, L0_ffn_expert_w, L0_ffn_expert_b)
    x = x + _L1_attn_ref(_layernorm(x, axis=-1), L1_attn_u_w, L1_attn_u_b, L1_attn_v_w, L1_attn_v_b, L1_attn_o_w, L1_attn_o_b, L1_attn_t_zero, L1_attn_t_pos)
    x = x + _L1_ffn_ref(_layernorm(x, axis=-1), L1_ffn_Wr, L1_ffn_br, L1_ffn_ln_g, L1_ffn_ln_b, L1_ffn_W1, L1_ffn_b1, L1_ffn_W2, L1_ffn_b2)
    return x

_drawn_inputs = setup_inputs


def setup_inputs(seed=0):
    import zlib

    import numpy as np

    out = dict(_drawn_inputs(seed))
    spreads = {'L0_attn_ln1_w': (1.0, 0.2),
     'L0_attn_ln1_b': (0.0, 0.29),
     'L0_attn_attn_b': (0.0, 0.1),
     'L0_attn_aproj_b': (0.0, 0.1),
     'L0_attn_ln2_w': (1.0, 0.2),
     'L0_attn_ln2_b': (0.0, 0.412),
     'L0_attn_fc_b': (0.0, 0.1),
     'L0_attn_mproj_b': (0.0, 0.1),
     'L0_ffn_router_b': (0.0, 0.1),
     'L0_ffn_expert_b': (0.0, 0.43),
     'L1_ffn_br': (0.0, 0.8),
     'L1_ffn_ln_g': (1.0, 0.6),
     'L1_ffn_ln_b': (0.0, 2.0),
     'L1_ffn_b1': (0.0, 2.0),
     'L1_ffn_b2': (0.0, 2.0)}
    factors = {'L1_attn_u_w': 8.0,
     'L1_attn_u_b': 8.0,
     'L1_attn_v_w': 8.0,
     'L1_attn_v_b': 8.0,
     'L1_attn_o_w': 8.0,
     'L1_attn_o_b': 200.0,
     'L1_attn_t_zero': 8.0,
     'L1_ffn_Wr': 5.329,
     'L1_ffn_W1': 7.317,
     'L1_ffn_W2': 5.892}
    for name, (base, spread) in spreads.items():
        noise = np.random.default_rng([zlib.crc32(name.encode()), seed]).standard_normal(out[name].shape)
        drawn = base * np.exp(spread * noise) if base else spread * noise
        out[name] = jnp.asarray(drawn.astype(out[name].dtype))
    for name, factor in factors.items():
        out[name] = (out[name] * factor).astype(out[name].dtype)
    return out
```

```python
from contextlib import ExitStack

import concourse.bass as bass
from concourse import mybir

F32 = mybir.dt.float32
ALU = mybir.AluOpType
ACT = mybir.ActivationFunctionType
AX_X = mybir.AxisListType.X

P = 128
S = 4096
E = 256
EH = E // P
L = 4
H = 16
HD = E // H
QW = 3 * HD
CT = 4
CW = CT * P
NC = S // CW
NT = S // P
NG = L * NC
F = 4 * E
FC = F // P
NX = 8
D1 = 512
MC = D1 // P
HW1 = H + 1
W2 = 3 * E // 2
EPS = 1e-5
TURN = 0.15915494309189535
ROUND = 12582912.0
TWO_PI = 6.2831845


def shape_constants():
    import numpy as np

    h = np.arange(H)
    base = np.zeros((H, H))
    for k in range(H // 2 + 1):
        g = np.sqrt(1 / H) if k in (0, H // 2) else np.sqrt(2 / H)
        base[:, k] = g * np.cos(2 * np.pi * h * k / H)
        if 0 < k < H // 2:
            base[:, H // 2 + k] = g * np.sin(2 * np.pi * h * k / H)
    one = np.float32
    k = np.fft.fftfreq(H).astype(one)[[*range(H // 2 + 1), *range(1, H // 2)]]
    ks = np.fft.fftfreq(S).astype(one)[:, None, None]
    km = np.sqrt(ks ** 2 + k[None, :, None] ** 2 + k[None, None, :] ** 2 + one(1e-10))
    filt = np.cos(np.arctan(np.log(km + one(1e-10)).astype(np.float64))).reshape(S, E)
    lam = np.arange(S, dtype=one) / one(S)
    t = np.arange(S, dtype=one) * one(0.1)
    phase = t - one(2) * lam + one(0.5) * lam ** 2
    mod = 1 + 0.1 * (np.sin((t + lam).astype(np.float64)) * np.cos(phase.astype(np.float64)))
    scale = (filt * mod[:, None]).reshape(NC, P, CT, EH, P).transpose(4, 3, 0, 2, 1)
    return {
        "c_heads": np.kron(base, base).astype(one),
        "c_filter": np.ascontiguousarray(scale.reshape(P, EH, S)).astype(one),
        "c_prio": np.arange(NX, 0, -1).astype(one),
        "c_ident": np.eye(P, dtype=one),
    }


def attention(nc, d, x, ident, bank):
    with ExitStack() as ctx:
        def sb(name, *shape):
            return ctx.enter_context(nc.sbuf_tensor(name, [P, *shape], F32))

        filt = sb("filt", EH, S)
        heads = sb("heads", EH, E)
        at_w = sb("at_w", EH, 3 * E)
        back_w = sb("back_w", L, EH, E)
        fc_w = sb("fc_w", EH, F)
        mp_w = sb("mp_w", FC, E)
        at_b = sb("at_b", 3 * E)
        ap_b = sb("ap_b", E)
        mp_b = sb("mp_b", E)
        fc_b = sb("fc_b", FC)
        ln1 = sb("ln1", 2, EH)
        ln2 = sb("ln2", 2, EH)
        xn = sb("xn", CT, E)
        xt1 = sb("xt1", EH, CW)
        xt2 = sb("xt2", EH, CW)
        qkv = sb("qkv", 2 * CT, HW1, QW)
        dif = sb("dif", 2, 2, H, QW)
        cosv = sb("cosv", 2, 2, H, QW)
        whole = sb("whole", H, QW)
        ham = sb("ham", CT, E)
        hb = [sb(f"hb{i}", 2, HW1 if i == 0 else H, HD) for i in range(6)]
        ham_t = sb("ham_t", EH, CW)
        coef = sb("coef", EH, CW)
        hid = sb("hid", FC, CW)
        stat = sb("stat", CT, 6)
        mv1 = sb("mv1", CT, 2)
        mv2 = sb("mv2", CT, 2)
        rs1 = sb("rs1", CT)
        rs2 = sb("rs2", CT)
        ve = sb("ve", CT)
        half = sb("half", CT)

        names = """x_in0 x_rest ident_in heads_in ap_in filt_in at_w_in at_s_in fc_w_in mp_w_in mp_s_in
            before_in back_pe back_act t1_pe t1_act qkv_pe qkv_act added biased pool_step prep cosd
            ham_step ham_done tp_pe tp_act r_pe filt_dve g_pe res1 var1 rs1_pool ln1_done var2 rs2_pool
            ln2_done t2_pe t2_act fc_pe gelu mm_pe res2 pb_done mb_done eps held_pool held_sp zeroed""".split()
        s = {n: ctx.enter_context(nc.semaphore(n)) for n in names}

        rows = "b (c p t) e -> p (b c) t e"
        x_in = d["L0_attn_x"].rearrange(rows, p=P, t=CT)
        xc = x[:, :, :].rearrange("p (c t) e -> p c t e", t=CT)

        def hold(eng, what, value):
            if isinstance(value, int) and value <= 0:
                return
            eng.wait_ge(what, value)
            if not isinstance(value, int):
                eng.sem_inc(s["held_pool" if eng.engine == mybir.EngineType.Pool else "held_sp"], 1)

        def after(eng, what, value):
            if not isinstance(value, int) or value > 0:
                eng.wait_ge(what, value)

        def steps(eng, step):
            for n in range(-1, 8):
                step(n, n % 2)
            with eng.Fori(4, 15) as pair:
                step(2 * pair, 0)
                step(2 * pair + 1, 1)
            for n in range(NG - 2, NG + 4):
                step(n, n % 2)

        def on(g):
            return not isinstance(g, int) or 0 <= g < NG

        block = ctx.enter_context(nc.Block())

        @block.sync
        def _(sp):
            def by_channel(to, name, l, done):
                sp.dma_start(to, d[name][l].rearrange("(k p) -> p k", p=P),
                             allow_slow_non_contiguous=True).then_inc(s[done], 16)

            def matrix(to, name, l, done):
                sp.dma_start(to, d[name][l].rearrange("(k p) n -> p k n", p=P)).then_inc(s[done], 16)

            def load_attention(l):
                matrix(at_w[:, :, :], "L0_attn_attn_w", l, "at_w_in")
                sp.dma_start(at_b[:, :], d["L0_attn_attn_b"][l].partition_broadcast(P)).then_inc(s["at_s_in"], 16)
                sp.dma_start(ap_b[:, :], d["L0_attn_aproj_b"][l].partition_broadcast(P)).then_inc(s["at_s_in"], 16)
                by_channel(ln1[:, 0, :], "L0_attn_ln1_w", l, "at_s_in")
                by_channel(ln1[:, 1, :], "L0_attn_ln1_b", l, "at_s_in")

            def load_mlp(l):
                matrix(fc_w[:, :, :], "L0_attn_fc_w", l, "fc_w_in")
                by_channel(fc_b[:, :], "L0_attn_fc_b", l, "fc_w_in")
                by_channel(ln2[:, 0, :], "L0_attn_ln2_w", l, "fc_w_in")
                by_channel(ln2[:, 1, :], "L0_attn_ln2_b", l, "fc_w_in")
                hold(sp, s["mm_pe"], 2 * NC * l)
                hold(sp, s["mb_done"], NC * l)
                matrix(mp_w[:, :, :], "L0_attn_mproj_w", l, "mp_w_in")
                sp.dma_start(mp_b[:, :], d["L0_attn_mproj_b"][l].partition_broadcast(P)).then_inc(s["mp_s_in"], 16)

            def load_before(g, parity, start):
                hold(sp, s["biased"], CT * g + CT)
                hold(sp, s["ham_done"], 2 * g - 1)
                last = qkv[:, CT * parity + CT - 1, 1:HW1, :]
                sp.dma_start(dif[1:P, 0, 0, :, :], last[0:P - 1]).then_inc(s["before_in"], 16)
                first = qkv[0:1, 0, 1:HW1, :] if start else qkv[P - 1:P, CT * (1 - parity) + CT - 1, 1:HW1, :]
                sp.dma_start(dif[0:1, 0, 0, :, :], first).then_inc(s["before_in"], 16)

            def layer(l):
                load_before(NC * l, 0, True)
                load_before(NC * l + 1, 1, False)
                load_before(NC * l + 2, 0, False)
                if not isinstance(l, int):
                    hold(sp, s["fc_pe"], FC * NC * l)
                    hold(sp, s["gelu"], FC * NC * l)
                    load_mlp(l)
                load_before(NC * l + 3, 1, False)
                with sp.Fori(2, NC // 2) as pair:
                    load_before(NC * l + 2 * pair, 0, False)
                    load_before(NC * l + (2 * pair + 1), 1, False)

            sp.dma_start(xc[:, 0], x_in[:, 0]).then_inc(s["x_in0"], 16)
            sp.dma_start(ident[:, :], d["c_ident"]).then_inc(s["ident_in"], 16)
            load_attention(0)
            for c in range(1, NC):
                sp.dma_start(xc[:, c], x_in[:, c]).then_inc(s["x_rest"], 16)
            sp.dma_start(heads[:, :, :], d["c_heads"].rearrange("(k p) n -> p k n", p=P)).then_inc(s["heads_in"], 16)
            for l in range(L):
                sp.dma_start(hid[:, 2 * l:2 * l + 2, 0:E],
                             d["L0_attn_aproj_w"][l].rearrange("(k p) n -> p k n", p=P)).then_inc(s["ap_in"], 16)
            load_mlp(0)
            sp.dma_start(filt[:, :, :], d["c_filter"]).then_inc(s["filt_in"], 16)
            layer(0)
            with sp.Fori(1, L) as l:
                hold(sp, s["qkv_pe"], 8 * NC * l)
                hold(sp, s["t1_act"], NC * l)
                hold(sp, s["biased"], CT * NC * l)
                hold(sp, s["pb_done"], NC * l)
                load_attention(l)
                layer(l)

        @block.tensor
        def _(pe):
            def turn(rows_of, done):
                for e in range(EH):
                    for t in range(CT):
                        mm = pe.transpose(bank[e][:, t * P:(t + 1) * P], rows_of[:, t, e * P:(e + 1) * P], ident[:, :])
                mm.then_inc(s[done], 1)

            def compose_back():
                pe.wait_ge(s["heads_in"], 16)
                pe.wait_ge(s["ap_in"], 16 * L)
                for l in range(L):
                    for e in range(EH):
                        for k in range(EH):
                            mm = pe.matmul(bank[2 + l][:, e * E:(e + 1) * E], heads[:, k, e * P:(e + 1) * P],
                                           hid[:, 2 * l + k, 0:E], start=(k == 0), stop=(k == EH - 1))
                mm.then_inc(s["back_pe"], 1)

            def step(n, parity):
                if on(n - 2):
                    after(pe, s["ham_done"], 2 * (n - 1))
                    after(pe, s["t1_act"], n + 1 if not isinstance(n, int) else min(n + 1, NG))
                    turn(ham, "tp_pe")
                if on(n):
                    after(pe, s["t1_act"], n + 1)
                    after(pe, s["at_w_in"], 16 * (n // NC + 1))
                    after(pe, s["filt_dve"], n - 2)
                    for t in range(CT):
                        for j in range(2):
                            if t:
                                after(pe, s["qkv_act"], 8 * n + (2 * t + j - 1))
                            for k in range(EH):
                                mm = pe.matmul(bank[6 + j][:, 0:W2], xt1[:, k, t * P:(t + 1) * P],
                                               at_w[:, k, W2 * j:W2 * j + W2], start=(k == 0), stop=(k == EH - 1))
                            mm.then_inc(s["qkv_pe"], 1)
                if on(n - 3):
                    after(pe, s["ln2_done"], n - 2)
                    after(pe, s["tp_act"], n - 1 if not isinstance(n, int) else min(n - 1, NG))
                    turn(xn, "t2_pe")
                if on(n - 2):
                    after(pe, s["tp_act"], n - 1)
                    if on(n):
                        after(pe, s["qkv_act"], 8 * n + 8)
                    else:
                        after(pe, s["filt_dve"], n - 2)
                    for e in range(EH):
                        for k in range(EH):
                            mm = pe.matmul(bank[6 + e][:, :], heads[:, k, e * P:(e + 1) * P], ham_t[:, k, :],
                                           start=(k == 0), stop=(k == EH - 1))
                    mm.then_inc(s["r_pe"], 1)
                if on(n - 3):
                    after(pe, s["t2_act"], n - 2)
                    after(pe, s["fc_w_in"], 64 * ((n - 3) // NC + 1))
                    after(pe, s["res1"], n - 2)
                    for f in range(FC):
                        if f > 1:
                            after(pe, s["gelu"], FC * (n - 3) + (f - 1))
                        for k in range(EH):
                            mm = pe.matmul(bank[2 + f % 2][:, :], fc_w[:, k, f * P:(f + 1) * P], xt2[:, k, :],
                                           start=(k == 0), stop=(k == EH - 1))
                        mm.then_inc(s["fc_pe"], 1)
                if on(n + 1):
                    after(pe, s["ln1_done"], n + 2)
                    after(pe, s["t2_act"], n - 2)
                    after(pe, s["tp_act"], n - 1)
                    turn(xn, "t1_pe")
                if isinstance(n, int) and n == 1:
                    compose_back()
                if isinstance(n, int) and n == 2:
                    pe.wait_ge(s["back_act"], 1)
                if on(n - 3):
                    after(pe, s["gelu"], FC * (n - 2))
                if on(n - 2):
                    after(pe, s["filt_dve"], n - 1)
                    for b in range(2):
                        for t in range(2):
                            at = (2 * b + t) * P
                            for k in range(EH):
                                mm = pe.matmul(bank[2 + b][:, t * E:(t + 1) * E], coef[:, k, at:at + P],
                                               back_w[:, bass.ds((n - 2) // NC, 1), k, :].rearrange("p l e -> p (l e)"),
                                               start=(k == 0), stop=(k == EH - 1))
                    mm.then_inc(s["g_pe"], 1)
                if on(n - 3):
                    after(pe, s["mp_w_in"], 16 * ((n - 3) // NC + 1))
                    after(pe, s["res2"], n - 3)
                    for b in range(2):
                        for t in range(2):
                            at = (2 * b + t) * P
                            for f in range(FC):
                                mm = pe.matmul(bank[4 + b][:, t * E:(t + 1) * E], hid[:, f, at:at + P],
                                               mp_w[:, f, :], start=(f == 0), stop=(f == FC - 1))
                        mm.then_inc(s["mm_pe"], 1)

            pe.wait_ge(s["ident_in"], 16)
            steps(pe, step)

        @block.scalar
        def _(act):
            def turned(ln, to, done):
                for e in range(EH):
                    ins = nc.scalar.activation(to[:, e, :], bank[e][:, :], ACT.Identity,
                                               bias=ln[:, 1, e:e + 1], scale=ln[:, 0, e:e + 1])
                ins.then_inc(s[done], 1)

            def sine(half_index, b):
                after(act, s["prep"], half_index + 1)
                nc.scalar.activation(cosv[:, b, :, :, :], cosv[:, b, :, :, :], ACT.Sin,
                                     scale=TWO_PI).then_inc(s["cosd"], 1)

            def step(n, parity):
                if on(n - 2):
                    after(act, s["tp_pe"], n - 1)
                    for e in range(EH):
                        ins = nc.scalar.activation(ham_t[:, e, :], bank[e][:, :], ACT.Copy)
                    ins.then_inc(s["tp_act"], 1)
                if on(n):
                    after(act, s["ham_done"], 2 * (n - 1))
                    for t in range(CT):
                        for j in range(2):
                            after(act, s["qkv_pe"], 8 * n + (2 * t + j + 1))
                            to = qkv[:, CT * parity + t, 1 + 8 * j:9 + 8 * j, :]
                            nc.scalar.activation(to.rearrange("p h w -> p (h w)"), bank[6 + j][:, 0:W2],
                                                 ACT.Copy).then_inc(s["qkv_act"], 1)
                if on(n - 3):
                    after(act, s["fc_w_in"], 64 * ((n - 3) // NC + 1))
                    after(act, s["t2_pe"], n - 2)
                    turned(ln2, xt2, "t2_act")
                if on(n - 1):
                    sine(2 * (n - 1) + 1, 1)
                if on(n - 3):
                    for f in range(FC):
                        after(act, s["fc_pe"], FC * (n - 3) + (f + 1))
                        if f == 0:
                            after(act, s["mm_pe"], 2 * (n - 3))
                        nc.scalar.activation(hid[:, f, :], bank[2 + f % 2][:, :], ACT.Gelu,
                                             bias=fc_b[:, f:f + 1]).then_inc(s["gelu"], 1)
                if on(n + 1):
                    after(act, s["at_s_in"], 64 * ((n + 1) // NC + 1))
                    after(act, s["t1_pe"], n + 2)
                    after(act, s["qkv_pe"], 8 * n + 8)
                    turned(ln1, xt1, "t1_act")
                if on(n):
                    sine(2 * n, 0)
                if isinstance(n, int) and n == 1:
                    act.wait_ge(s["back_pe"], 1)
                    for l in range(L):
                        ins = nc.scalar.activation(back_w[:, l, :, :].rearrange("p k n -> p (k n)"),
                                                   bank[2 + l][:, :], ACT.Copy)
                    ins.then_inc(s["back_act"], 1)

            steps(act, step)

        @block.gpsimd
        def _(pool):
            def minus(o, a, b):
                return nc.gpsimd.tensor_tensor(o, a, b, ALU.subtract)

            def plus(o, a, b):
                return nc.gpsimd.tensor_tensor(o, a, b, ALU.add)

            def copy(o, a):
                return nc.gpsimd.tensor_scalar(o, a, 1.0, 1.0, ALU.mult, ALU.mult)

            def prep(i, b, parity):
                a = CT * parity + 2 * b
                hold(pool, s["ham_done"], i - 1)
                if b:
                    minus(dif[:, b, :, :, :], qkv[:, a:a + 2, 1:HW1, :], qkv[:, a - 1:a + 1, 1:HW1, :])
                else:
                    minus(dif[:, b, 1, :, :], qkv[:, a + 1, 1:HW1, :], qkv[:, a, 1:HW1, :])
                    hold(pool, s["before_in"], 16 * i + 32)
                    minus(dif[:, b, 0, :, :], qkv[:, a, 1:HW1, :], dif[:, b, 0, :, :])
                k = s["pool_step"]
                nc.gpsimd.tensor_scalar(cosv[:, b, :, :, :], qkv[:, a:a + 2, 1:HW1, :], TURN, 0.25,
                                        ALU.mult, ALU.add).then_inc(k, 1)
                hold(pool, s["prep"], i)
                hold(pool, k, 4 * i + 1)
                for t in range(2):
                    part = cosv[:, b, t, :, :]
                    if t:
                        hold(pool, k, 4 * i + 3)
                    nc.gpsimd.tensor_scalar(whole[:, :, :], part, ROUND, ROUND, ALU.add, ALU.subtract).then_inc(k, 1)
                    hold(pool, k, 4 * i + (2 + 2 * t))
                    ins = minus(part, part, whole[:, :, :])
                    ins.then_inc(s["prep"] if t else k, 1)

            def rstd(n_eps, mv, rs, done):
                nc.gpsimd.tensor_scalar(ve[:, :], mv[:, :, 1], EPS, 0.0, ALU.add, ALU.add).then_inc(s["eps"], 1)
                hold(pool, s["eps"], n_eps)
                nc.gpsimd.tensor_tensor(rs[:, :], ve[:, :], half[:, :], ALU.pow).then_inc(s[done], 1)

            def add_row(g, b, done):
                now = xc[:, bass.ds(g % NC, 1), :, :].rearrange("p c t e -> p (c t) e")
                nc.gpsimd.tensor_tensor(now, now, b[:, :].unsqueeze(1).broadcast_to([P, CT, E]),
                                        ALU.add).then_inc(s[done], 1)

            def step(n, parity):
                ones = lambda g: g + 1 + (min(g + 1, NC) if isinstance(g, int) else NC)
                if on(n + 1):
                    g = n + 1
                    twos = max(0, min(n - 2, NG)) if isinstance(n, int) else n - 2
                    if isinstance(g, int) and g < NC:
                        hold(pool, s["var1"], ones(g) - 1)
                        rstd(ones(g) - 1 + twos, mv1, rs1, "rs1_pool")
                        hold(pool, s["rs1_pool"], ones(g) - 1)
                    hold(pool, s["var1"], ones(g))
                    rstd(ones(g) + twos, mv1, rs1, "rs1_pool")
                    hold(pool, s["rs1_pool"], ones(g))
                if on(n - 1):
                    prep(2 * (n - 1) + 1, 1, 1 - parity)
                if on(n - 3):
                    hold(pool, s["mp_s_in"], 16 * ((n - 3) // NC + 1))
                    hold(pool, s["ln2_done"], n - 2)
                    add_row(n - 3, mp_b, "mb_done")
                if on(n):
                    hold(pool, s["at_s_in"], 64 * (n // NC + 1))
                    hold(pool, s["ln1_done"], n + 1)
                    add_row(n, ap_b, "pb_done")
                    for t in range(CT):
                        a = CT * parity + t
                        rows_of = qkv[:, a, 1:HW1, :].rearrange("p h w -> p (h w)")
                        hold(pool, s["qkv_act"], 8 * n + (2 * t + 2))
                        plus(rows_of, rows_of, at_b[:, :]).then_inc(s["added"], 1)
                        hold(pool, s["added"], CT * n + (t + 1))
                        copy(qkv[:, a, 0, :], qkv[:, a, H, :]).then_inc(s["biased"], 1)
                    hold(pool, s["biased"], CT * n + CT)
                    prep(2 * n, 0, parity)
                if on(n - 2):
                    hold(pool, s["var2"], n - 1)
                    g1 = min(n + 2, NG) if isinstance(n, int) else n + 2
                    done1 = g1 + (min(g1, NC) if isinstance(n, int) else NC)
                    rstd(done1 + (n - 1), mv2, rs2, "rs2_pool")
                    hold(pool, s["rs2_pool"], n - 1)

            nc.gpsimd.memset(half[:, :], -0.5).then_inc(s["zeroed"], 1)
            pool.wait_ge(s["zeroed"], 1)
            steps(pool, step)

        @block.vector
        def _(dve):
            def tile(g, t):
                return xc[:, bass.ds(g % NC, 1), t, :].rearrange("p c e -> p (c e)")

            def stats(g, mv, done):
                dve.drain()
                for t in range(CT):
                    nc.vector.bn_stats(stat[:, t, :], tile(g, t))
                dve.drain()
                for t in range(CT):
                    ins = nc.vector.bn_aggr(mv[:, t, :], stat[:, t, :])
                ins.then_inc(s[done], 1)

            def norm(g, to, mv, rs, done=None):
                for t in range(CT):
                    ins = nc.vector.tensor_scalar(to(t), tile(g, t), mv[:, t, 0:1], rs[:, t:t + 1],
                                                  ALU.subtract, ALU.mult)
                if done is not None:
                    ins.then_inc(s[done], 1)

            def add_banks(g, b0, done, each):
                for b in range(2):
                    each(b)
                    now = xc[:, bass.ds(g % NC, 1), 2 * b:2 * b + 2, :].rearrange("p c t e -> p (c t e)")
                    ins = nc.vector.tensor_tensor(now, now, bank[b0 + b][:, :], ALU.add)
                ins.then_inc(s[done], 1)

            def hamilton(g, b, parity):
                i = 2 * g + b
                a = CT * parity + 2 * b
                ext = lambda j: qkv[:, a:a + 2, :, HD * j:HD * j + HD]
                quat = [[ext(j)[:, :, 1:HW1, :], dif[:, b, :, :, HD * j:HD * j + HD], ext(j)[:, :, 0:H, :],
                         cosv[:, b, :, :, HD * j:HD * j + HD]] for j in range(3)]
                A, B, C = quat
                to = ham[:, 2 * b:2 * b + 2, :].rearrange("p t (h d) -> p t h d", h=H)
                t0 = hb[0][:, :, :, :]
                u, v, z, acc, w = [hb[j][:, :, :, :] for j in range(1, 6)]
                mul, add, sub = ALU.mult, ALU.add, ALU.subtract
                base = 33 * i

                def op(o, i0, i1, f, last=None):
                    if last is not None:
                        after(dve, s["ham_step"], base + (last + 1))
                    nc.vector.tensor_tensor(o, i0, i1, f).then_inc(s["ham_step"], 1)

                after(dve, s["ham_done"], i)
                after(dve, s["cosd"], i + 1)
                op(t0, ext(1), ext(2), mul)
                op(u, B[1], C[1], mul)
                op(v, B[3], C[3], mul)
                op(acc, t0[:, :, 1:HW1, :], t0[:, :, 0:H, :], sub, 0)
                op(z, B[0], C[1], mul)
                op(u, u, v, add, 2)
                op(v, B[1], C[0], mul, 5)
                op(w, B[2], C[3], mul)
                op(acc, acc, u, sub)
                op(z, z, v, add, 6)
                op(u, B[3], C[2], mul, 8)
                op(v, B[0], C[2], mul, 9)
                after(dve, s["tp_pe"], g)
                op(to, A[0], acc, mul)
                op(acc, z, w, add, 12)
                op(z, B[1], C[3], mul, 13)
                op(w, B[2], C[0], mul)
                op(acc, acc, u, sub)
                op(v, v, z, sub, 14)
                op(u, B[3], C[1], mul, 16)
                op(z, B[0], C[3], mul, 17)
                op(acc, A[1], acc, mul)
                op(v, v, w, add)
                op(w, B[1], C[2], mul, 21)
                op(to, to, acc, sub)
                op(v, v, u, add)
                op(u, B[2], C[1], mul, 24)
                op(z, z, w, add)
                op(v, A[2], v, mul)
                op(acc, B[3], C[0], mul)
                op(z, z, u, sub, 26)
                op(to, to, v, sub, 27)
                op(z, z, acc, add, 29)
                op(z, A[3], z, mul, 31)
                dve.wait_ge(s["ham_step"], base + 33)
                nc.vector.tensor_tensor(to, to, z, sub).then_inc(s["ham_done"], 1)

            def step(n, parity):
                if on(n - 4):
                    after(dve, s["mb_done"], n - 3)
                    add_banks(n - 4, 4, "res2", lambda b: after(dve, s["mm_pe"], 2 * (n - 4) + (b + 1)))
                if on(n - 3):
                    after(dve, s["rs2_pool"], n - 2)
                    after(dve, s["t1_pe"], min(n + 1, NG) if isinstance(n, int) else n + 1)
                    norm(n - 3, lambda t: xn[:, t, :], mv2, rs2, "ln2_done")
                first_norm = isinstance(n, int) and n + 1 < NC
                if on(n + 1):
                    if first_norm:
                        dve.wait_ge(*((s["x_in0"], 16) if n < 0 else (s["x_rest"], 16 * (NC - 1))))
                        stats(n + 1, mv1, "var1")
                        dve.wait_ge(s["rs1_pool"], 2 * (n + 1) + 1)
                        norm(n + 1, lambda t: tile(n + 1, t), mv1, rs1)
                    stats(n + 1, mv1, "var1")
                if on(n - 1):
                    hamilton(n - 1, 0, 1 - parity)
                if on(n - 2):
                    if isinstance(n, int) and n == 2:
                        dve.wait_ge(s["filt_in"], 16)
                    after(dve, s["r_pe"], n - 1)
                    after(dve, s["g_pe"], n - 2)
                    for e in range(EH):
                        ins = nc.vector.tensor_tensor(
                            coef[:, e, :], bank[6 + e][:, :],
                            filt[:, e, bass.ds(CW * ((n - 2) % NC), CW)], ALU.mult)
                    ins.then_inc(s["filt_dve"], 1)
                if on(n + 1):
                    after(dve, s["rs1_pool"], 2 * (n + 2) if first_norm else n + 2 + NC)
                    after(dve, s["t1_pe"], n + 1)
                    after(dve, s["t2_pe"], n - 2)
                    norm(n + 1, lambda t: xn[:, t, :], mv1, rs1, "ln1_done")
                if on(n - 1):
                    hamilton(n - 1, 1, 1 - parity)
                if on(n - 2):
                    after(dve, s["pb_done"], n - 1)
                    after(dve, s["g_pe"], n - 1)
                    add_banks(n - 2, 2, "res1", lambda b: None)
                    stats(n - 2, mv2, "var2")

            steps(dve, step)


def tail(nc, d, out, x, ident, bank):
    with ExitStack() as ctx:
        def sb(name, *shape):
            return ctx.enter_context(nc.sbuf_tensor(name, [P, *shape], F32))

        big = sb("big", 2, FC, 512)
        ew = sb("ew", EH, NX, E)
        eb = sb("eb", CT, E)
        uw = sb("uw", EH, D1)
        vw = sb("vw", EH, D1)
        ow = sb("ow", MC, E)
        ub = sb("ub", MC)
        vb = sb("vb", MC)
        tz = sb("tz", MC)
        ob = sb("ob", E)
        rw = sb("rw", 2, EH, NX)
        rb = sb("rb", 2, NX)
        prio = sb("prio", NX)
        lng = sb("lng", 2, EH)
        b1 = sb("b1", NX, FC)
        xt = sb("xt", EH, S)
        rt = sb("rt", 2, EH, CW)
        rows = sb("rows", 2, CT, E)
        hid = sb("hid2", FC, CW)
        su, sv = hid[:, 0:MC, :], hid[:, MC:2 * MC, :]
        stat = sb("stat2", CT, 6)
        mv = sb("mv", NT, 2)
        ve = sb("ve2", NT)
        sc = [sb(f"sc{i}", NT) for i in range(6)]
        half = sb("half2", 3, NT)
        lg = sb("lg", NT, NX)
        ex = sb("ex", NT, NX)
        pick = sb("pick", NT, NX)
        mg = sb("mg", NT, NX)
        mx = sb("mx", NT)
        gate = sb("gate", NT)
        mgt = sb("mgt", 2, P)

        names = """x0_in x0_rest added ew_in rw_in at_in e2_in moments small rows_done turned evac
            logits eb_in zero picked expd mgt_pe mgt_act bias_pe bias_dve ex_pe ex_dve held2
            pool2 u_pe u_act prod o_pe o_dve ahead ob_done w_in0 w_in1 h_pe h_act y_pe y_dve out2""".split()
        s = {n: ctx.enter_context(nc.semaphore("f_" + n)) for n in names}
        x0 = big[:, :, :, :].rearrange("p a f n -> p (a f n)").rearrange("p (c t e) -> p c t e", c=NC, t=CT)
        w1 = [big[:, b, 0:4, :].rearrange("p (k f) n -> p k (f n)", k=EH) for b in range(2)]
        w2 = [big[:, b, 4:8, :].rearrange("p f (g n) -> p (f g) n", g=2) for b in range(2)]
        by_row = "b (c p t) e -> p (b c) t e"
        x_in = d["L0_attn_x"].rearrange(by_row, p=P, t=CT)
        x_out = out.rearrange(by_row, p=P, t=CT)
        xc = x[:, :, :].rearrange("p (c t) e -> p c t e", t=CT)

        block = ctx.enter_context(nc.Block())

        @block.sync
        def _(sp):
            sp.dma_start(x0[:, 0], x_in[:, 0]).then_inc(s["x0_in"], 16)
            for c in range(1, NC):
                sp.dma_start(x0[:, c], x_in[:, c]).then_inc(s["x0_rest"], 16)
            for i, (w, b) in enumerate((("L0_ffn_router_w", "L0_ffn_router_b"), ("L1_ffn_Wr", "L1_ffn_br"))):
                sp.dma_start(rw[:, i, :, :], d[w].rearrange("(k p) n -> p k n", p=P)).then_inc(s["rw_in"], 16)
                sp.dma_start(rb[:, i, :], d[b].partition_broadcast(P)).then_inc(s["rw_in"], 16)
            sp.dma_start(prio[:, :], d["c_prio"].partition_broadcast(P)).then_inc(s["rw_in"], 16)
            for k in range(EH):
                sp.dma_start(ew[:, k, :, :], d["L0_ffn_expert_w"][:, k * P:(k + 1) * P, :].rearrange("x p n -> p x n")).then_inc(s["ew_in"], 16)
            sp.wait_ge(s["zero"], 1)
            for t in range(CT):
                sp.dma_start(eb[NX * t:NX * t + NX, t, :], d["L0_ffn_expert_b"]).then_inc(s["eb_in"], 16)
            for to, name in ((uw, "L1_attn_u_w"), (vw, "L1_attn_v_w"), (ow, "L1_attn_o_w")):
                sp.dma_start(to[:, :, :], d[name].rearrange("(k p) n -> p k n", p=P)).then_inc(s["at_in"], 16)
            for to, name in ((ub, "L1_attn_u_b"), (vb, "L1_attn_v_b")):
                sp.dma_start(to[:, :], d[name].rearrange("(k p) -> p k", p=P), allow_slow_non_contiguous=True).then_inc(s["at_in"], 16)
            heads = d["L1_attn_t_zero"].rearrange("(m h) o -> h (m o)", h=2)
            for h in range(2):
                sp.dma_start(tz[64 * h:64 * h + 64, :], heads[h].partition_broadcast(64), allow_slow_non_contiguous=True).then_inc(s["at_in"], 16)
            sp.dma_start(ob[:, :], d["L1_attn_o_b"].partition_broadcast(P)).then_inc(s["at_in"], 16)
            for i, name in enumerate(("L1_ffn_ln_g", "L1_ffn_ln_b")):
                sp.dma_start(lng[:, i, :], d[name].rearrange("(k p) -> p k", p=P), allow_slow_non_contiguous=True).then_inc(s["e2_in"], 16)
            sp.dma_start(b1[:, :, :], d["L1_ffn_b1"].rearrange("x (f p) -> p x f", p=P), allow_slow_non_contiguous=True).then_inc(s["e2_in"], 16)
            sp.wait_ge(s["added"], NC)

            def load(e, b):
                sp.dma_start(w1[b], d["L1_ffn_W1"][bass.ds(e, 1)].rearrange("x (k p) f -> p k (x f)", p=P)).then_inc(s[f"w_in{b}"], 16)
                sp.dma_start(w2[b], d["L1_ffn_W2"][bass.ds(e, 1)].rearrange("x (k p) f -> p k (x f)", p=P)).then_inc(s[f"w_in{b}"], 16)
            load(0, 0)
            load(1, 1)
            sp.wait_ge(s["bias_pe"], NC)
            for t in range(CT):
                sp.dma_start(eb[NX * t:NX * t + NX, t, :], d["L1_ffn_b2"]).then_inc(s["eb_in"], 16)
            with sp.Fori(1, NX // 2) as pair:
                for b in range(2):
                    sp.wait_ge(s["y_pe"], NC * (2 * pair - 1 + b))
                    sp.sem_inc(s["held2"], 1)
                    load(2 * pair + b, b)
            sp.wait_ge(s["y_dve"], NC * NX)
            sp.dma_start(x_out, xc).then_inc(s["out2"], 16)
            sp.wait_ge(s["out2"], 16)

        @block.tensor
        def _(pe):
            def turn(n, c):
                pe.wait_ge(s["rows_done"], n + 1)
                if n:
                    pe.wait_ge(s["evac"], n)
                for e in range(EH):
                    for t in range(CT):
                        mm = pe.transpose(bank[e][:, t * P:(t + 1) * P], rows[:, n % 2, t, e * P:(e + 1) * P], ident[:, :])
                mm.then_inc(s["turned"], 1)

            def route(i, n, c, of):
                pe.wait_ge(s["evac"], n + 1)
                for t in range(CT):
                    for k in range(EH):
                        mm = pe.matmul(bank[2][:, NX * (CT * c + t):NX * (CT * c + t + 1)],
                                       of[:, k, t * P:(t + 1) * P], rw[:, i, k, :], start=(k == 0), stop=(k == EH - 1))
                mm.then_inc(s["logits"], 1)

            def biases(i):
                for c in range(NC):
                    n = NC * i + c
                    if c == 0:
                        pe.wait_ge(s["picked"], i + 1)
                        pe.wait_ge(s["evac"], NC * (1 + 2 * i))
                    if n:
                        pe.wait_ge(s["mgt_act"], n)
                    pe.transpose(bank[0][0:NX * CT, 0:P], mg[:, CT * c:CT * c + CT, :].rearrange("p t x -> p (t x)"),
                                 ident[:, :]).then_inc(s["mgt_pe"], 1)
                    pe.wait_ge(s["mgt_act"], n + 1)
                    if n:
                        pe.wait_ge(s["bias_dve"], n)
                    for t in range(CT):
                        mm = pe.matmul(bank[4 + t // 2][:, (t % 2) * E:(t % 2 + 1) * E], mgt[0:NX * CT, n % 2, :],
                                       eb[0:NX * CT, t, :], start=True, stop=True)
                    mm.then_inc(s["bias_pe"], 1)

            pe.wait_ge(s["rw_in"], 16 * 5)
            for c in range(NC):
                turn(c, c)
                if c:
                    route(0, c - 1, c - 1, xt[:, :, CW * (c - 1):CW * c])
            route(0, NC - 1, NC - 1, xt[:, :, CW * (NC - 1):CW * NC])
            pe.wait_ge(s["eb_in"], 16 * CT)
            biases(0)
            pe.wait_ge(s["ew_in"], 32)
            pe.wait_ge(s["bias_dve"], NC)
            for i in range(NT):
                if i > 1:
                    pe.wait_ge(s["ex_dve"], i - 1)
                for q in range(4):
                    for k in range(EH):
                        mm = pe.matmul(bank[4 * (i % 2) + q][:, :], xt[:, k, P * i:P * i + P],
                                       ew[:, k, 2 * q:2 * q + 2, :].rearrange("p x n -> p (x n)"),
                                       start=(k == 0), stop=(k == EH - 1))
                mm.then_inc(s["ex_pe"], 1)
            pe.wait_ge(s["at_in"], 16 * 8)
            pe.wait_ge(s["ex_dve"], NT)

            def project(c):
                pe.wait_ge(s["prod"], c + 1)
                if c:
                    pe.wait_ge(s["o_dve"], c)
                for t in range(CT):
                    for m in range(MC):
                        mm = pe.matmul(bank[6 + t // 2][:, (t % 2) * E:(t % 2 + 1) * E], su[:, m, t * P:(t + 1) * P],
                                       ow[:, m, :], start=(m == 0), stop=(m == MC - 1))
                mm.then_inc(s["o_pe"], 1)

            for c in range(NC):
                turn(NC + c, c)
                if c:
                    project(c - 1)
                pe.wait_ge(s["evac"], NC + c + 1)
                for m in range(MC):
                    for j, w in enumerate((uw, vw)):
                        q = 2 * m + j
                        n = 8 * c + q
                        if n >= 4:
                            pe.wait_ge(s["u_act"], n - 3)
                        for k in range(EH):
                            mm = pe.matmul(bank[2 + q % 4][:, :], w[:, k, m * P:(m + 1) * P], rt[:, c % 2, k, :],
                                           start=(k == 0), stop=(k == EH - 1))
                        mm.then_inc(s["u_pe"], 1)
            project(NC - 1)
            pe.wait_ge(s["u_act"], 8 * NC)
            for c in range(NC):
                turn(2 * NC + c, c)
                route(1, 2 * NC + c, c, rt[:, c % 2])
            pe.wait_ge(s["eb_in"], 32 * CT)
            pe.wait_ge(s["o_dve"], NC)
            biases(1)
            pe.wait_ge(s["bias_dve"], 2 * NC)

            def up(n, c, b, first):
                for f in range(FC):
                    if not first or f > 1:
                        pe.wait_ge(s["h_act"], FC * n + f - 1)
                    for k in range(EH):
                        mm = pe.matmul(bank[f % 2][:, :], w1[b][:, k, f * P:(f + 1) * P], xt[:, k, bass.ds(CW * c, CW)],
                                       start=(k == 0), stop=(k == EH - 1))
                    mm.then_inc(s["h_pe"], 1)

            def down(n, b, first):
                pe.wait_ge(s["h_act"], FC * (n + 1))
                if not first:
                    pe.wait_ge(s["y_dve"], n)
                for t in range(CT):
                    for f in range(FC):
                        mm = pe.matmul(bank[4 + t // 2][:, (t % 2) * E:(t % 2 + 1) * E], hid[:, f, t * P:(t + 1) * P],
                                       w2[b][:, f, :], start=(f == 0), stop=(f == FC - 1))
                mm.then_inc(s["y_pe"], 1)

            for b in range(2):
                pe.wait_ge(s[f"w_in{b}"], 32)
                for c in range(NC):
                    up(NC * b + c, c, b, b + c == 0)
                    down(NC * b + c, b, b + c == 0)
            with pe.Fori(1, NX // 2) as pair:
                for b in range(2):
                    with pe.Fori(0, NC) as c:
                        pe.wait_ge(s[f"w_in{b}"], 32 * (pair + 1))
                        n = NC * 2 * pair + (NC * b + c)
                        up(n, c, b, False)
                        down(n, b, False)

        @block.scalar
        def _(act):
            def evac(n, to):
                act.wait_ge(s["turned"], n + 1)
                for e in range(EH):
                    ins = nc.scalar.activation(to(e), bank[e][:, :], ACT.Copy)
                return ins

            def softmax(i):
                act.wait_ge(s["expd"], 2 * i + 1)
                nc.scalar.activation(ex[:, :, :], lg[:, :, :], ACT.Exp).then_inc(s["expd"], 1)

            def turn_gates(i):
                for c in range(NC):
                    n = NC * i + c
                    act.wait_ge(s["mgt_pe"], n + 1)
                    if n > 1:
                        act.wait_ge(s["bias_pe"], n - 1)
                    nc.scalar.activation(mgt[0:NX * CT, n % 2, :], bank[0][0:NX * CT, 0:P], ACT.Copy).then_inc(s["mgt_act"], 1)

            for c in range(NC):
                evac(c, lambda e: xt[:, e, CW * c:CW * c + CW]).then_inc(s["evac"], 1)
            softmax(0)
            turn_gates(0)
            act.wait_ge(s["at_in"], 16 * 8)
            for c in range(NC):
                if c > 1:
                    act.wait_ge(s["u_pe"], 8 * (c - 1))
                evac(NC + c, lambda e: rt[:, c % 2, e, :]).then_inc(s["evac"], 1)
                for q in range(8):
                    if q == 0 and c:
                        act.wait_ge(s["o_pe"], c)
                    act.wait_ge(s["u_pe"], 8 * c + q + 1)
                    to, b = ((su, ub), (sv, vb))[q % 2]
                    nc.scalar.activation(to[:, q // 2, :], bank[2 + q % 4][:, :], ACT.Silu,
                                         bias=b[:, q // 2:q // 2 + 1]).then_inc(s["u_act"], 1)
            act.wait_ge(s["u_pe"], 8 * NC)
            act.wait_ge(s["ex_pe"], NT)
            act.wait_ge(s["e2_in"], 48)
            for c in range(NC):
                if c > 1:
                    act.wait_ge(s["logits"], NC + c - 1)
                evac(2 * NC + c, lambda e: rt[:, c % 2, e, :])
                for e in range(EH):
                    ins = nc.scalar.activation(xt[:, e, CW * c:CW * c + CW], bank[e][:, :], ACT.Identity,
                                               bias=lng[:, 1, e:e + 1], scale=lng[:, 0, e:e + 1])
                ins.then_inc(s["evac"], 1)
            softmax(1)
            turn_gates(1)

            def relu(n, e, first):
                for f in range(FC):
                    act.wait_ge(s["h_pe"], FC * n + (f + 1))
                    if f == 0 and not first:
                        act.wait_ge(s["y_pe"], n)
                    nc.scalar.activation(hid[:, f, :], bank[f % 2][:, :], ACT.Relu,
                                         bias=b1[:, bass.ds(e, 1), f]).then_inc(s["h_act"], 1)

            for n in range(2 * NC):
                relu(n, n // NC, n == 0)
            with act.Fori(2 * NC, NX * NC) as n:
                relu(n, n // NC, False)

        @block.gpsimd
        def _(pool):
            k = s["pool2"]
            count = [0]

            def step(ins):
                ins.then_inc(k, 1)
                count[0] += 1
                pool.wait_ge(k, count[0])

            def power(o, a, which):
                step(nc.gpsimd.tensor_tensor(o, a, half[:, which, :], ALU.pow))

            def plus(o, a, v):
                step(nc.gpsimd.tensor_scalar(o, a, v, 0.0, ALU.add, ALU.add))

            def times(o, a, b):
                step(nc.gpsimd.tensor_tensor(o, a, b, ALU.mult))

            for i, v in enumerate((-0.5, 0.5, -1.0)):
                step(nc.gpsimd.memset(half[:, i, :], v))
            nc.gpsimd.memset(eb[:, :, :], 0.0).then_inc(s["zero"], 1)
            var = mv[:, :, 1]
            rstd, t, a, c, ir, _ = [q[:, :] for q in sc]
            pool.wait_ge(s["moments"], 1)
            plus(ve[:, :], var, EPS)
            nc.gpsimd.tensor_tensor(rstd, ve[:, :], half[:, 0, :], ALU.pow).then_inc(s["small"], 1)
            pool.wait_ge(s["moments"], 2)
            plus(ve[:, :], var, EPS)
            power(rstd, ve[:, :], 0)
            power(t, var, 1)
            times(t, t, rstd)
            plus(t, t, 1e-8)
            power(t, t, 2)
            times(t, t, rstd)
            plus(a, rstd, 1.0)
            times(c, rstd, mv[:, :, 0])
            nc.gpsimd.tensor_scalar(c, c, -1.0, 1.0, ALU.mult, ALU.mult).then_inc(s["small"], 1)
            pool.wait_ge(s["at_in"], 16 * 8)
            for ch in range(NC):
                pool.wait_ge(s["ahead"], ch + 1)
                nc.gpsimd.tensor_tensor(xc[:, ch], xc[:, ch], ob[:, :].unsqueeze(1).broadcast_to([P, CT, E]), ALU.add).then_inc(s["ob_done"], 1)
            pool.wait_ge(s["moments"], 3)
            plus(ve[:, :], var, EPS)
            power(rstd, ve[:, :], 0)
            times(ve[:, :], rstd, rstd)
            times(ve[:, :], ve[:, :], var)
            plus(ve[:, :], ve[:, :], EPS)
            power(t, ve[:, :], 0)
            times(t, t, rstd)
            nc.gpsimd.tensor_tensor(ir, ve[:, :], half[:, 1, :], ALU.pow).then_inc(s["small"], 1)

        @block.vector
        def _(dve):
            V = nc.vector

            def stats(c):
                dve.drain()
                for t in range(CT):
                    V.bn_stats(stat[:, t, :], x[:, CT * c + t, :])
                dve.drain()
                for t in range(CT):
                    ins = V.bn_aggr(mv[:, CT * c + t, :], stat[:, t, :])
                return ins

            def norm(n, c, scale):
                if n > 1:
                    dve.wait_ge(s["turned"], n - 1)
                for t in range(CT):
                    i = CT * c + t
                    ins = V.tensor_scalar(rows[:, n % 2, t, :], x[:, i, :], mv[:, i, 0:1], scale[:, i:i + 1],
                                          ALU.subtract, ALU.mult)
                ins.then_inc(s["rows_done"], 1)

            def choose(i):
                dve.wait_ge(s["logits"], NC * (i + 1))
                if i:
                    V.tensor_tensor(lg[:, :, :], bank[2][:, 0:NT * NX].rearrange("p (t x) -> p t x", x=NX),
                                    sc[4][:, :].unsqueeze(2).broadcast_to([P, NT, NX]), ALU.mult)
                    dve.drain()
                    V.tensor_tensor(lg[:, :, :], lg[:, :, :], rb[:, i, :].unsqueeze(1).broadcast_to([P, NT, NX]), ALU.add)
                else:
                    V.tensor_tensor(lg[:, :, :], bank[2][:, 0:NT * NX].rearrange("p (t x) -> p t x", x=NX),
                                    rb[:, i, :].unsqueeze(1).broadcast_to([P, NT, NX]), ALU.add)
                dve.drain()
                V.tensor_reduce(mx[:, :], lg[:, :, :], AX_X, ALU.max)
                dve.drain()
                V.tensor_tensor(lg[:, :, :], lg[:, :, :], mx[:, :].unsqueeze(2).broadcast_to([P, NT, NX]), ALU.subtract).then_inc(s["expd"], 1)
                dve.drain()
                V.tensor_scalar(pick[:, :, :], lg[:, :, :], 0.0, None, ALU.is_ge)
                dve.drain()
                V.tensor_tensor(pick[:, :, :], pick[:, :, :], prio[:, :].unsqueeze(1).broadcast_to([P, NT, NX]), ALU.mult)
                dve.drain()
                V.tensor_reduce(mx[:, :], pick[:, :, :], AX_X, ALU.max)
                dve.drain()
                V.tensor_tensor(pick[:, :, :], pick[:, :, :], mx[:, :].unsqueeze(2).broadcast_to([P, NT, NX]), ALU.is_equal)
                dve.wait_ge(s["expd"], 2 * i + 2)
                V.tensor_reduce(gate[:, :], ex[:, :, :], AX_X, ALU.add)
                dve.drain()
                V.reciprocal(gate[:, :], gate[:, :])
                dve.drain()
                V.tensor_tensor(mg[:, :, :], pick[:, :, :], gate[:, :].unsqueeze(2).broadcast_to([P, NT, NX]), ALU.mult).then_inc(s["picked"], 1)

            def add(c, b0, wait=None):
                for b in range(2):
                    part = xc[:, c, 2 * b:2 * b + 2, :].rearrange("p t e -> p (t e)")
                    ins = V.tensor_tensor(part, part, bank[b0 + b][:, :], ALU.add)
                return ins

            for c in range(NC):
                dve.wait_ge(*((s["x0_rest"], 16 * (NC - 1)) if c else (s["x0_in"], 16)))
                V.tensor_tensor(xc[:, c], xc[:, c], x0[:, c], ALU.add).then_inc(s["added"], 1)
                ins = stats(c)
            ins.then_inc(s["moments"], 1)
            dve.wait_ge(s["small"], 1)
            for c in range(NC):
                norm(c, c, sc[0])
            dve.wait_ge(s["rw_in"], 80)
            choose(0)
            for c in range(NC):
                dve.wait_ge(s["bias_pe"], c + 1)
                add(c, 4).then_inc(s["bias_dve"], 1)
            for i in range(NT):
                dve.wait_ge(s["ex_pe"], i + 1)
                for e in range(NX):
                    dve.drain()
                    ins = V.scalar_tensor_tensor(out=x[:, i, :], in0=bank[4 * (i % 2) + e // 2][:, (e % 2) * E:(e % 2 + 1) * E],
                                                 scalar=mg[:, i, e:e + 1], in1=x[:, i, :], op0=ALU.mult, op1=ALU.add)
                ins.then_inc(s["ex_dve"], 1)
                if i % CT == CT - 1:
                    ins = stats(i // CT)
            ins.then_inc(s["moments"], 1)
            dve.wait_ge(s["small"], 2)
            dve.wait_ge(s["at_in"], 16 * 8)
            for c in range(NC):
                norm(NC + c, c, sc[1])
                for t in range(CT):
                    i = CT * c + t
                    ins = V.tensor_scalar(x[:, i, :], x[:, i, :], sc[2][:, i:i + 1], sc[3][:, i:i + 1], ALU.mult, ALU.add)
                ins.then_inc(s["ahead"], 1)
                def gated(c):
                    dve.wait_ge(s["u_act"], 8 * (c + 1))
                    for m in range(MC):
                        ins = V.scalar_tensor_tensor(out=su[:, m, :], in0=sv[:, m, :], scalar=tz[:, m:m + 1], in1=su[:, m, :],
                                                     op0=ALU.mult, op1=ALU.mult)
                    ins.then_inc(s["prod"], 1)
                def result(c):
                    dve.wait_ge(s["ob_done"], c + 1)
                    dve.wait_ge(s["o_pe"], c + 1)
                    add(c, 6).then_inc(s["o_dve"], 1)
                    return stats(c)
                if c:
                    gated(c - 1)
                if c > 1:
                    result(c - 2)
            gated(NC - 1)
            result(NC - 2)
            result(NC - 1).then_inc(s["moments"], 1)
            dve.wait_ge(s["small"], 3)
            for c in range(NC):
                norm(2 * NC + c, c, sc[1])
            choose(1)
            for c in range(NC):
                dve.wait_ge(s["bias_pe"], NC + c + 1)
                add(c, 4).then_inc(s["bias_dve"], 1)

            def combine(n, e, c, first):
                dve.wait_ge(s["y_pe"], n + 1)
                for t in range(CT):
                    now = xc[:, bass.ds(c, 1), t, :].rearrange("p c e -> p (c e)")
                    ins = V.scalar_tensor_tensor(out=now, in0=bank[4 + t // 2][:, (t % 2) * E:(t % 2 + 1) * E],
                                                 scalar=mg[:, bass.ds(CT * c + t, 1), bass.ds(e, 1)].rearrange("p t x -> p (t x)"),
                                                 in1=now, op0=ALU.mult, op1=ALU.add)
                ins.then_inc(s["y_dve"], 1)

            dve.drain()
            for n in range(NC):
                combine(n, 0, n, True)
            dve.drain()
            with dve.Fori(NC, NX * NC) as n:
                combine(n, n // NC, n % NC, False)


def program(nc, d, out):
    with ExitStack() as ctx:
        x = ctx.enter_context(nc.sbuf_tensor("x", [P, NT, E], F32))
        ident = ctx.enter_context(nc.sbuf_tensor("ident", [P, P], F32))
        bank = [ctx.enter_context(nc.psum_tensor(f"bank{i}", [P, 512], F32)) for i in range(8)]
        attention(nc, d, x, ident, bank)
        tail(nc, d, out, x, ident, bank)


_INS = ["L0_attn_x", "L0_attn_ln1_w", "L0_attn_ln1_b", "L0_attn_attn_w", "L0_attn_attn_b", "L0_attn_aproj_w",
        "L0_attn_aproj_b", "L0_attn_ln2_w", "L0_attn_ln2_b", "L0_attn_fc_w", "L0_attn_fc_b", "L0_attn_mproj_w",
        "L0_attn_mproj_b", "L0_ffn_router_w", "L0_ffn_router_b", "L0_ffn_expert_w", "L0_ffn_expert_b",
        "L1_attn_u_w", "L1_attn_u_b", "L1_attn_v_w", "L1_attn_v_b", "L1_attn_o_w", "L1_attn_o_b",
        "L1_attn_t_zero", "L1_ffn_Wr", "L1_ffn_br", "L1_ffn_ln_g", "L1_ffn_ln_b", "L1_ffn_W1", "L1_ffn_b1",
        "L1_ffn_W2", "L1_ffn_b2"]
_TURNED = ["L1_attn_u_w", "L1_attn_v_w", "L1_attn_o_w"]
_SHAPE = (1, S, E)


def kernel(**inputs):
    import numpy as _np
    import concourse.bacc as _bacc
    from concourse.bass_utils import run_bass_kernel_spmd as _run

    nc = _bacc.Bacc("TRN2", target_bir_lowering=False, num_devices=1)
    arrays, aps = {}, {}
    for name in _INS:
        a = _np.asarray(inputs[name])
        arrays[name] = _np.ascontiguousarray(a.T if name in _TURNED else a)
    arrays.update(shape_constants())
    for name, a in arrays.items():
        aps[name] = nc.dram_tensor(name, a.shape, mybir.dt.from_np(a.dtype), kind="ExternalInput").ap()
    out = nc.dram_tensor("out", _SHAPE, F32, kind="ExternalOutput").ap()
    program(nc, aps, out)
    r = _run(nc, [arrays], core_ids=[0])
    return r.results[0]["out"]
```

```python
from contextlib import ExitStack

import concourse.bass as bass
from concourse import mybir

F32 = mybir.dt.float32
ALU = mybir.AluOpType
ACT = mybir.ActivationFunctionType
AX_X = mybir.AxisListType.X

P = 128
S = 4096
E = 256
EH = E // P
L = 4
H = 16
HD = E // H
QW = 3 * HD
CT = 4
CW = CT * P
NC = S // CW
NT = S // P
NG = L * NC
F = 4 * E
FC = F // P
NX = 8
D1 = 512
MC = D1 // P
XW = 2 * EH * F
PAY = 2 * E + 4
SLOTS = NT + NX
I32 = mybir.dt.int32
HW1 = H + 1
W2 = 3 * E // 2
EPS = 1e-5
TURN = 0.15915494309189535
ROUND = 12582912.0
TWO_PI = 6.2831845


def shape_constants():
    import numpy as np

    h = np.arange(H)
    base = np.zeros((H, H))
    for k in range(H // 2 + 1):
        g = np.sqrt(1 / H) if k in (0, H // 2) else np.sqrt(2 / H)
        base[:, k] = g * np.cos(2 * np.pi * h * k / H)
        if 0 < k < H // 2:
            base[:, H // 2 + k] = g * np.sin(2 * np.pi * h * k / H)
    one = np.float32
    k = np.fft.fftfreq(H).astype(one)[[*range(H // 2 + 1), *range(1, H // 2)]]
    ks = np.fft.fftfreq(S).astype(one)[:, None, None]
    km = np.sqrt(ks ** 2 + k[None, :, None] ** 2 + k[None, None, :] ** 2 + one(1e-10))
    filt = np.cos(np.arctan(np.log(km + one(1e-10)).astype(np.float64))).reshape(S, E)
    lam = np.arange(S, dtype=one) / one(S)
    t = np.arange(S, dtype=one) * one(0.1)
    phase = t - one(2) * lam + one(0.5) * lam ** 2
    mod = 1 + 0.1 * (np.sin((t + lam).astype(np.float64)) * np.cos(phase.astype(np.float64)))
    scale = (filt * mod[:, None]).reshape(NC, P, CT, EH, P).transpose(4, 3, 0, 2, 1)
    return {
        "c_heads": np.kron(base, base).astype(one),
        "c_filter": np.ascontiguousarray(scale.reshape(P, EH, S)).astype(one),
        "c_low": np.triu(np.ones((P, P)), 1).astype(one),
        "c_slot": np.arange(SLOTS).astype(one),
        "c_token": np.arange(S).reshape(NC, P, CT).transpose(1, 0, 2).reshape(P, NT).astype(one),
        "c_fill": np.tile(np.array([0] * (2 * E + 1) + [S] + [0] * (PAY - 2 * E - 2)), (P, 1)).astype(one),
        "c_prio": np.arange(NX, 0, -1).astype(one),
        "c_ident": np.eye(P, dtype=one),
    }


def attention(nc, d, x, ident, bank):
    with ExitStack() as ctx:
        def sb(name, *shape):
            return ctx.enter_context(nc.sbuf_tensor(name, [P, *shape], F32))

        filt = sb("filt", 2, EH, CW)
        heads = sb("heads", EH, E)
        at_w = sb("at_w", EH, 3 * E)
        back_w = sb("back_w", L, EH, E)
        fc_w = sb("fc_w", EH, F)
        mp_w = sb("mp_w", FC, E)
        at_b = sb("at_b", 3 * E)
        ap_b = sb("ap_b", E)
        mp_b = sb("mp_b", E)
        fc_b = sb("fc_b", FC)
        ln1 = sb("ln1", 2, EH)
        ln2 = sb("ln2", 2, EH)
        xn = sb("xn", CT, E)
        xt1 = sb("xt1", EH, CW)
        xt2 = sb("xt2", EH, CW)
        qkv = sb("qkv", 2 * CT, HW1, QW)
        dif = sb("dif", 2, 2, H, QW)
        cosv = sb("cosv", 2, 2, H, QW)
        whole = sb("whole", 2, 2, H, QW)
        turns1 = sb("turns1", 2, H, QW)
        third = sb("third", 2, 2, H, HD)
        term = sb("term", 2, H, HD)
        ham = sb("ham", CT, E)
        hb = [sb(f"hb{i}", 2, HW1 if i == 0 else H, HD) for i in range(6)]
        ham_t = sb("ham_t", EH, CW)
        coef = sb("coef", EH, CW)
        hid = sb("hid", FC, CW)
        stat = sb("stat", CT, 6)
        mv1 = sb("mv1", CT, 2)
        mv2 = sb("mv2", CT, 2)
        rs1 = sb("rs1", CT)
        rs2 = sb("rs2", CT)
        ve = sb("ve", CT)
        half = sb("half", CT)
        quarter = sb("quarter", 1)
        up_to_whole = sb("up_to_whole", 1)
        down_again = sb("down_again", 1)

        names = """x_in0 x_rest ident_in heads_in ap_in filt_in0 filt_in1 at_w_in ln1_in at_s_in fc_w_in mp_w_in mp_s_in
            before_in back_pe back_act t1_pe t1_act qkv_pe qkv_act added biased pool_step prep cosd
            ham_step ham_done third_step third_done turn_step whole_done tp_pe tp_act r_pe filt_dve g_pe res1 var1 rs1_pool ln1_done var2 rs2_pool
            ln2_done t2_pe t2_act fc_pe gelu mm_pe res2 pb_done mb_done eps held_pool held_sp zeroed""".split()
        s = {n: ctx.enter_context(nc.semaphore(n)) for n in names}

        rows = "b (c p t) e -> p (b c) t e"
        x_in = d["L0_attn_x"].rearrange(rows, p=P, t=CT)
        xc = x[:, :, :].rearrange("p (c t) e -> p c t e", t=CT)

        def hold(eng, what, value):
            if isinstance(value, int) and value <= 0:
                return
            eng.wait_ge(what, value)
            if not isinstance(value, int):
                eng.sem_inc(s["held_pool" if eng.engine == mybir.EngineType.Pool else "held_sp"], 1)

        def quaternions(b, parity):
            a = CT * parity + 2 * b
            ext = lambda j: qkv[:, a:a + 2, :, HD * j:HD * j + HD]
            return [[ext(j)[:, :, 1:HW1, :], dif[:, b, :, :, HD * j:HD * j + HD], ext(j)[:, :, 0:H, :],
                     cosv[:, b, :, :, HD * j:HD * j + HD]] for j in range(3)]

        def after(eng, what, value):
            if not isinstance(value, int) or value > 0:
                eng.wait_ge(what, value)

        def steps(eng, step):
            for n in range(-1, 8):
                step(n, n % 2)
            with eng.Fori(4, 15) as pair:
                step(2 * pair, 0)
                step(2 * pair + 1, 1)
            for n in range(NG - 2, NG + 4):
                step(n, n % 2)

        def on(g):
            return not isinstance(g, int) or 0 <= g < NG

        block = ctx.enter_context(nc.Block())

        @block.sync
        def _(sp):
            def by_channel(to, name, l, done):
                sp.dma_start(to, d[name][l].rearrange("(k p) -> p k", p=P),
                             allow_slow_non_contiguous=True).then_inc(s[done], 16)

            def matrix(to, name, l, done):
                sp.dma_start(to, d[name][l].rearrange("(k p) n -> p k n", p=P)).then_inc(s[done], 16)

            def load_attention(l):
                hold(sp, s["t1_act"], NC * l)
                by_channel(ln1[:, 0, :], "L0_attn_ln1_w", l, "ln1_in")
                by_channel(ln1[:, 1, :], "L0_attn_ln1_b", l, "ln1_in")
                hold(sp, s["qkv_pe"], 8 * NC * l)
                matrix(at_w[:, :, :], "L0_attn_attn_w", l, "at_w_in")

            def load_attention_biases(l):
                hold(sp, s["biased"], CT * NC * l)
                hold(sp, s["pb_done"], NC * l)
                sp.dma_start(at_b[:, :], d["L0_attn_attn_b"][l].partition_broadcast(P)).then_inc(s["at_s_in"], 16)
                sp.dma_start(ap_b[:, :], d["L0_attn_aproj_b"][l].partition_broadcast(P)).then_inc(s["at_s_in"], 16)

            def load_mlp(l):
                matrix(fc_w[:, :, :], "L0_attn_fc_w", l, "fc_w_in")
                by_channel(fc_b[:, :], "L0_attn_fc_b", l, "fc_w_in")
                by_channel(ln2[:, 0, :], "L0_attn_ln2_w", l, "fc_w_in")
                by_channel(ln2[:, 1, :], "L0_attn_ln2_b", l, "fc_w_in")
                hold(sp, s["mm_pe"], 2 * NC * l)
                hold(sp, s["mb_done"], NC * l)
                matrix(mp_w[:, :, :], "L0_attn_mproj_w", l, "mp_w_in")
                sp.dma_start(mp_b[:, :], d["L0_attn_mproj_b"][l].partition_broadcast(P)).then_inc(s["mp_s_in"], 16)

            def load_before(g, parity, start):
                hold(sp, s["biased"], CT * g + CT)
                hold(sp, s["ham_done"], 2 * g - 1)
                last = qkv[:, CT * parity + CT - 1, 1:HW1, :]
                sp.dma_start(dif[1:P, 0, 0, :, :], last[0:P - 1]).then_inc(s["before_in"], 16)
                first = qkv[0:1, 0, 1:HW1, :] if start else qkv[P - 1:P, CT * (1 - parity) + CT - 1, 1:HW1, :]
                sp.dma_start(dif[0:1, 0, 0, :, :], first).then_inc(s["before_in"], 16)

            def load_filter(g, c, parity):
                hold(sp, s["filt_dve"], g - 1)
                sp.dma_start(filt[:, parity, :, :], d["c_filter"][:, :, bass.ds(CW * c, CW)]).then_inc(s[f"filt_in{parity}"], 16)

            def for_chunk(l, c, parity, start=False):
                load_before(NC * l + c, parity, start)
                load_filter(NC * l + c, c, parity)

            def layer(l, last):
                for c in range(NC):
                    if c == 3 and not (isinstance(l, int) and l == 0):
                        hold(sp, s["fc_pe"], FC * NC * l)
                        hold(sp, s["gelu"], FC * NC * l)
                        load_mlp(l)
                    if c == NC - 1 and not last:
                        load_attention(l + 1)
                    for_chunk(l, c, c % 2, c == 0)

            sp.dma_start(xc[:, 0], x_in[:, 0]).then_inc(s["x_in0"], 16)
            sp.dma_start(ident[:, :], d["c_ident"]).then_inc(s["ident_in"], 16)
            load_attention(0)
            load_attention_biases(0)
            for c in range(1, NC):
                sp.dma_start(xc[:, c], x_in[:, c]).then_inc(s["x_rest"], 16)
            sp.dma_start(heads[:, :, :], d["c_heads"].rearrange("(k p) n -> p k n", p=P)).then_inc(s["heads_in"], 16)
            for l in range(L):
                sp.dma_start(hid[:, 2 * l:2 * l + 2, 0:E],
                             d["L0_attn_aproj_w"][l].rearrange("(k p) n -> p k n", p=P)).then_inc(s["ap_in"], 16)
            load_mlp(0)
            layer(0, False)
            with sp.Fori(1, L - 1) as l:
                load_attention_biases(l)
                layer(l, False)
            load_attention_biases(L - 1)
            layer(L - 1, True)

        @block.tensor
        def _(pe):
            def turn(rows_of, done):
                for e in range(EH):
                    for t in range(CT):
                        mm = pe.transpose(bank[e][:, t * P:(t + 1) * P], rows_of[:, t, e * P:(e + 1) * P], ident[:, :])
                mm.then_inc(s[done], 1)

            def compose_back():
                pe.wait_ge(s["heads_in"], 16)
                pe.wait_ge(s["ap_in"], 16 * L)
                for l in range(L):
                    for e in range(EH):
                        for k in range(EH):
                            mm = pe.matmul(bank[2 + l][:, e * E:(e + 1) * E], heads[:, k, e * P:(e + 1) * P],
                                           hid[:, 2 * l + k, 0:E], start=(k == 0), stop=(k == EH - 1))
                mm.then_inc(s["back_pe"], 1)

            def step(n, parity):
                if on(n - 2):
                    after(pe, s["ham_done"], 2 * (n - 1))
                    after(pe, s["t1_act"], n + 1 if not isinstance(n, int) else min(n + 1, NG))
                    turn(ham, "tp_pe")
                if on(n):
                    after(pe, s["t1_act"], n + 1)
                    after(pe, s["at_w_in"], 16 * (n // NC + 1))
                    after(pe, s["filt_dve"], n - 2)
                    for t in range(CT):
                        for j in range(2):
                            if t:
                                after(pe, s["qkv_act"], 8 * n + (2 * t + j - 1))
                            for k in range(EH):
                                mm = pe.matmul(bank[6 + j][:, 0:W2], xt1[:, k, t * P:(t + 1) * P],
                                               at_w[:, k, W2 * j:W2 * j + W2], start=(k == 0), stop=(k == EH - 1))
                            mm.then_inc(s["qkv_pe"], 1)
                if on(n - 3):
                    after(pe, s["ln2_done"], n - 2)
                    after(pe, s["tp_act"], n - 1 if not isinstance(n, int) else min(n - 1, NG))
                    turn(xn, "t2_pe")
                if on(n - 2):
                    after(pe, s["tp_act"], n - 1)
                    if on(n):
                        after(pe, s["qkv_act"], 8 * n + 8)
                    else:
                        after(pe, s["filt_dve"], n - 2)
                    for e in range(EH):
                        for k in range(EH):
                            mm = pe.matmul(bank[6 + e][:, :], heads[:, k, e * P:(e + 1) * P], ham_t[:, k, :],
                                           start=(k == 0), stop=(k == EH - 1))
                    mm.then_inc(s["r_pe"], 1)
                if on(n - 3):
                    after(pe, s["t2_act"], n - 2)
                    after(pe, s["fc_w_in"], 64 * ((n - 3) // NC + 1))
                    after(pe, s["res1"], n - 2)
                    for f in range(FC):
                        if f > 1:
                            after(pe, s["gelu"], FC * (n - 3) + (f - 1))
                        for k in range(EH):
                            mm = pe.matmul(bank[2 + f % 2][:, :], fc_w[:, k, f * P:(f + 1) * P], xt2[:, k, :],
                                           start=(k == 0), stop=(k == EH - 1))
                        mm.then_inc(s["fc_pe"], 1)
                if on(n + 1):
                    after(pe, s["ln1_done"], n + 2)
                    after(pe, s["t2_act"], n - 2)
                    after(pe, s["tp_act"], n - 1)
                    turn(xn, "t1_pe")
                if isinstance(n, int) and n == 1:
                    compose_back()
                if isinstance(n, int) and n == 2:
                    pe.wait_ge(s["back_act"], 1)
                if on(n - 3):
                    after(pe, s["gelu"], FC * (n - 2))
                if on(n - 2):
                    after(pe, s["filt_dve"], n - 1)
                    for b in range(2):
                        for t in range(2):
                            at = (2 * b + t) * P
                            for k in range(EH):
                                mm = pe.matmul(bank[2 + b][:, t * E:(t + 1) * E], coef[:, k, at:at + P],
                                               back_w[:, bass.ds((n - 2) // NC, 1), k, :].rearrange("p l e -> p (l e)"),
                                               start=(k == 0), stop=(k == EH - 1))
                    mm.then_inc(s["g_pe"], 1)
                if on(n - 3):
                    after(pe, s["mp_w_in"], 16 * ((n - 3) // NC + 1))
                    after(pe, s["res2"], n - 3)
                    for b in range(2):
                        for t in range(2):
                            at = (2 * b + t) * P
                            for f in range(FC):
                                mm = pe.matmul(bank[4 + b][:, t * E:(t + 1) * E], hid[:, f, at:at + P],
                                               mp_w[:, f, :], start=(f == 0), stop=(f == FC - 1))
                        mm.then_inc(s["mm_pe"], 1)

            pe.wait_ge(s["ident_in"], 16)
            steps(pe, step)

        @block.scalar
        def _(act):
            def turned(ln, to, done):
                for e in range(EH):
                    ins = nc.scalar.activation(to[:, e, :], bank[e][:, :], ACT.Identity,
                                               bias=ln[:, 1, e:e + 1], scale=ln[:, 0, e:e + 1])
                ins.then_inc(s[done], 1)

            def whole_turns(g, b, parity):
                i = 2 * g + b
                a = CT * parity + 2 * b
                to = turns1[:, :, :, :] if b else cosv[:, 0, :, :, :]
                k = s["turn_step"]
                after(act, s["biased"], CT * g + 2 * b + 2)
                after(act, s["prep"], i - 1)
                if not b:
                    after(act, s["ham_done"], i - 1)
                    after(act, s["third_done"], i - 1)
                nc.scalar.activation(to, qkv[:, a:a + 2, 1:HW1, :], ACT.Identity, scale=TURN,
                                     bias=quarter[:, 0:1]).then_inc(k, 1)
                act.wait_ge(k, 2 * i + 1)
                nc.scalar.activation(whole[:, b, :, :, :], to, ACT.Identity,
                                     bias=up_to_whole[:, 0:1]).then_inc(k, 1)
                act.wait_ge(k, 2 * i + 2)
                nc.scalar.activation(whole[:, b, :, :, :], whole[:, b, :, :, :], ACT.Identity,
                                     bias=down_again[:, 0:1]).then_inc(s["whole_done"], 1)

            def sine(half_index, b):
                after(act, s["prep"], half_index + 1)
                nc.scalar.activation(cosv[:, b, :, :, :], cosv[:, b, :, :, :], ACT.Sin,
                                     scale=TWO_PI).then_inc(s["cosd"], 1)

            def step(n, parity):
                if on(n - 2):
                    after(act, s["tp_pe"], n - 1)
                    for e in range(EH):
                        ins = nc.scalar.activation(ham_t[:, e, :], bank[e][:, :], ACT.Copy)
                    ins.then_inc(s["tp_act"], 1)
                if on(n):
                    after(act, s["ham_done"], 2 * (n - 1))
                    for t in range(CT):
                        for j in range(2):
                            after(act, s["qkv_pe"], 8 * n + (2 * t + j + 1))
                            to = qkv[:, CT * parity + t, 1 + 8 * j:9 + 8 * j, :]
                            nc.scalar.activation(to.rearrange("p h w -> p (h w)"), bank[6 + j][:, 0:W2],
                                                 ACT.Copy).then_inc(s["qkv_act"], 1)
                        if t == 0 and on(n - 1):
                            sine(2 * (n - 1), 0)
                elif on(n - 1):
                    sine(2 * (n - 1), 0)
                if on(n - 3):
                    after(act, s["fc_w_in"], 64 * ((n - 3) // NC + 1))
                    after(act, s["t2_pe"], n - 2)
                    turned(ln2, xt2, "t2_act")
                if on(n - 1):
                    sine(2 * (n - 1) + 1, 1)
                if on(n - 3):
                    for f in range(FC):
                        after(act, s["fc_pe"], FC * (n - 3) + (f + 1))
                        if f == 0:
                            after(act, s["mm_pe"], 2 * (n - 3))
                        nc.scalar.activation(hid[:, f, :], bank[2 + f % 2][:, :], ACT.Gelu,
                                             bias=fc_b[:, f:f + 1]).then_inc(s["gelu"], 1)
                if on(n + 1):
                    after(act, s["ln1_in"], 32 * ((n + 1) // NC + 1))
                    after(act, s["t1_pe"], n + 2)
                    after(act, s["qkv_pe"], 8 * n + 8)
                    turned(ln1, xt1, "t1_act")
                if on(n):
                    whole_turns(n, 0, parity)
                    whole_turns(n, 1, parity)
                if isinstance(n, int) and n == 1:
                    act.wait_ge(s["back_pe"], 1)
                    for l in range(L):
                        ins = nc.scalar.activation(back_w[:, l, :, :].rearrange("p k n -> p (k n)"),
                                                   bank[2 + l][:, :], ACT.Copy)
                    ins.then_inc(s["back_act"], 1)

            act.wait_ge(s["zeroed"], 4)
            steps(act, step)

        @block.gpsimd
        def _(pool):
            def minus(o, a, b):
                return nc.gpsimd.tensor_tensor(o, a, b, ALU.subtract)

            def plus(o, a, b):
                return nc.gpsimd.tensor_tensor(o, a, b, ALU.add)

            def copy(o, a):
                return nc.gpsimd.tensor_scalar(o, a, 1.0, 1.0, ALU.mult, ALU.mult)

            def prep(i, b, parity):
                a = CT * parity + 2 * b
                hold(pool, s["ham_done"], i - 1)
                if b:
                    minus(dif[:, b, :, :, :], qkv[:, a:a + 2, 1:HW1, :], qkv[:, a - 1:a + 1, 1:HW1, :])
                else:
                    minus(dif[:, b, 1, :, :], qkv[:, a + 1, 1:HW1, :], qkv[:, a, 1:HW1, :])
                    hold(pool, s["before_in"], 16 * i + 32)
                    minus(dif[:, b, 0, :, :], qkv[:, a, 1:HW1, :], dif[:, b, 0, :, :])
                hold(pool, s["whole_done"], i + 1)
                turns = turns1[:, :, :, :] if b else cosv[:, 0, :, :, :]
                minus(cosv[:, b, :, :, :], turns, whole[:, b, :, :, :]).then_inc(s["prep"], 1)

            def third_part(g, b, parity):
                i = 2 * g + b
                B, C = quaternions(b, parity)[1:]
                to, other = third[:, b, :, :, :], term[:, :, :, :]
                k = s["third_step"]
                hold(pool, s["cosd"], i + 1)
                hold(pool, s["ham_done"], i - 1)
                hold(pool, s["third_done"], i)
                nc.gpsimd.tensor_tensor(other, B[1], C[2], ALU.mult)
                nc.gpsimd.tensor_tensor(to, B[0], C[3], ALU.mult).then_inc(k, 1)
                for j, (p, q, f) in enumerate(((B[2], C[1], ALU.add), (B[3], C[0], ALU.subtract), (None, None, ALU.add))):
                    hold(pool, k, 5 * i + (2 * j + 1))
                    ins = nc.gpsimd.tensor_tensor(to, to, other, f)
                    ins.then_inc(s["third_done"] if p is None else k, 1)
                    if p is not None:
                        hold(pool, k, 5 * i + (2 * j + 2))
                        nc.gpsimd.tensor_tensor(other, p, q, ALU.mult).then_inc(k, 1)

            def rstd(n_eps, mv, rs, done):
                nc.gpsimd.tensor_scalar(ve[:, :], mv[:, :, 1], EPS, 0.0, ALU.add, ALU.add).then_inc(s["eps"], 1)
                hold(pool, s["eps"], n_eps)
                nc.gpsimd.tensor_tensor(rs[:, :], ve[:, :], half[:, :], ALU.pow).then_inc(s[done], 1)

            def add_row(g, b, done):
                now = xc[:, bass.ds(g % NC, 1), :, :].rearrange("p c t e -> p (c t) e")
                nc.gpsimd.tensor_tensor(now, now, b[:, :].unsqueeze(1).broadcast_to([P, CT, E]),
                                        ALU.add).then_inc(s[done], 1)

            def step(n, parity):
                ones = lambda g: g + 1 + (min(g + 1, NC) if isinstance(g, int) else NC)
                if on(n + 1):
                    g = n + 1
                    twos = max(0, min(n - 2, NG)) if isinstance(n, int) else n - 2
                    if isinstance(g, int) and g < NC:
                        hold(pool, s["var1"], ones(g) - 1)
                        rstd(ones(g) - 1 + twos, mv1, rs1, "rs1_pool")
                        hold(pool, s["rs1_pool"], ones(g) - 1)
                    hold(pool, s["var1"], ones(g))
                    rstd(ones(g) + twos, mv1, rs1, "rs1_pool")
                    hold(pool, s["rs1_pool"], ones(g))
                if on(n - 1):
                    prep(2 * (n - 1) + 1, 1, 1 - parity)
                    third_part(n - 1, 0, 1 - parity)
                if on(n):
                    hold(pool, s["at_s_in"], 32 * (n // NC + 1))
                    for t in range(CT):
                        a = CT * parity + t
                        rows_of = qkv[:, a, 1:HW1, :].rearrange("p h w -> p (h w)")
                        hold(pool, s["qkv_act"], 8 * n + (2 * t + 2))
                        plus(rows_of, rows_of, at_b[:, :]).then_inc(s["added"], 1)
                        hold(pool, s["added"], CT * n + (t + 1))
                        copy(qkv[:, a, 0, :], qkv[:, a, H, :]).then_inc(s["biased"], 1)
                if on(n - 1):
                    third_part(n - 1, 1, 1 - parity)
                if on(n - 3):
                    hold(pool, s["mp_s_in"], 16 * ((n - 3) // NC + 1))
                    hold(pool, s["ln2_done"], n - 2)
                    add_row(n - 3, mp_b, "mb_done")
                if on(n):
                    hold(pool, s["ln1_done"], n + 1)
                    add_row(n, ap_b, "pb_done")
                    hold(pool, s["biased"], CT * n + CT)
                    prep(2 * n, 0, parity)
                if on(n - 2):
                    hold(pool, s["var2"], n - 1)
                    g1 = min(n + 2, NG) if isinstance(n, int) else n + 2
                    done1 = g1 + (min(g1, NC) if isinstance(n, int) else NC)
                    rstd(done1 + (n - 1), mv2, rs2, "rs2_pool")
                    hold(pool, s["rs2_pool"], n - 1)

            for to, v in ((half, -0.5), (quarter, 0.25), (up_to_whole, ROUND), (down_again, -ROUND)):
                nc.gpsimd.memset(to[:, :], v).then_inc(s["zeroed"], 1)
            pool.wait_ge(s["zeroed"], 4)
            steps(pool, step)

        @block.vector
        def _(dve):
            def tile(g, t):
                return xc[:, bass.ds(g % NC, 1), t, :].rearrange("p c e -> p (c e)")

            def stats(g, mv, done):
                dve.drain()
                for t in range(CT):
                    nc.vector.bn_stats(stat[:, t, :], tile(g, t))
                dve.drain()
                for t in range(CT):
                    ins = nc.vector.bn_aggr(mv[:, t, :], stat[:, t, :])
                ins.then_inc(s[done], 1)

            def norm(g, to, mv, rs, done=None):
                for t in range(CT):
                    ins = nc.vector.tensor_scalar(to(t), tile(g, t), mv[:, t, 0:1], rs[:, t:t + 1],
                                                  ALU.subtract, ALU.mult)
                if done is not None:
                    ins.then_inc(s[done], 1)

            def add_banks(g, b0, done, each):
                for b in range(2):
                    each(b)
                    now = xc[:, bass.ds(g % NC, 1), 2 * b:2 * b + 2, :].rearrange("p c t e -> p (c t e)")
                    ins = nc.vector.tensor_tensor(now, now, bank[b0 + b][:, :], ALU.add)
                ins.then_inc(s[done], 1)

            def hamilton(g, b, parity):
                i = 2 * g + b
                a = CT * parity + 2 * b
                ext = lambda j: qkv[:, a:a + 2, :, HD * j:HD * j + HD]
                A, B, C = quaternions(b, parity)
                to = ham[:, 2 * b:2 * b + 2, :].rearrange("p t (h d) -> p t h d", h=H)
                t0 = hb[0][:, :, :, :]
                u, v, z, acc, w = [hb[j][:, :, :, :] for j in range(1, 6)]
                mul, add, sub = ALU.mult, ALU.add, ALU.subtract
                base = 26 * i

                def op(o, i0, i1, f, last=None):
                    if last is not None:
                        after(dve, s["ham_step"], base + (last + 1))
                    nc.vector.tensor_tensor(o, i0, i1, f).then_inc(s["ham_step"], 1)

                after(dve, s["ham_done"], i)
                after(dve, s["cosd"], i + 1)
                op(t0, ext(1), ext(2), mul)
                op(u, B[1], C[1], mul)
                op(v, B[3], C[3], mul)
                op(acc, t0[:, :, 1:HW1, :], t0[:, :, 0:H, :], sub, 0)
                op(z, B[0], C[1], mul)
                op(u, u, v, add, 2)
                op(v, B[1], C[0], mul, 5)
                op(w, B[2], C[3], mul)
                op(acc, acc, u, sub)
                op(z, z, v, add, 6)
                op(u, B[3], C[2], mul, 8)
                op(v, B[0], C[2], mul, 9)
                after(dve, s["tp_pe"], g)
                op(to, A[0], acc, mul)
                op(acc, z, w, add, 12)
                op(z, B[1], C[3], mul, 13)
                op(w, B[2], C[0], mul)
                op(acc, acc, u, sub)
                op(v, v, z, sub, 14)
                op(u, B[3], C[1], mul, 16)
                op(acc, A[1], acc, mul)
                op(v, v, w, add, 17)
                after(dve, s["third_done"], i + 1)
                op(z, A[3], third[:, b, :, :, :], mul)
                op(to, to, acc, sub, 19)
                op(v, v, u, add, 20)
                op(to, to, z, sub, 22)
                op(v, A[2], v, mul, 23)
                dve.wait_ge(s["ham_step"], base + 26)
                nc.vector.tensor_tensor(to, to, v, sub).then_inc(s["ham_done"], 1)

            def step(n, parity):
                first_norm = isinstance(n, int) and n + 1 < NC
                if on(n + 1):
                    if first_norm:
                        dve.wait_ge(*((s["x_in0"], 16) if n < 0 else (s["x_rest"], 16 * (NC - 1))))
                        stats(n + 1, mv1, "var1")
                        dve.wait_ge(s["rs1_pool"], 2 * (n + 1) + 1)
                        norm(n + 1, lambda t: tile(n + 1, t), mv1, rs1)
                    stats(n + 1, mv1, "var1")
                if on(n - 3):
                    after(dve, s["rs2_pool"], n - 2)
                    after(dve, s["t1_pe"], min(n + 1, NG) if isinstance(n, int) else n + 1)
                    norm(n - 3, lambda t: xn[:, t, :], mv2, rs2, "ln2_done")
                if on(n - 1):
                    hamilton(n - 1, 0, 1 - parity)
                if on(n - 4):
                    after(dve, s["mb_done"], n - 3)
                    add_banks(n - 4, 4, "res2", lambda b: after(dve, s["mm_pe"], 2 * (n - 4) + (b + 1)))
                if on(n - 2):
                    after(dve, s[f"filt_in{parity}"], 16 * ((n - 2) // 2 + 1))
                    after(dve, s["r_pe"], n - 1)
                    after(dve, s["g_pe"], n - 2)
                    for e in range(EH):
                        ins = nc.vector.tensor_tensor(
                            coef[:, e, :], bank[6 + e][:, :],
                            filt[:, parity, e, :], ALU.mult)
                    ins.then_inc(s["filt_dve"], 1)
                if on(n + 1):
                    after(dve, s["rs1_pool"], 2 * (n + 2) if first_norm else n + 2 + NC)
                    after(dve, s["t1_pe"], n + 1)
                    after(dve, s["t2_pe"], n - 2)
                    norm(n + 1, lambda t: xn[:, t, :], mv1, rs1, "ln1_done")
                if on(n - 1):
                    hamilton(n - 1, 1, 1 - parity)
                if on(n - 2):
                    after(dve, s["pb_done"], n - 1)
                    after(dve, s["g_pe"], n - 1)
                    add_banks(n - 2, 2, "res1", lambda b: None)
                    stats(n - 2, mv2, "var2")

            steps(dve, step)


def tail(nc, d, out, x, ident, bank):
    with ExitStack() as ctx:
        def sb(name, *shape):
            return ctx.enter_context(nc.sbuf_tensor(name, [P, *shape], F32))

        arena = sb("arena", NX // 2 * XW + NT * PAY)
        xt = arena[:, 0:EH * S].rearrange("p (k s) -> p k s", k=EH)
        a0 = EH * S
        ew = arena[:, a0:a0 + EH * NX * E].rearrange("p (k x n) -> p k x n", k=EH, x=NX)
        a0 += EH * NX * E
        uw, vw = (arena[:, a0 + i * EH * D1:a0 + (i + 1) * EH * D1].rearrange("p (k n) -> p k n", k=EH)
                  for i in range(2))
        ow = arena[:, a0 + 2 * EH * D1:a0 + 2 * EH * D1 + MC * E].rearrange("p (k n) -> p k n", k=MC)
        x0 = arena[:, NX // 2 * XW:NX // 2 * XW + NT * E].rearrange("p (c t e) -> p c t e", c=NC, t=CT)
        pay = arena[:, NX // 2 * XW:].rearrange("p (i w) -> p i w", w=PAY)
        w1 = arena[:, 0:NX * XW].rearrange("p (x w) -> p x w", x=NX)[:, :, 0:EH * F].rearrange("p x (k f) -> p x k f", k=EH)
        w2 = arena[:, 0:NX * XW].rearrange("p (x w) -> p x w", x=NX)[:, :, EH * F:].rearrange("p x (f n) -> p x f n", f=FC)
        eb = sb("eb", CT, E)
        ub = sb("ub", MC)
        vb = sb("vb", MC)
        tz = sb("tz", MC)
        ob = sb("ob", E)
        rw = sb("rw", 2, EH, NX)
        rb = sb("rb", 2, NX)
        prio = sb("prio", NX)
        lng = sb("lng", 2, EH)
        b1 = sb("b1", NX, FC)
        rt = sb("rt", 2, EH, CW)
        rows = sb("rows", 2, CT, E)
        hid = sb("hid2", FC, CW)
        su, sv = hid[:, 0:MC, :], hid[:, MC:2 * MC, :]
        stat = sb("stat2", CT, 6)
        mv = sb("mv", NT, 2)
        ve = sb("ve2", NT)
        sc = [sb(f"sc{i}", NT) for i in range(6)]
        half = sb("half2", 3, NT)
        lg = sb("lg", NT, NX)
        ex = sb("ex", NT, NX)
        pick = sb("pick", NT, NX)
        mg = sb("mg", NT, NX)
        mx = sb("mx", NT)
        gate = sb("gate", NT)
        mgt = sb("mgt", 2, P)
        low = sb("low", P)
        ones = sb("ones", P)
        count = sb("count", NX)
        tiles = sb("tiles", NX)
        ends = [sb("ends0", NX), sb("ends1", NX)]
        owner = sb("owner", SLOTS)
        slot_no = sb("slot_no", SLOTS)
        token = sb("token", NT)
        dest = sb("dest", NT)
        dest_i = ctx.enter_context(nc.sbuf_tensor("dest_i", [P, NT], I32))
        toki = ctx.enter_context(nc.sbuf_tensor("toki", [P, 2], I32))
        owner_i = ctx.enter_context(nc.sbuf_tensor("owner_i", [1, SLOTS], I32))

        names = """x0_in x0_rest added ew_in rw_in at_in e2_in moments small rows_done turned evac
            logits eb_in zero picked expd mgt_pe mgt_act bias_pe bias_dve ex_pe ex_dve held2
            pool2 u_pe u_act prod o_pe o_dve ahead ob_done
            filled w_in b2_in const_in ranks_pe dest_done owners sent n_in0 n_in1 r_in0 r_in1
            xs_pe xs_act hr_pe hr_dve ht_pe ht_act y_pe y_dve out0 out1 held3""".split()
        s = {n: ctx.enter_context(nc.semaphore("f_" + n)) for n in names}
        by_row = "b (c p t) e -> p (b c) t e"
        x_in = d["L0_attn_x"].rearrange(by_row, p=P, t=CT)
        out_rows = out.rearrange("b s e -> (b s) e")
        order = nc.dram_tensor("order", [SLOTS * P, PAY], F32).ap()
        h_rows = hid[:, 0:2, :].rearrange("p f n -> p (f n)")
        h_t = hid[:, 2:4, :].rearrange("p f n -> p (f n)").rearrange("p (f n) -> p f n", f=FC)
        xn_t = hid[:, 4, 0:EH * P].rearrange("p (k n) -> p k n", k=EH)
        y_b = hid[:, 5, 0:E]
        ge = hid[:, 6, 0:SLOTS * NX].rearrange("p (n x) -> p n x", x=NX)
        b2 = rt[:, :, :, :].rearrange("p a k n -> p (a k n)").rearrange("p (x e) -> p x e", x=NX)
        in_n = [rows[:, 0, b, :] for b in range(2)]
        in_r = [rows[:, b, 2:4, :].rearrange("p t e -> p (t e)")[:, 0:PAY - E] for b in range(2)]
        res = [rows[:, 1, b, :] for b in range(2)]
        tok = [toki[:, b:b + 1] for b in range(2)]
        xc = x[:, :, :].rearrange("p (c t) e -> p c t e", t=CT)

        def after(eng, what, value):
            if not isinstance(value, int) or value > 0:
                eng.wait_ge(what, value)

        def slots(eng, step):
            for n in range(-1, 4):
                step(n, n % 2)
            with eng.Fori(2, SLOTS // 2 - 1) as pair:
                for b in range(2):
                    step(2 * pair + b, b)
            for n in range(SLOTS - 2, SLOTS + 1):
                step(n, n % 2)

        block = ctx.enter_context(nc.Block())

        @block.sync
        def _(sp):
            sp.dma_start(x0[:, 0], x_in[:, 0]).then_inc(s["x0_in"], 16)
            for c in range(1, NC):
                sp.dma_start(x0[:, c], x_in[:, c]).then_inc(s["x0_rest"], 16)
            for i in range(SLOTS):
                sp.dma_start(order[P * i:P * i + P, :], d["c_fill"]).then_inc(s["filled"], 16)
            for i, (w, b) in enumerate((("L0_ffn_router_w", "L0_ffn_router_b"), ("L1_ffn_Wr", "L1_ffn_br"))):
                sp.dma_start(rw[:, i, :, :], d[w].rearrange("(k p) n -> p k n", p=P)).then_inc(s["rw_in"], 16)
                sp.dma_start(rb[:, i, :], d[b].partition_broadcast(P)).then_inc(s["rw_in"], 16)
            sp.dma_start(prio[:, :], d["c_prio"].partition_broadcast(P)).then_inc(s["rw_in"], 16)
            for k in range(EH):
                sp.dma_start(ew[:, k, :, :], d["L0_ffn_expert_w"][:, k * P:(k + 1) * P, :].rearrange("x p n -> p x n")).then_inc(s["ew_in"], 16)
            sp.wait_ge(s["zero"], 1)
            for t in range(CT):
                sp.dma_start(eb[NX * t:NX * t + NX, t, :], d["L0_ffn_expert_b"]).then_inc(s["eb_in"], 16)
            for to, name in ((uw, "L1_attn_u_w"), (vw, "L1_attn_v_w"), (ow, "L1_attn_o_w")):
                sp.dma_start(to[:, :, :], d[name].rearrange("(k p) n -> p k n", p=P)).then_inc(s["at_in"], 16)
            for to, name in ((ub, "L1_attn_u_b"), (vb, "L1_attn_v_b")):
                sp.dma_start(to[:, :], d[name].rearrange("(k p) -> p k", p=P), allow_slow_non_contiguous=True).then_inc(s["at_in"], 16)
            heads = d["L1_attn_t_zero"].rearrange("(m h) o -> h (m o)", h=2)
            for h in range(2):
                sp.dma_start(tz[64 * h:64 * h + 64, :], heads[h].partition_broadcast(64), allow_slow_non_contiguous=True).then_inc(s["at_in"], 16)
            sp.dma_start(ob[:, :], d["L1_attn_o_b"].partition_broadcast(P)).then_inc(s["at_in"], 16)
            for i, name in enumerate(("L1_ffn_ln_g", "L1_ffn_ln_b")):
                sp.dma_start(lng[:, i, :], d[name].rearrange("(k p) -> p k", p=P), allow_slow_non_contiguous=True).then_inc(s["e2_in"], 16)
            sp.dma_start(b1[:, :, :], d["L1_ffn_b1"].rearrange("x (f p) -> p x f", p=P), allow_slow_non_contiguous=True).then_inc(s["e2_in"], 16)
            sp.dma_start(low[:, :], d["c_low"]).then_inc(s["const_in"], 16)
            sp.dma_start(slot_no[:, :], d["c_slot"].partition_broadcast(P)).then_inc(s["const_in"], 16)
            sp.dma_start(token[:, :], d["c_token"]).then_inc(s["const_in"], 16)
            sp.wait_ge(s["o_pe"], NC)

            def load(e):
                sp.dma_start(w1[:, e, :, :], d["L1_ffn_W1"][e].rearrange("(k p) f -> p k f", p=P)).then_inc(s["w_in"], 16)
                sp.dma_start(w2[:, e, :, :], d["L1_ffn_W2"][e].rearrange("(k p) f -> p k f", p=P)).then_inc(s["w_in"], 16)

            for e in range(NX // 2):
                load(e)
                sp.wait_ge(s["w_in"], 32 * (e + 1))
            sp.wait_ge(s["logits"], 2 * NC)
            sp.dma_start(b2, d["L1_ffn_b2"].rearrange("x e -> (x e)").partition_broadcast(P)).then_inc(s["b2_in"], 16)

            def fetch(n, b, first):
                if not first:
                    sp.wait_ge(s["xs_pe"], n - 1)
                    sp.sem_inc(s["held3"], 1)
                sp.dma_start(in_n[b], order[bass.ds(P * n, P), 0:E]).then_inc(s[f"n_in{b}"], 16)
                if not first:
                    sp.wait_ge(s["y_dve"], n - 1)
                    sp.sem_inc(s["held3"], 1)
                sp.dma_start(in_r[b], order[bass.ds(P * n, P), E:PAY]).then_inc(s[f"r_in{b}"], 16)

            sp.wait_ge(s["sent"], 16 * NT)
            fetch(0, 0, True)
            fetch(1, 1, True)
            for e in range(NX // 2, NX):
                load(e)
                sp.wait_ge(s["w_in"], 32 * (e + 1))
            with sp.Fori(1, SLOTS // 2) as pair:
                for b in range(2):
                    fetch(2 * pair + b, b, False)

        @block.tensor
        def _(pe):
            def turn(n, c, of=None):
                pe.wait_ge(s["rows_done"], n + 1)
                if n:
                    pe.wait_ge(s["evac"], n)
                for e in range(EH):
                    for t in range(CT):
                        mm = pe.transpose(bank[e][:, t * P:(t + 1) * P], (of(t) if of else rows[:, n % 2, t, :])[:, e * P:(e + 1) * P], ident[:, :])
                mm.then_inc(s["turned"], 1)

            def route(i, n, c, of):
                pe.wait_ge(s["evac"], n + 1)
                for t in range(CT):
                    for k in range(EH):
                        mm = pe.matmul(bank[2][:, NX * (CT * c + t):NX * (CT * c + t + 1)],
                                       of[:, k, t * P:(t + 1) * P], rw[:, i, k, :], start=(k == 0), stop=(k == EH - 1))
                mm.then_inc(s["logits"], 1)

            def biases(i):
                for c in range(NC):
                    n = NC * i + c
                    if c == 0:
                        pe.wait_ge(s["picked"], i + 1)
                        pe.wait_ge(s["evac"], NC * (1 + 2 * i))
                    if n:
                        pe.wait_ge(s["mgt_act"], n)
                    pe.transpose(bank[0][0:NX * CT, 0:P], mg[:, CT * c:CT * c + CT, :].rearrange("p t x -> p (t x)"),
                                 ident[:, :]).then_inc(s["mgt_pe"], 1)
                    pe.wait_ge(s["mgt_act"], n + 1)
                    if n:
                        pe.wait_ge(s["bias_dve"], n)
                    for t in range(CT):
                        mm = pe.matmul(bank[4 + t // 2][:, (t % 2) * E:(t % 2 + 1) * E], mgt[0:NX * CT, n % 2, :],
                                       eb[0:NX * CT, t, :], start=True, stop=True)
                    mm.then_inc(s["bias_pe"], 1)

            pe.wait_ge(s["rw_in"], 16 * 5)
            for c in range(NC):
                turn(c, c)
                if c:
                    route(0, c - 1, c - 1, xt[:, :, CW * (c - 1):CW * c])
            route(0, NC - 1, NC - 1, xt[:, :, CW * (NC - 1):CW * NC])
            pe.wait_ge(s["eb_in"], 16 * CT)
            biases(0)
            pe.wait_ge(s["ew_in"], 32)
            pe.wait_ge(s["bias_dve"], NC)
            for i in range(NT):
                if i > 1:
                    pe.wait_ge(s["ex_dve"], i - 1)
                for q in range(4):
                    for k in range(EH):
                        mm = pe.matmul(bank[4 * (i % 2) + q][:, :], xt[:, k, P * i:P * i + P],
                                       ew[:, k, 2 * q:2 * q + 2, :].rearrange("p x n -> p (x n)"),
                                       start=(k == 0), stop=(k == EH - 1))
                mm.then_inc(s["ex_pe"], 1)
            pe.wait_ge(s["at_in"], 16 * 8)
            pe.wait_ge(s["ex_dve"], NT)

            def project(c):
                pe.wait_ge(s["prod"], c + 1)
                if c:
                    pe.wait_ge(s["o_dve"], c)
                for t in range(CT):
                    for m in range(MC):
                        mm = pe.matmul(bank[6 + t // 2][:, (t % 2) * E:(t % 2 + 1) * E], su[:, m, t * P:(t + 1) * P],
                                       ow[:, m, :], start=(m == 0), stop=(m == MC - 1))
                mm.then_inc(s["o_pe"], 1)

            for c in range(NC):
                turn(NC + c, c)
                if c:
                    project(c - 1)
                pe.wait_ge(s["evac"], NC + c + 1)
                for m in range(MC):
                    for j, w in enumerate((uw, vw)):
                        q = 2 * m + j
                        n = 8 * c + q
                        if n >= 4:
                            pe.wait_ge(s["u_act"], n - 3)
                        for k in range(EH):
                            mm = pe.matmul(bank[2 + q % 4][:, :], w[:, k, m * P:(m + 1) * P], rt[:, c % 2, k, :],
                                           start=(k == 0), stop=(k == EH - 1))
                        mm.then_inc(s["u_pe"], 1)
            project(NC - 1)
            pe.wait_ge(s["u_act"], 8 * NC)
            for c in range(NC):
                turn(2 * NC + c, c, lambda t: pay[:, CT * c + t, 0:E])
                route(1, 2 * NC + c, c, rt[:, c % 2])
            pe.wait_ge(s["picked"], 2)
            pe.wait_ge(s["const_in"], 48)
            picked = pick[:, :, :].rearrange("p t x -> p (t x)")
            pe.matmul(bank[4][:, 0:NT * NX], low[:, :], picked, start=True, stop=True)
            pe.matmul(bank[5][:, 0:NT * NX], ones[:, :], picked, start=True, stop=True).then_inc(s["ranks_pe"], 1)

            def expert(n):
                return pe.value_load(owner_i[0:1, bass.ds(n, 1)], min_val=0, max_val=NX - 1)

            def step(n, b):
                up = not isinstance(n, int) or 0 <= n < SLOTS
                down = not isinstance(n, int) or n > 0
                if up:
                    e = expert(n)
                    after(pe, s["xs_act"], n + 1)
                    after(pe, s["w_in"], 32 * (e + 1))
                    after(pe, s["hr_dve"], n)
                    for q in range(2):
                        for k in range(EH):
                            mm = pe.matmul(bank[1 + q][:, :], xn_t[:, k, :],
                                           w1[:, bass.ds(e, 1), k, 512 * q:512 * q + 512].rearrange("p x f -> p (x f)"),
                                           start=(k == 0), stop=(k == EH - 1))
                    mm.then_inc(s["hr_pe"], 1)
                if not isinstance(n, int) or n + 1 < SLOTS:
                    after(pe, s[f"n_in{1 - b}"], 16 * ((n + 1) // 2 + 1))
                    after(pe, s["xs_act"], n + 1)
                    for k in range(EH):
                        mm = pe.transpose(bank[0][:, k * P:(k + 1) * P], in_n[1 - b][:, k * P:(k + 1) * P], ident[:, :])
                    mm.then_inc(s["xs_pe"], 1)
                if down:
                    e = expert(n - 1)
                    after(pe, s["ht_act"], n)
                    after(pe, s["y_dve"], n - 1)
                    for f in range(FC):
                        mm = pe.matmul(bank[5][:, 0:E], h_t[:, f, :], w2[:, bass.ds(e, 1), f, :].rearrange("p x n -> p (x n)"),
                                       start=(f == 0), stop=(f == FC - 1))
                    mm.then_inc(s["y_pe"], 1)
                if up:
                    after(pe, s["hr_dve"], n + 1)
                    after(pe, s["ht_act"], n)
                    for f in range(FC):
                        mm = pe.transpose(bank[3 + f // 4][:, (f % 4) * P:(f % 4 + 1) * P], h_rows[:, f * P:(f + 1) * P], ident[:, :])
                    mm.then_inc(s["ht_pe"], 1)

            pe.wait_ge(s["owners"], 1)
            slots(pe, step)

        @block.scalar
        def _(act):
            def evac(n, to):
                act.wait_ge(s["turned"], n + 1)
                for e in range(EH):
                    ins = nc.scalar.activation(to(e), bank[e][:, :], ACT.Copy)
                return ins

            def softmax(i):
                act.wait_ge(s["expd"], 2 * i + 1)
                nc.scalar.activation(ex[:, :, :], lg[:, :, :], ACT.Exp).then_inc(s["expd"], 1)

            def turn_gates(i):
                for c in range(NC):
                    n = NC * i + c
                    act.wait_ge(s["mgt_pe"], n + 1)
                    if n > 1:
                        act.wait_ge(s["bias_pe"], n - 1)
                    nc.scalar.activation(mgt[0:NX * CT, n % 2, :], bank[0][0:NX * CT, 0:P], ACT.Copy).then_inc(s["mgt_act"], 1)

            for c in range(NC):
                evac(c, lambda e: xt[:, e, CW * c:CW * c + CW]).then_inc(s["evac"], 1)
            softmax(0)
            turn_gates(0)
            act.wait_ge(s["at_in"], 16 * 8)
            for c in range(NC):
                if c > 1:
                    act.wait_ge(s["u_pe"], 8 * (c - 1))
                evac(NC + c, lambda e: rt[:, c % 2, e, :]).then_inc(s["evac"], 1)
                for q in range(8):
                    if q == 0 and c:
                        act.wait_ge(s["o_pe"], c)
                    act.wait_ge(s["u_pe"], 8 * c + q + 1)
                    to, b = ((su, ub), (sv, vb))[q % 2]
                    nc.scalar.activation(to[:, q // 2, :], bank[2 + q % 4][:, :], ACT.Silu,
                                         bias=b[:, q // 2:q // 2 + 1]).then_inc(s["u_act"], 1)
            act.wait_ge(s["u_pe"], 8 * NC)
            act.wait_ge(s["e2_in"], 48)
            for c in range(NC):
                if c > 1:
                    act.wait_ge(s["logits"], NC + c - 1)
                evac(2 * NC + c, lambda e: rt[:, c % 2, e, :]).then_inc(s["evac"], 1)
            softmax(1)

            def step(n, b):
                if not isinstance(n, int) or n + 1 < SLOTS:
                    after(act, s["xs_pe"], n + 2)
                    after(act, s["hr_pe"], n + 1)
                    for k in range(EH):
                        ins = nc.scalar.activation(xn_t[:, k, :], bank[0][:, k * P:(k + 1) * P], ACT.Identity,
                                                   bias=lng[:, 1, k:k + 1], scale=lng[:, 0, k:k + 1])
                    ins.then_inc(s["xs_act"], 1)
                if not isinstance(n, int) or 0 <= n < SLOTS:
                    e = act.value_load(owner_i[0:1, bass.ds(n, 1)], min_val=0, max_val=NX - 1)
                    after(act, s["ht_pe"], n + 1)
                    after(act, s["y_pe"], n)
                    for f in range(FC):
                        ins = nc.scalar.activation(h_t[:, f, :], bank[3 + f // 4][:, (f % 4) * P:(f % 4 + 1) * P], ACT.Relu,
                                                   bias=b1[:, bass.ds(e, 1), f])
                    ins.then_inc(s["ht_act"], 1)

            act.wait_ge(s["owners"], 1)
            act.wait_ge(s["o_pe"], NC)
            slots(act, step)

        @block.gpsimd
        def _(pool):
            k = s["pool2"]
            done_so_far = [0]

            def done(ins):
                ins.then_inc(k, 1)
                done_so_far[0] += 1
                pool.wait_ge(k, done_so_far[0])

            def power(o, a, which):
                done(nc.gpsimd.tensor_tensor(o, a, half[:, which, :], ALU.pow))

            def plus(o, a, v):
                done(nc.gpsimd.tensor_scalar(o, a, v, 0.0, ALU.add, ALU.add))

            def times(o, a, b):
                done(nc.gpsimd.tensor_tensor(o, a, b, ALU.mult))

            for i, v in enumerate((-0.5, 0.5, -1.0)):
                done(nc.gpsimd.memset(half[:, i, :], v))
            done(nc.gpsimd.memset(ones[:, :], 1.0))
            nc.gpsimd.memset(eb[:, :, :], 0.0).then_inc(s["zero"], 1)
            var = mv[:, :, 1]
            rstd, t, a, c, ir, _ = [q[:, :] for q in sc]
            pool.wait_ge(s["moments"], 1)
            plus(ve[:, :], var, EPS)
            nc.gpsimd.tensor_tensor(rstd, ve[:, :], half[:, 0, :], ALU.pow).then_inc(s["small"], 1)
            pool.wait_ge(s["moments"], 2)
            plus(ve[:, :], var, EPS)
            power(rstd, ve[:, :], 0)
            power(t, var, 1)
            times(t, t, rstd)
            plus(t, t, 1e-8)
            power(t, t, 2)
            times(t, t, rstd)
            plus(a, rstd, 1.0)
            times(c, rstd, mv[:, :, 0])
            nc.gpsimd.tensor_scalar(c, c, -1.0, 1.0, ALU.mult, ALU.mult).then_inc(s["small"], 1)
            pool.wait_ge(s["at_in"], 16 * 8)
            for ch in range(NC):
                pool.wait_ge(s["ahead"], ch + 1)
                nc.gpsimd.tensor_tensor(xc[:, ch], xc[:, ch], ob[:, :].unsqueeze(1).broadcast_to([P, CT, E]), ALU.add).then_inc(s["ob_done"], 1)
            pool.wait_ge(s["moments"], 3)
            plus(ve[:, :], var, EPS)
            power(rstd, ve[:, :], 0)
            times(ve[:, :], rstd, rstd)
            times(ve[:, :], ve[:, :], var)
            plus(ve[:, :], ve[:, :], EPS)
            power(t, ve[:, :], 0)
            times(t, t, rstd)
            nc.gpsimd.tensor_tensor(ir, ve[:, :], half[:, 1, :], ALU.pow).then_inc(s["small"], 1)

            pool.wait_ge(s["filled"], 16 * SLOTS)
            pool.wait_ge(s["dest_done"], 1)
            for i in range(NT):
                nc.gpsimd.indirect_dma_start(order, bass.IndirectOffsetOnAxis(dest_i[:, i:i + 1], 0), pay[:, i, :], None,
                                             bounds_check=SLOTS * P - 1, oob_is_err=False).then_inc(s["sent"], 16)

            def step(n, b):
                if isinstance(n, int) and not 0 < n <= SLOTS:
                    return
                pool.wait_ge(s["y_dve"], n)
                if not isinstance(n, int):
                    pool.sem_inc(s["held3"], 1)
                nc.gpsimd.indirect_dma_start(out_rows, bass.IndirectOffsetOnAxis(tok[1 - b], 0), res[1 - b], None,
                                             bounds_check=S - 1, oob_is_err=False).then_inc(s[f"out{1 - b}"], 16)

            slots(pool, step)
            for b in range(2):
                pool.wait_ge(s[f"out{b}"], 16 * (SLOTS // 2))

        @block.vector
        def _(dve):
            V = nc.vector

            def stats(c, of=lambda i: x[:, i, :]):
                dve.drain()
                for t in range(CT):
                    V.bn_stats(stat[:, t, :], of(CT * c + t))
                dve.drain()
                for t in range(CT):
                    ins = V.bn_aggr(mv[:, CT * c + t, :], stat[:, t, :])
                return ins

            def norm(n, c, scale):
                if n > 1:
                    dve.wait_ge(s["turned"], n - 1)
                for t in range(CT):
                    i = CT * c + t
                    ins = V.tensor_scalar(rows[:, n % 2, t, :], x[:, i, :], mv[:, i, 0:1], scale[:, i:i + 1],
                                          ALU.subtract, ALU.mult)
                ins.then_inc(s["rows_done"], 1)

            def choose(i):
                dve.wait_ge(s["logits"], NC * (i + 1))
                if i:
                    V.tensor_tensor(lg[:, :, :], bank[2][:, 0:NT * NX].rearrange("p (t x) -> p t x", x=NX),
                                    sc[4][:, :].unsqueeze(2).broadcast_to([P, NT, NX]), ALU.mult)
                    dve.drain()
                    V.tensor_tensor(lg[:, :, :], lg[:, :, :], rb[:, i, :].unsqueeze(1).broadcast_to([P, NT, NX]), ALU.add)
                else:
                    V.tensor_tensor(lg[:, :, :], bank[2][:, 0:NT * NX].rearrange("p (t x) -> p t x", x=NX),
                                    rb[:, i, :].unsqueeze(1).broadcast_to([P, NT, NX]), ALU.add)
                dve.drain()
                V.tensor_reduce(mx[:, :], lg[:, :, :], AX_X, ALU.max)
                dve.drain()
                V.tensor_tensor(lg[:, :, :], lg[:, :, :], mx[:, :].unsqueeze(2).broadcast_to([P, NT, NX]), ALU.subtract).then_inc(s["expd"], 1)
                dve.drain()
                V.tensor_scalar(pick[:, :, :], lg[:, :, :], 0.0, None, ALU.is_ge)
                dve.drain()
                V.tensor_tensor(pick[:, :, :], pick[:, :, :], prio[:, :].unsqueeze(1).broadcast_to([P, NT, NX]), ALU.mult)
                dve.drain()
                V.tensor_reduce(mx[:, :], pick[:, :, :], AX_X, ALU.max)
                dve.drain()
                V.tensor_tensor(pick[:, :, :], pick[:, :, :], mx[:, :].unsqueeze(2).broadcast_to([P, NT, NX]), ALU.is_equal)
                dve.wait_ge(s["expd"], 2 * i + 2)
                V.tensor_reduce(gate[:, :], ex[:, :, :], AX_X, ALU.add)
                dve.drain()
                V.reciprocal(gate[:, :], gate[:, :])
                dve.drain()
                V.tensor_tensor(mg[:, :, :], pick[:, :, :], gate[:, :].unsqueeze(2).broadcast_to([P, NT, NX]), ALU.mult).then_inc(s["picked"], 1)

            def add(c, b0, wait=None):
                for b in range(2):
                    part = xc[:, c, 2 * b:2 * b + 2, :].rearrange("p t e -> p (t e)")
                    ins = V.tensor_tensor(part, part, bank[b0 + b][:, :], ALU.add)
                return ins

            for c in range(NC):
                dve.wait_ge(*((s["x0_rest"], 16 * (NC - 1)) if c else (s["x0_in"], 16)))
                V.tensor_tensor(xc[:, c], xc[:, c], x0[:, c], ALU.add).then_inc(s["added"], 1)
                ins = stats(c)
            ins.then_inc(s["moments"], 1)
            dve.wait_ge(s["small"], 1)
            for c in range(NC):
                norm(c, c, sc[0])
            dve.wait_ge(s["rw_in"], 80)
            choose(0)
            for c in range(NC):
                dve.wait_ge(s["bias_pe"], c + 1)
                add(c, 4).then_inc(s["bias_dve"], 1)
            for i in range(NT):
                dve.wait_ge(s["ex_pe"], i + 1)
                for e in range(NX):
                    dve.drain()
                    ins = V.scalar_tensor_tensor(out=x[:, i, :], in0=bank[4 * (i % 2) + e // 2][:, (e % 2) * E:(e % 2 + 1) * E],
                                                 scalar=mg[:, i, e:e + 1], in1=x[:, i, :], op0=ALU.mult, op1=ALU.add)
                ins.then_inc(s["ex_dve"], 1)
                if i % CT == CT - 1:
                    ins = stats(i // CT)
            ins.then_inc(s["moments"], 1)
            dve.wait_ge(s["small"], 2)
            dve.wait_ge(s["at_in"], 16 * 8)
            for c in range(NC):
                norm(NC + c, c, sc[1])
                for t in range(CT):
                    i = CT * c + t
                    ins = V.tensor_scalar(x[:, i, :], x[:, i, :], sc[2][:, i:i + 1], sc[3][:, i:i + 1], ALU.mult, ALU.add)
                ins.then_inc(s["ahead"], 1)
                def gated(c):
                    dve.wait_ge(s["u_act"], 8 * (c + 1))
                    for m in range(MC):
                        ins = V.scalar_tensor_tensor(out=su[:, m, :], in0=sv[:, m, :], scalar=tz[:, m:m + 1], in1=su[:, m, :],
                                                     op0=ALU.mult, op1=ALU.mult)
                    ins.then_inc(s["prod"], 1)
                def result(c):
                    dve.wait_ge(s["ob_done"], c + 1)
                    dve.wait_ge(s["o_pe"], c + 1)
                    for b in range(2):
                        a = CT * c + 2 * b
                        ins = V.tensor_tensor(pay[:, a:a + 2, E:2 * E], x[:, a:a + 2, :],
                                              bank[6 + b][:, :].rearrange("p (t e) -> p t e", t=2), ALU.add)
                    ins.then_inc(s["o_dve"], 1)
                    return stats(c, lambda i: pay[:, i, E:2 * E])
                if c:
                    gated(c - 1)
                if c > 1:
                    result(c - 2)
            gated(NC - 1)
            result(NC - 2)
            result(NC - 1).then_inc(s["moments"], 1)
            dve.wait_ge(s["small"], 3)
            for i in range(NT):
                ins = V.tensor_scalar(pay[:, i, 0:E], pay[:, i, E:2 * E], mv[:, i, 0:1], sc[1][:, i:i + 1],
                                      ALU.subtract, ALU.mult)
                if i % CT == CT - 1:
                    ins.then_inc(s["rows_done"], 1)
            choose(1)
            dve.wait_ge(s["const_in"], 48)
            V.tensor_copy(pay[:, :, 2 * E:2 * E + 1], gate[:, :].unsqueeze(2))
            V.tensor_copy(pay[:, :, 2 * E + 1:2 * E + 2], token[:, :].unsqueeze(2))
            V.memset(pay[:, :, 2 * E + 2:PAY], 0.0)
            dve.wait_ge(s["ranks_pe"], 1)
            per_tile = bank[5][:, 0:NT * NX].rearrange("p (t x) -> p t x", x=NX)
            V.memset(lg[:, 0:1, :], 0.0)
            V.tensor_copy(lg[:, 1:NT, :], per_tile[:, 0:NT - 1, :])
            dve.drain()
            a, b = lg, ex
            for sh in (1, 2, 4, 8, 16):
                V.tensor_copy(b[:, 0:sh, :], a[:, 0:sh, :])
                V.tensor_tensor(b[:, sh:NT, :], a[:, sh:NT, :], a[:, 0:NT - sh, :], ALU.add)
                dve.drain()
                a, b = b, a
            V.tensor_tensor(count[:, :], a[:, NT - 1, :], per_tile[:, NT - 1, :], ALU.add)
            V.tensor_tensor(b[:, :, :], a[:, :, :], bank[4][:, 0:NT * NX].rearrange("p (t x) -> p t x", x=NX), ALU.add)
            dve.drain()
            V.tensor_scalar(tiles[:, :], count[:, :], 1.0 / P, 0.5 - 1.0 / (2 * P), ALU.mult, ALU.add)
            dve.drain()
            V.tensor_scalar(tiles[:, :], tiles[:, :], ROUND, ROUND, ALU.add, ALU.subtract)
            dve.drain()
            u, v = tiles, ends[0]
            for sh in (1, 2, 4):
                V.tensor_copy(v[:, 0:sh], u[:, 0:sh])
                V.tensor_tensor(v[:, sh:NX], u[:, sh:NX], u[:, 0:NX - sh], ALU.add)
                dve.drain()
                u, v = v, (ends[1] if v is ends[0] else ends[0])
            end = u
            V.tensor_tensor(v[:, :], end[:, :], tiles[:, :], ALU.subtract)
            V.tensor_tensor(ge[:, :, :], slot_no[:, :].unsqueeze(2).broadcast_to([P, SLOTS, NX]),
                            end[:, :].unsqueeze(1).broadcast_to([P, SLOTS, NX]), ALU.is_ge)
            dve.drain()
            V.tensor_scalar(v[:, :], v[:, :], float(P), 0.0, ALU.mult, ALU.add)
            V.tensor_reduce(owner[:, :], ge[:, :, :], AX_X, ALU.add)
            dve.drain()
            V.tensor_scalar(owner[:, :], owner[:, :], float(NX - 1), None, ALU.min)
            V.tensor_tensor(b[:, :, :], b[:, :, :], v[:, :].unsqueeze(1).broadcast_to([P, NT, NX]), ALU.add)
            dve.drain()
            V.tensor_copy(owner_i[:, :], owner[0:1, :]).then_inc(s["owners"], 1)
            V.tensor_tensor(b[:, :, :], b[:, :, :], pick[:, :, :], ALU.mult)
            dve.drain()
            V.tensor_reduce(dest[:, :], b[:, :, :], AX_X, ALU.add)
            dve.drain()
            V.tensor_copy(dest_i[:, :], dest[:, :]).then_inc(s["dest_done"], 1)

            def step(n, b):
                if not isinstance(n, int) or 0 <= n < SLOTS:
                    after(dve, s["hr_pe"], n + 1)
                    after(dve, s["ht_pe"], n)
                    for q in range(2):
                        ins = V.tensor_copy(h_rows[:, 512 * q:512 * q + 512], bank[1 + q][:, :])
                    ins.then_inc(s["hr_dve"], 1)
                if isinstance(n, int) and not 0 < n <= SLOTS:
                    return
                e = dve.value_load(owner_i[0:1, bass.ds(n - 1, 1)], min_val=0, max_val=NX - 1)
                b = 1 - b
                after(dve, s["y_pe"], n)
                V.tensor_tensor(y_b, bank[5][:, 0:E], b2[:, bass.ds(e, 1), :].rearrange("p x e -> p (x e)"), ALU.add)
                after(dve, s[f"r_in{b}"], 16 * ((n + 1) // 2))
                after(dve, s[f"out{b}"], 16 * ((n - 1) // 2))
                V.tensor_copy(tok[b], in_r[b][:, E + 1:E + 2])
                dve.drain()
                V.scalar_tensor_tensor(out=res[b], in0=y_b, scalar=in_r[b][:, E:E + 1], in1=in_r[b][:, 0:E],
                                       op0=ALU.mult, op1=ALU.add).then_inc(s["y_dve"], 1)

            dve.wait_ge(s["b2_in"], 16)
            slots(dve, step)


def program(nc, d, out):
    with ExitStack() as ctx:
        x = ctx.enter_context(nc.sbuf_tensor("x", [P, NT, E], F32))
        ident = ctx.enter_context(nc.sbuf_tensor("ident", [P, P], F32))
        bank = [ctx.enter_context(nc.psum_tensor(f"bank{i}", [P, 512], F32)) for i in range(8)]
        attention(nc, d, x, ident, bank)
        tail(nc, d, out, x, ident, bank)


_INS = ["L0_attn_x", "L0_attn_ln1_w", "L0_attn_ln1_b", "L0_attn_attn_w", "L0_attn_attn_b", "L0_attn_aproj_w",
        "L0_attn_aproj_b", "L0_attn_ln2_w", "L0_attn_ln2_b", "L0_attn_fc_w", "L0_attn_fc_b", "L0_attn_mproj_w",
        "L0_attn_mproj_b", "L0_ffn_router_w", "L0_ffn_router_b", "L0_ffn_expert_w", "L0_ffn_expert_b",
        "L1_attn_u_w", "L1_attn_u_b", "L1_attn_v_w", "L1_attn_v_b", "L1_attn_o_w", "L1_attn_o_b",
        "L1_attn_t_zero", "L1_ffn_Wr", "L1_ffn_br", "L1_ffn_ln_g", "L1_ffn_ln_b", "L1_ffn_W1", "L1_ffn_b1",
        "L1_ffn_W2", "L1_ffn_b2"]
_TURNED = ["L1_attn_u_w", "L1_attn_v_w", "L1_attn_o_w"]
_SHAPE = (1, S, E)


def kernel(**inputs):
    import numpy as _np
    import concourse.bacc as _bacc
    from concourse.bass_utils import run_bass_kernel_spmd as _run

    nc = _bacc.Bacc("TRN2", target_bir_lowering=False, num_devices=1)
    arrays, aps = {}, {}
    for name in _INS:
        a = _np.asarray(inputs[name])
        arrays[name] = _np.ascontiguousarray(a.T if name in _TURNED else a)
    arrays.update(shape_constants())
    for name, a in arrays.items():
        aps[name] = nc.dram_tensor(name, a.shape, mybir.dt.from_np(a.dtype), kind="ExternalInput").ap()
    out = nc.dram_tensor("out", _SHAPE, F32, kind="ExternalOutput").ap()
    program(nc, aps, out)
    r = _run(nc, [arrays], core_ids=[0])
    return r.results[0]["out"]
```

```python
from contextlib import ExitStack

import concourse.bass as bass
from concourse import mybir

F32 = mybir.dt.float32
F32R = mybir.dt.float32r
ALU = mybir.AluOpType
ACT = mybir.ActivationFunctionType
AX_X = mybir.AxisListType.X

P = 128
S = 4096
E = 256
EH = E // P
L = 4
H = 16
HD = E // H
QW = 3 * HD
CT = 4
CW = CT * P
NC = S // CW
NT = S // P
NG = L * NC
F = 4 * E
FC = F // P
NX = 8
D1 = 512
MC = D1 // P
XW = 2 * EH * F
PAY = 2 * E + 4
SLOTS = NT + NX
I32 = mybir.dt.int32
HW1 = H + 1
W2 = 3 * E // 2
EPS = 1e-5
TURN = 0.15915494309189535
ROUND = 12582912.0
TWO_PI = 6.2831845


def shape_constants():
    import numpy as np

    h = np.arange(H)
    base = np.zeros((H, H))
    for k in range(H // 2 + 1):
        g = np.sqrt(1 / H) if k in (0, H // 2) else np.sqrt(2 / H)
        base[:, k] = g * np.cos(2 * np.pi * h * k / H)
        if 0 < k < H // 2:
            base[:, H // 2 + k] = g * np.sin(2 * np.pi * h * k / H)
    one = np.float32
    k = np.fft.fftfreq(H).astype(one)[[*range(H // 2 + 1), *range(1, H // 2)]]
    ks = np.fft.fftfreq(S).astype(one)[:, None, None]
    km = np.sqrt(ks ** 2 + k[None, :, None] ** 2 + k[None, None, :] ** 2 + one(1e-10))
    filt = np.cos(np.arctan(np.log(km + one(1e-10)).astype(np.float64))).reshape(S, E)
    lam = np.arange(S, dtype=one) / one(S)
    t = np.arange(S, dtype=one) * one(0.1)
    phase = t - one(2) * lam + one(0.5) * lam ** 2
    mod = 1 + 0.1 * (np.sin((t + lam).astype(np.float64)) * np.cos(phase.astype(np.float64)))
    scale = (filt * mod[:, None]).reshape(NC, P, CT, EH, P).transpose(4, 3, 0, 2, 1)
    return {
        "c_heads": np.kron(base, base).astype(one),
        "c_filter": np.ascontiguousarray(scale.reshape(P, EH, S)).astype(one),
        "c_low": np.triu(np.ones((P, P)), 1).astype(one),
        "c_slot": np.arange(SLOTS).astype(one),
        "c_token": np.arange(S).reshape(NC, P, CT).transpose(1, 0, 2).reshape(P, NT).astype(one),
        "c_fill": np.tile(np.array([0] * (2 * E + 1) + [S] + [0] * (PAY - 2 * E - 2)), (P, 1)).astype(one),
        "c_prio": np.arange(NX, 0, -1).astype(one),
        "c_ident": np.eye(P, dtype=one),
    }


def attention(nc, d, x, ident, bank, order, filled):
    with ExitStack() as ctx:
        def sb(name, *shape):
            return ctx.enter_context(nc.sbuf_tensor(name, [P, *shape], F32))

        def shared(name, *shape):
            with nc.sbuf_tensor(name, [P, *shape], F32) as t:
                return t

        def sbr(name, *shape):
            return ctx.enter_context(nc.sbuf_tensor(name, [P, *shape], F32R))

        filt = sb("filt", 2, EH, CW)
        heads = sb("heads", EH, E)
        at_w = sb("at_w", EH, 3 * E)
        back_w = sb("back_w", L, EH, E)
        fc_whole = shared("fc_whole", EH, F)
        fc_lo = sbr("fc_lo", EH, F)
        fc_w = (sbr("fc_hi", EH, F), fc_lo)
        mp_w = sb("mp_w", FC, E)
        at_b_whole = shared("at_b_whole", 3 * E)
        at_b = sbr("at_b", 3 * E)
        both = sbr("both", P)
        ap_b = sb("ap_b", E)
        mp_b = sb("mp_b", E)
        fc_b = sb("fc_b", FC)
        ln1 = sb("ln1", 2, EH)
        ln2 = sb("ln2", 2, EH)
        xn = sb("xn", CT, E)
        xt1 = sb("xt1", EH, CW)
        xt2_whole = shared("xt2_whole", EH, CW)
        xt2_lo = sbr("xt2_lo", EH, CW)
        xt2 = (sbr("xt2_hi", EH, CW), xt2_lo)
        qkv = sb("qkv", 2 * CT, HW1, QW)
        dif = sb("dif", 2, 2, H, QW)
        cosv = sb("cosv", 2, 2, H, QW)
        whole = sb("whole", 2, 2, H, QW)
        third = sb("third", 2, 2, H, HD)
        term = sb("term", 2, H, HD)
        ham = sb("ham", CT, E)
        hb = [sb(f"hb{i}", 2, HW1 if i == 0 else H, HD) for i in range(6)]
        ham_t = sb("ham_t", EH, CW)
        coef = ham_t
        hid = sb("hid", FC, CW)
        stat = sb("stat", CT, 6)
        mv1 = sb("mv1", CT, 2)
        mv2 = sb("mv2", CT, 2)
        rs1 = sb("rs1", CT)
        rs2 = sb("rs2", CT)
        ve = sb("ve", CT)
        half = sb("half", CT)
        quarter = sb("quarter", 1)
        up_to_whole = sb("up_to_whole", 1)
        down_again = sb("down_again", 1)

        names = """x_in0 x_rest ident_in heads_in ap_in filt_in0 filt_in1
            at_w_in fc_w_hi fc_w_lo at_b_split lo2 cleared ln1_in at_s_in fc_w_in mp_w_in mp_s_in
            before_in back_pe back_act t1_pe t1_act qkv_pe qkv_act pool_step prep cosd
            ham_step ham_done third_step third_done turn_step whole_done tp_pe tp_act r_pe filt_dve g_pe res1 var1 rs1_pool ln1_done var2 rs2_pool
            ln2_done t2_pe t2_act fc_pe gelu mm_pe res2 pb_done mb_done eps held_pool held_sp zeroed""".split()
        s = {n: ctx.enter_context(nc.semaphore(n)) for n in names}

        rows = "b (c p t) e -> p (b c) t e"
        x_in = d["L0_attn_x"].rearrange(rows, p=P, t=CT)
        xc = x[:, :, :].rearrange("p (c t) e -> p c t e", t=CT)

        def hold(eng, what, value):
            if isinstance(value, int) and value <= 0:
                return
            eng.wait_ge(what, value)
            if not isinstance(value, int):
                eng.sem_inc(s["held_pool" if eng.engine == mybir.EngineType.Pool else "held_sp"], 1)

        def quaternions(b, parity):
            a = CT * parity + 2 * b
            ext = lambda j: qkv[:, a:a + 2, :, HD * j:HD * j + HD]
            return [[ext(j)[:, :, 1:HW1, :], dif[:, b, :, :, HD * j:HD * j + HD], ext(j)[:, :, 0:H, :],
                     cosv[:, b, :, :, HD * j:HD * j + HD]] for j in range(3)]

        def after(eng, what, value):
            if not isinstance(value, int) or value > 0:
                eng.wait_ge(what, value)

        def steps(eng, step):
            for n in range(-1, NC):
                step(n, n % NC)
            with eng.Fori(1, L - 1) as l:
                for k in range(NC):
                    step(NC * l + k, k)
            for n in range(NG - NC, NG + 4):
                step(n, n % NC)

        def begins(g):
            return not isinstance(g, int) or g < NG

        def on(g):
            return not isinstance(g, int) or 0 <= g < NG

        block = ctx.enter_context(nc.Block())

        @block.sync
        def _(sp):
            def by_channel(to, name, l, done):
                sp.dma_start(to, d[name][l].rearrange("(k p) -> p k", p=P),
                             allow_slow_non_contiguous=True).then_inc(s[done], 16)

            def matrix(to, name, l, done):
                sp.dma_start(to, d[name][l].rearrange("(k p) n -> p k n", p=P)).then_inc(s[done], 16)

            def load_attention(l):
                hold(sp, s["t1_act"], NC * l)
                by_channel(ln1[:, 0, :], "L0_attn_ln1_w", l, "ln1_in")
                by_channel(ln1[:, 1, :], "L0_attn_ln1_b", l, "ln1_in")
                hold(sp, s["qkv_pe"], 8 * NC * l)
                matrix(at_w[:, :, :], "L0_attn_attn_w", l, "at_w_in")
                for p in (0, 32):
                    sp.dma_start(at_b_whole[p:p + 1, :], d["L0_attn_attn_b"][l].partition_broadcast(1)).then_inc(s["at_w_in"], 16)

            def load_projection_bias(l):
                hold(sp, s["pb_done"], NC * l)
                sp.dma_start(ap_b[:, :], d["L0_attn_aproj_b"][l].partition_broadcast(P)).then_inc(s["at_s_in"], 16)

            def load_mlp(l):
                matrix(fc_whole[:, :, :], "L0_attn_fc_w", l, "fc_w_in")
                by_channel(fc_b[:, :], "L0_attn_fc_b", l, "fc_w_in")
                by_channel(ln2[:, 0, :], "L0_attn_ln2_w", l, "fc_w_in")
                by_channel(ln2[:, 1, :], "L0_attn_ln2_b", l, "fc_w_in")
                hold(sp, s["mm_pe"], 2 * NC * l)
                hold(sp, s["mb_done"], NC * l)
                matrix(mp_w[:, :, :], "L0_attn_mproj_w", l, "mp_w_in")
                sp.dma_start(mp_b[:, :], d["L0_attn_mproj_b"][l].partition_broadcast(P)).then_inc(s["mp_s_in"], 16)

            def load_before(g, parity, start):
                hold(sp, s["qkv_act"], 8 * g + 8)
                hold(sp, s["ham_done"], 2 * g - 1)
                last = qkv[:, CT * parity + CT - 1, 1:HW1, :]
                sp.dma_start(dif[1:P, 0, 0, :, :], last[0:P - 1]).then_inc(s["before_in"], 16)
                first = qkv[0:1, 0, 1:HW1, :] if start else qkv[P - 1:P, CT * (1 - parity) + CT - 1, 1:HW1, :]
                sp.dma_start(dif[0:1, 0, 0, :, :], first).then_inc(s["before_in"], 16)

            def load_filter(g, c, parity):
                hold(sp, s["filt_dve"], g - 1)
                sp.dma_start(filt[:, parity, :, :], d["c_filter"][:, :, bass.ds(CW * c, CW)]).then_inc(s[f"filt_in{parity}"], 16)

            def for_chunk(l, c, parity, start=False):
                load_before(NC * l + c, parity, start)
                load_filter(NC * l + c, c, parity)

            def layer(l, last):
                for c in range(NC):
                    if c == 3 and not (isinstance(l, int) and l == 0):
                        hold(sp, s["fc_pe"], FC * NC * l)
                        hold(sp, s["gelu"], FC * NC * l)
                        load_mlp(l)
                    if c == NC - 1 and not last:
                        load_attention(l + 1)
                    for_chunk(l, c, c % 2, c == 0)

            sp.dma_start(xc[:, 0], x_in[:, 0]).then_inc(s["x_in0"], 16)
            sp.dma_start(ident[:, :], d["c_ident"]).then_inc(s["ident_in"], 16)
            sp.wait_ge(s["cleared"], 1)
            load_attention(0)
            load_projection_bias(0)
            for c in range(1, NC):
                sp.dma_start(xc[:, c], x_in[:, c]).then_inc(s["x_rest"], 16)
            sp.dma_start(heads[:, :, :], d["c_heads"].rearrange("(k p) n -> p k n", p=P)).then_inc(s["heads_in"], 16)
            for l in range(L):
                sp.dma_start(hid[:, 2 * l:2 * l + 2, 0:E],
                             d["L0_attn_aproj_w"][l].rearrange("(k p) n -> p k n", p=P)).then_inc(s["ap_in"], 16)
            load_mlp(0)
            for i in range(SLOTS):
                sp.dma_start(order[P * i:P * i + P, :], d["c_fill"]).then_inc(filled, 16)
            layer(0, False)
            with sp.Fori(1, L - 1) as l:
                load_projection_bias(l)
                layer(l, False)
            load_projection_bias(L - 1)
            layer(L - 1, True)

        @block.tensor
        def _(pe):
            def turn(rows_of, done):
                for e in range(EH):
                    for t in range(CT):
                        mm = pe.transpose(bank[e][:, t * P:(t + 1) * P], rows_of[:, t, e * P:(e + 1) * P], ident[:, :])
                mm.then_inc(s[done], 1)

            def compose_back():
                pe.wait_ge(s["heads_in"], 16)
                pe.wait_ge(s["ap_in"], 16 * L)
                for l in range(L):
                    for e in range(EH):
                        for k in range(EH):
                            mm = pe.matmul(bank[2 + l][:, e * E:(e + 1) * E], heads[:, k, e * P:(e + 1) * P],
                                           hid[:, 2 * l + k, 0:E], start=(k == 0), stop=(k == EH - 1))
                mm.then_inc(s["back_pe"], 1)

            def step(n, k_of):
                parity = k_of % 2
                if on(n - 2):
                    after(pe, s["ham_done"], 2 * (n - 1))
                    after(pe, s["t1_act"], n + 1 if not isinstance(n, int) else min(n + 1, NG))
                    turn(ham, "tp_pe")
                if on(n):
                    after(pe, s["t1_act"], n + 1)
                    after(pe, s["at_w_in"], 48 * (n // NC + 1))
                    after(pe, s["at_b_split"], n // NC + 1)
                    after(pe, s["filt_dve"], n - 2)
                for t in range(CT):
                    if on(n):
                        for j in range(2):
                            if t:
                                after(pe, s["qkv_act"], 8 * n + (2 * t + j - 1))
                            to, cols = bank[6 + j][:, 0:W2], slice(W2 * j, W2 * j + W2)
                            pe.matmul(to, both[0:33, :], at_b[0:33, cols], start=True, stop=False)
                            for k in range(EH):
                                mm = pe.matmul(to, xt1[:, k, t * P:(t + 1) * P], at_w[:, k, cols],
                                               start=False, stop=(k == EH - 1))
                            mm.then_inc(s["qkv_pe"], 1)
                    if t == 1 and on(n - 3):
                        after(pe, s["ln2_done"], n - 2)
                        after(pe, s["tp_act"], n - 1 if not isinstance(n, int) else min(n - 1, NG))
                        turn(xn, "t2_pe")
                if on(n - 2):
                    after(pe, s["tp_act"], n - 1)
                    if on(n):
                        after(pe, s["qkv_act"], 8 * n + 8)
                    else:
                        after(pe, s["filt_dve"], n - 2)
                    for e in range(EH):
                        for k in range(EH):
                            mm = pe.matmul(bank[6 + e][:, :], heads[:, k, e * P:(e + 1) * P], ham_t[:, k, :],
                                           start=(k == 0), stop=(k == EH - 1))
                    mm.then_inc(s["r_pe"], 1)
                if on(n - 3):
                    after(pe, s["t2_act"], n - 2)
                    after(pe, s["lo2"], n - 2)
                    after(pe, s["fc_w_lo"], (n - 3) // NC + 1)
                    after(pe, s["res1"], n - 2)
                    for f in range(FC):
                        if f > 1:
                            after(pe, s["gelu"], FC * (n - 3) + (f - 1))
                        to = bank[2 + f % 2][:, :]
                        for k in range(EH):
                            w = [part[:, k, f * P:(f + 1) * P] for part in fc_w]
                            pe.matmul(to, w[0], xt2[0][:, k, :], start=(k == 0), stop=False)
                            pe.matmul(to, w[0], xt2[1][:, k, :], start=False, stop=False)
                            mm = pe.matmul(to, w[1], xt2[0][:, k, :], start=False, stop=(k == EH - 1))
                        mm.then_inc(s["fc_pe"], 1)
                if on(n + 1):
                    after(pe, s["ln1_done"], n + 2)
                    after(pe, s["t2_act"], n - 2)
                    after(pe, s["tp_act"], n - 1)
                    turn(xn, "t1_pe")
                if isinstance(n, int) and n == 1:
                    compose_back()
                if isinstance(n, int) and n == 2:
                    pe.wait_ge(s["back_act"], 1)
                if on(n - 3):
                    after(pe, s["gelu"], FC * (n - 2))
                if on(n - 2):
                    after(pe, s["filt_dve"], n - 1)
                    for b in range(2):
                        for t in range(2):
                            at = (2 * b + t) * P
                            for k in range(EH):
                                mm = pe.matmul(bank[2 + b][:, t * E:(t + 1) * E], coef[:, k, at:at + P],
                                               back_w[:, bass.ds((n - 2) // NC, 1), k, :].rearrange("p l e -> p (l e)"),
                                               start=(k == 0), stop=(k == EH - 1))
                    mm.then_inc(s["g_pe"], 1)
                if on(n - 3):
                    after(pe, s["mp_w_in"], 16 * ((n - 3) // NC + 1))
                    after(pe, s["res2"], n - 3)
                    for b in range(2):
                        for t in range(2):
                            at = (2 * b + t) * P
                            for f in range(FC):
                                mm = pe.matmul(bank[4 + b][:, t * E:(t + 1) * E], hid[:, f, at:at + P],
                                               mp_w[:, f, :], start=(f == 0), stop=(f == FC - 1))
                        mm.then_inc(s["mm_pe"], 1)

            pe.wait_ge(s["ident_in"], 16)
            steps(pe, step)

        @block.scalar
        def _(act):
            def turned(ln, to, done):
                for e in range(EH):
                    for place in to:
                        ins = nc.scalar.activation(place[:, e, :], bank[e][:, :], ACT.Identity,
                                                   bias=ln[:, 1, e:e + 1], scale=ln[:, 0, e:e + 1])
                ins.then_inc(s[done], 1)

            def whole_turns(g, b, parity):
                i = 2 * g + b
                a = CT * parity + 2 * b
                to = cosv[:, b, :, :, :]
                k = s["turn_step"]
                after(act, s["qkv_act"], 8 * g + 4 * b + 4)
                after(act, s["prep"], i - 1)
                after(act, s["ham_done"], i - 1)
                after(act, s["third_done"], i - 1)
                nc.scalar.activation(to, qkv[:, a:a + 2, 1:HW1, :], ACT.Identity, scale=TURN,
                                     bias=quarter[:, 0:1]).then_inc(k, 1)
                act.wait_ge(k, 2 * i + 1)
                nc.scalar.activation(whole[:, b, :, :, :], to, ACT.Identity,
                                     bias=up_to_whole[:, 0:1]).then_inc(k, 1)
                act.wait_ge(k, 2 * i + 2)
                nc.scalar.activation(whole[:, b, :, :, :], whole[:, b, :, :, :], ACT.Identity,
                                     bias=down_again[:, 0:1]).then_inc(s["whole_done"], 1)

            def sine(half_index, b):
                after(act, s["prep"], half_index + 1)
                nc.scalar.activation(cosv[:, b, :, :, :], cosv[:, b, :, :, :], ACT.Sin,
                                     scale=TWO_PI).then_inc(s["cosd"], 1)

            def step(n, k_of):
                parity = k_of % 2
                for t in range(CT):
                    if t == 0 and on(n - 2):
                        after(act, s["tp_pe"], n - 1)
                        after(act, s["g_pe"], n - 2)
                        for e in range(EH):
                            ins = nc.scalar.activation(ham_t[:, e, :], bank[e][:, :], ACT.Copy)
                        ins.then_inc(s["tp_act"], 1)
                    if on(n):
                        if t == 0:
                            after(act, s["ham_done"], 2 * (n - 1))
                        for j in range(2):
                            after(act, s["qkv_pe"], 8 * n + (2 * t + j + 1))
                            to = qkv[:, CT * parity + t, 1 + 8 * j:9 + 8 * j, :]
                            ins = nc.scalar.activation(to.rearrange("p h w -> p (h w)"), bank[6 + j][:, 0:W2], ACT.Copy)
                            if j:
                                ins = nc.scalar.activation(qkv[:, CT * parity + t, 0, :], bank[7][:, W2 - QW:W2], ACT.Copy)
                            ins.then_inc(s["qkv_act"], 1)
                    if t == 1 and on(n - 3):
                        after(act, s["fc_w_in"], 64 * ((n - 3) // NC + 1))
                        after(act, s["t2_pe"], n - 2)
                        after(act, s["fc_pe"], FC * (n - 3))
                        turned(ln2, (xt2[0], xt2_whole), "t2_act")
                if on(n - 1):
                    sine(2 * (n - 1) + 1, 1)
                for f in range(FC):
                    if on(n - 3):
                        after(act, s["fc_pe"], FC * (n - 3) + (f + 1))
                        if f == 0:
                            after(act, s["mm_pe"], 2 * (n - 3))
                        nc.scalar.activation(hid[:, f, :], bank[2 + f % 2][:, :], ACT.Gelu,
                                             bias=fc_b[:, f:f + 1]).then_inc(s["gelu"], 1)
                if on(n + 1):
                    after(act, s["ln1_in"], 32 * ((n + 1) // NC + 1))
                    after(act, s["t1_pe"], n + 2)
                    after(act, s["qkv_pe"], 8 * n + 8)
                    turned(ln1, (xt1,), "t1_act")
                if on(n):
                    whole_turns(n, 0, parity)
                    whole_turns(n, 1, parity)
                    sine(2 * n, 0)
                if k_of == 2 and begins(n - 2):
                    act.wait_ge(s["fc_w_in"], 64 * ((n - 2) // NC + 1))
                    after(act, s["fc_pe"], FC * (n - 2))
                    nc.scalar.activation(fc_w[0][:, :, :], fc_whole[:, :, :], ACT.Copy).then_inc(s["fc_w_hi"], 1)
                if isinstance(n, int) and n == 1:
                    act.wait_ge(s["back_pe"], 1)
                    for l in range(L):
                        ins = nc.scalar.activation(back_w[:, l, :, :].rearrange("p k n -> p (k n)"),
                                                   bank[2 + l][:, :], ACT.Copy)
                    ins.then_inc(s["back_act"], 1)

            act.wait_ge(s["zeroed"], 4)
            steps(act, step)

        @block.gpsimd
        def _(pool):
            def minus(o, a, b):
                return nc.gpsimd.tensor_tensor(o, a, b, ALU.subtract)

            def plus(o, a, b):
                return nc.gpsimd.tensor_tensor(o, a, b, ALU.add)

            def copy(o, a):
                return nc.gpsimd.tensor_scalar(o, a, 1.0, 1.0, ALU.mult, ALU.mult)

            def prep(i, b, parity):
                a = CT * parity + 2 * b
                hold(pool, s["ham_done"], i - 1)
                hold(pool, s["qkv_act"], 4 * i + 4)
                if b:
                    minus(dif[:, b, :, :, :], qkv[:, a:a + 2, 1:HW1, :], qkv[:, a - 1:a + 1, 1:HW1, :])
                else:
                    minus(dif[:, b, 1, :, :], qkv[:, a + 1, 1:HW1, :], qkv[:, a, 1:HW1, :])
                    hold(pool, s["before_in"], 16 * i + 32)
                    minus(dif[:, b, 0, :, :], qkv[:, a, 1:HW1, :], dif[:, b, 0, :, :])
                hold(pool, s["whole_done"], i + 1)
                minus(cosv[:, b, :, :, :], cosv[:, b, :, :, :], whole[:, b, :, :, :]).then_inc(s["prep"], 1)

            def third_part(g, b, parity):
                i = 2 * g + b
                B, C = quaternions(b, parity)[1:]
                to, other = third[:, b, :, :, :], term[:, :, :, :]
                k = s["third_step"]
                hold(pool, s["cosd"], i + 1)
                hold(pool, s["ham_done"], i - 1)
                hold(pool, s["third_done"], i)
                nc.gpsimd.tensor_tensor(other, B[1], C[2], ALU.mult)
                nc.gpsimd.tensor_tensor(to, B[0], C[3], ALU.mult).then_inc(k, 1)
                for j, (p, q, f) in enumerate(((B[2], C[1], ALU.add), (B[3], C[0], ALU.subtract), (None, None, ALU.add))):
                    hold(pool, k, 5 * i + (2 * j + 1))
                    ins = nc.gpsimd.tensor_tensor(to, to, other, f)
                    ins.then_inc(s["third_done"] if p is None else k, 1)
                    if p is not None:
                        hold(pool, k, 5 * i + (2 * j + 2))
                        nc.gpsimd.tensor_tensor(other, p, q, ALU.mult).then_inc(k, 1)

            def rstd(n_eps, mv, rs, done):
                nc.gpsimd.tensor_scalar(ve[:, :], mv[:, :, 1], EPS, 0.0, ALU.add, ALU.add).then_inc(s["eps"], 1)
                hold(pool, s["eps"], n_eps)
                nc.gpsimd.tensor_tensor(rs[:, :], ve[:, :], half[:, :], ALU.pow).then_inc(s[done], 1)

            def add_row(g, b, done):
                now = xc[:, bass.ds(g % NC, 1), :, :].rearrange("p c t e -> p (c t) e")
                nc.gpsimd.tensor_tensor(now, now, b[:, :].unsqueeze(1).broadcast_to([P, CT, E]),
                                        ALU.add).then_inc(s[done], 1)

            def step(n, k_of):
                parity = k_of % 2
                ones = lambda g: g + 1 + (min(g + 1, NC) if isinstance(g, int) else NC)
                if on(n + 1):
                    g = n + 1
                    twos = max(0, min(n - 2, NG)) if isinstance(n, int) else n - 2
                    if isinstance(g, int) and g < NC:
                        hold(pool, s["var1"], ones(g) - 1)
                        rstd(ones(g) - 1 + twos, mv1, rs1, "rs1_pool")
                        hold(pool, s["rs1_pool"], ones(g) - 1)
                    hold(pool, s["var1"], ones(g))
                    rstd(ones(g) + twos, mv1, rs1, "rs1_pool")
                    hold(pool, s["rs1_pool"], ones(g))
                if on(n - 1):
                    third_part(n - 1, 0, 1 - parity)
                if on(n - 1):
                    prep(2 * (n - 1) + 1, 1, 1 - parity)
                if on(n - 3):
                    hold(pool, s["t2_act"], n - 2)
                    nc.gpsimd.tensor_tensor(xt2[1][:, :, :], xt2_whole[:, :, :], xt2[0][:, :, :].bitcast(F32),
                                            ALU.subtract).then_inc(s["lo2"], 1)
                if on(n - 3):
                    hold(pool, s["mp_s_in"], 16 * ((n - 3) // NC + 1))
                    hold(pool, s["ln2_done"], n - 2)
                    add_row(n - 3, mp_b, "mb_done")
                if on(n):
                    hold(pool, s["at_s_in"], 16 * (n // NC + 1))
                    hold(pool, s["ln1_done"], n + 1)
                    add_row(n, ap_b, "pb_done")
                if on(n - 1):
                    third_part(n - 1, 1, 1 - parity)
                if on(n):
                    prep(2 * n, 0, parity)
                if on(n - 2):
                    hold(pool, s["var2"], n - 1)
                    g1 = min(n + 2, NG) if isinstance(n, int) else n + 2
                    done1 = g1 + (min(g1, NC) if isinstance(n, int) else NC)
                    rstd(done1 + (n - 1), mv2, rs2, "rs2_pool")
                    hold(pool, s["rs2_pool"], n - 1)

            for to, v in ((half, -0.5), (quarter, 0.25), (up_to_whole, ROUND), (down_again, -ROUND)):
                nc.gpsimd.memset(to[:, :], v).then_inc(s["zeroed"], 1)
            pool.wait_ge(s["zeroed"], 4)
            steps(pool, step)

        @block.vector
        def _(dve):
            def tile(g, t):
                return xc[:, bass.ds(g % NC, 1), t, :].rearrange("p c e -> p (c e)")

            def stats(g, mv, done):
                dve.drain()
                for t in range(CT):
                    nc.vector.bn_stats(stat[:, t, :], tile(g, t))
                dve.drain()
                for t in range(CT):
                    ins = nc.vector.bn_aggr(mv[:, t, :], stat[:, t, :])
                ins.then_inc(s[done], 1)

            def norm(g, to, mv, rs, done=None):
                for t in range(CT):
                    ins = nc.vector.tensor_scalar(to(t), tile(g, t), mv[:, t, 0:1], rs[:, t:t + 1],
                                                  ALU.subtract, ALU.mult)
                if done is not None:
                    ins.then_inc(s[done], 1)

            def add_banks(g, b0, done, each):
                for b in range(2):
                    each(b)
                    now = xc[:, bass.ds(g % NC, 1), 2 * b:2 * b + 2, :].rearrange("p c t e -> p (c t e)")
                    ins = nc.vector.tensor_tensor(now, now, bank[b0 + b][:, :], ALU.add)
                ins.then_inc(s[done], 1)

            def hamilton(g, b, parity):
                i = 2 * g + b
                a = CT * parity + 2 * b
                ext = lambda j: qkv[:, a:a + 2, :, HD * j:HD * j + HD]
                A, B, C = quaternions(b, parity)
                to = ham[:, 2 * b:2 * b + 2, :].rearrange("p t (h d) -> p t h d", h=H)
                t0 = hb[0][:, :, :, :]
                u, v, z, acc, w = [hb[j][:, :, :, :] for j in range(1, 6)]
                mul, add, sub = ALU.mult, ALU.add, ALU.subtract
                base = 26 * i

                def op(o, i0, i1, f, last=None):
                    if last is not None:
                        after(dve, s["ham_step"], base + (last + 1))
                    nc.vector.tensor_tensor(o, i0, i1, f).then_inc(s["ham_step"], 1)

                after(dve, s["ham_done"], i)
                after(dve, s["cosd"], i + 1)
                op(t0, ext(1), ext(2), mul)
                op(u, B[1], C[1], mul)
                op(v, B[3], C[3], mul)
                op(acc, t0[:, :, 1:HW1, :], t0[:, :, 0:H, :], sub, 0)
                op(z, B[0], C[1], mul)
                op(u, u, v, add, 2)
                op(v, B[1], C[0], mul, 5)
                op(w, B[2], C[3], mul)
                op(acc, acc, u, sub)
                op(z, z, v, add, 6)
                op(u, B[3], C[2], mul, 8)
                op(v, B[0], C[2], mul, 9)
                after(dve, s["tp_pe"], g)
                op(to, A[0], acc, mul)
                op(acc, z, w, add, 12)
                op(z, B[1], C[3], mul, 13)
                op(w, B[2], C[0], mul)
                op(acc, acc, u, sub)
                op(v, v, z, sub, 14)
                op(u, B[3], C[1], mul, 16)
                op(acc, A[1], acc, mul)
                op(v, v, w, add, 17)
                after(dve, s["third_done"], i + 1)
                op(z, A[3], third[:, b, :, :, :], mul)
                op(to, to, acc, sub, 19)
                op(v, v, u, add, 20)
                op(to, to, z, sub, 22)
                op(v, A[2], v, mul, 23)
                dve.wait_ge(s["ham_step"], base + 26)
                nc.vector.tensor_tensor(to, to, v, sub).then_inc(s["ham_done"], 1)

            def step(n, k_of):
                parity = k_of % 2
                first_norm = isinstance(n, int) and n + 1 < NC
                if on(n + 1):
                    if first_norm:
                        dve.wait_ge(*((s["x_in0"], 16) if n < 0 else (s["x_rest"], 16 * (NC - 1))))
                        stats(n + 1, mv1, "var1")
                        dve.wait_ge(s["rs1_pool"], 2 * (n + 1) + 1)
                        norm(n + 1, lambda t: tile(n + 1, t), mv1, rs1)
                    stats(n + 1, mv1, "var1")
                if on(n - 3):
                    after(dve, s["rs2_pool"], n - 2)
                    after(dve, s["t1_pe"], min(n + 1, NG) if isinstance(n, int) else n + 1)
                    norm(n - 3, lambda t: xn[:, t, :], mv2, rs2, "ln2_done")
                if k_of == 3 and begins(n - 3):
                    after(dve, s["fc_w_hi"], (n - 3) // NC + 1)
                    nc.vector.tensor_tensor(fc_w[1][:, :, :], fc_whole[:, :, :], fc_w[0][:, :, :].bitcast(F32),
                                            ALU.subtract).then_inc(s["fc_w_lo"], 1)
                if on(n - 1):
                    hamilton(n - 1, 0, 1 - parity)
                if on(n - 4):
                    after(dve, s["mb_done"], n - 3)
                    add_banks(n - 4, 4, "res2", lambda b: after(dve, s["mm_pe"], 2 * (n - 4) + (b + 1)))
                if on(n - 2):
                    after(dve, s[f"filt_in{parity}"], 16 * ((n - 2) // 2 + 1))
                    after(dve, s["r_pe"], n - 1)
                    after(dve, s["g_pe"], n - 2)
                    for e in range(EH):
                        ins = nc.vector.tensor_tensor(
                            coef[:, e, :], bank[6 + e][:, :],
                            filt[:, parity, e, :], ALU.mult)
                    ins.then_inc(s["filt_dve"], 1)
                if on(n + 1):
                    after(dve, s["rs1_pool"], 2 * (n + 2) if first_norm else n + 2 + NC)
                    after(dve, s["t1_pe"], n + 1)
                    after(dve, s["t2_pe"], n - 2)
                    norm(n + 1, lambda t: xn[:, t, :], mv1, rs1, "ln1_done")
                if on(n - 1):
                    hamilton(n - 1, 1, 1 - parity)
                if k_of == NC - 1 and begins(n + 1):
                    after(dve, s["at_w_in"], 48 * ((n + 1) // NC + 1))
                    first = hb[1][:, :, :, :].rearrange("p t h d -> p (t h d)")[32:33, 0:W2]
                    nc.vector.tensor_copy(at_b[0:1, :], at_b_whole[0:1, :])
                    for j in range(2):
                        cols = slice(W2 * j, W2 * j + W2)
                        dve.drain()
                        nc.vector.tensor_copy(first.bitcast(F32R), at_b_whole[32:33, cols])
                        dve.drain()
                        ins = nc.vector.tensor_tensor(at_b[32:33, cols], at_b_whole[32:33, cols], first, ALU.subtract)
                    ins.then_inc(s["at_b_split"], 1)
                if on(n - 2):
                    after(dve, s["pb_done"], n - 1)
                    after(dve, s["g_pe"], n - 1)
                    add_banks(n - 2, 2, "res1", lambda b: None)
                    stats(n - 2, mv2, "var2")

            ones = hb[0][:, :, :, :].rearrange("p t h d -> p (t h d)")[0:33, 0:P]
            nc.vector.memset(ones, 0.0)
            nc.vector.memset(at_b_whole[0:33, :], 0.0)
            dve.drain()
            for p in (0, 32):
                nc.vector.memset(ones[p:p + 1, :], 1.0)
            nc.vector.tensor_copy(at_b[0:33, :], at_b_whole[0:33, :]).then_inc(s["cleared"], 1)
            dve.drain()
            nc.vector.tensor_copy(both[0:33, :], ones)
            steps(dve, step)


def tail(nc, d, out, x, ident, bank, order, filled):
    with ExitStack() as ctx:
        def sb(name, *shape):
            return ctx.enter_context(nc.sbuf_tensor(name, [P, *shape], F32))

        def shared(name, *shape):
            with nc.sbuf_tensor(name, [P, *shape], F32) as t:
                return t

        def sbr(name, *shape):
            return ctx.enter_context(nc.sbuf_tensor(name, [P, *shape], F32R))

        arena = shared("arena", NX // 2 * XW + NT * PAY)
        xt_hi = sbr("xt_hi_parts", NC, EH, CW)
        ew_lo = sbr("ew_lo_parts", EH, NX * E)
        uv_lo = sbr("uv_lo_parts", 2, EH, D1)
        sb("arena_gap0", NX // 2 * XW - NC * EH * CW - EH * NX * E - 2 * EH * D1)
        xt_lo = sbr("xt_lo_parts", NC, EH, CW)
        sb("arena_gap1", (NT - CT) * PAY - NC * EH * CW)
        uv_hi = sbr("uv_hi_parts", 2, EH, D1)
        sb("arena_gap2", CT * PAY - 2 * EH * D1)

        def whole(at, n, pattern, **sizes):
            return arena[:, at:at + n].rearrange(pattern, **sizes)

        xt_whole = whole(NX // 2 * XW, NC * EH * CW, "p (c k s) -> p c k s", c=NC, k=EH)
        xt = (xt_hi, xt_lo)
        a0 = EH * S
        ew_whole = whole(a0, EH * NX * E, "p (k x n) -> p k (x n)", k=EH, x=NX)
        a0 += EH * NX * E
        uv_whole = whole(a0, 2 * EH * D1, "p (w k n) -> p w k n", w=2, k=EH)
        uv = (uv_hi, uv_lo)
        ow = arena[:, a0 + 2 * EH * D1:a0 + 2 * EH * D1 + MC * E].rearrange("p (k n) -> p k n", k=MC)
        x0 = arena[:, NX // 2 * XW:NX // 2 * XW + NT * E].rearrange("p (c t e) -> p c t e", c=NC, t=CT)
        pay = arena[:, NX // 2 * XW:].rearrange("p (i w) -> p i w", w=PAY)
        w1 = arena[:, 0:NX * XW].rearrange("p (x w) -> p x w", x=NX)[:, :, 0:EH * F].rearrange("p x (k f) -> p x k f", k=EH)
        w2 = arena[:, 0:NX * XW].rearrange("p (x w) -> p x w", x=NX)[:, :, EH * F:].rearrange("p x (f n) -> p x f n", f=FC)
        eb = sb("eb", CT, E)
        ub = sb("ub", MC)
        vb = sb("vb", MC)
        tz = sb("tz", MC)
        ob = sb("ob", E)
        rw = sb("rw", 2, EH, NX)
        rb = sb("rb", 2, NX)
        prio = sb("prio", NX)
        lng = sb("lng", 2, EH)
        b1 = sb("b1", NX, FC)
        rt = shared("rt", 2, EH, CW)
        rt_hi = sbr("rt_hi_parts", 2, EH, CW)
        rows = sb("rows", 2, CT, E)
        hid = shared("hid2", FC, CW)
        ew_hi = sbr("ew_hi_parts", EH, NX * E)
        su, sv = hid[:, 0:MC, :], hid[:, MC:2 * MC, :]
        stat = sb("stat2", CT, 6)
        mv = sb("mv", NT, 2)
        ve = sb("ve2", NT)
        sc = [sb(f"sc{i}", NT) for i in range(5)]
        half = sb("half2", 3, NT)
        lg = sb("lg", NT, NX)
        ex = sb("ex", NT, NX)
        pick = sb("pick", NT, NX)
        mg = sb("mg", NT, NX)
        mx = sb("mx", NT)
        gate = sb("gate", NT)
        low = sb("low", P)
        ones = sb("ones", P)
        count = sb("count", NX)
        tiles = sb("tiles", NX)
        ends = [sb("ends0", NX), sb("ends1", NX)]
        owner = sb("owner", SLOTS)
        slot_no = sb("slot_no", SLOTS)
        token = sb("token", NT)
        dest = sb("dest", NT)
        dest_i = ctx.enter_context(nc.sbuf_tensor("dest_i", [P, NT], I32))
        toki = ctx.enter_context(nc.sbuf_tensor("toki", [P, 2], I32))
        owner_i = ctx.enter_context(nc.sbuf_tensor("owner_i", [1, SLOTS], I32))

        names = """x0_in0 x0_in1 x0_in2 x0_in3 x0_in4 x0_in5 x0_in6 x0_in7
            added ew_in rw_in at_in e2_in moments_a moments_b moments_c small_a small_b small_c rows_a rows_b rows_c
            ew_hi ew_lo xt_lo uv_hi uv_lo rt_lo turned_a turned_b turned_c evac_a evac_b evac_c
            logits eb_in zero picked expd mgt_pe mgt_act bias_pe bias_dve ex_pe ex_dve
            pool2 u_pe u_act prod o_pe o_dve ahead ob_done
            w_late w_in b2_in const_in ranks_pe dest_done owners sent n_in0 n_in1 r_in0 r_in1
            xs_pe xs_act hr_pe hr_dve ht_pe ht_act y_pe y_dve out0 out1 held3""".split()
        s = {n: ctx.enter_context(nc.semaphore("f_" + n)) for n in names}
        by_row = "b (c p t) e -> p (b c) t e"
        x_in = d["L0_attn_x"].rearrange(by_row, p=P, t=CT)
        out_rows = out.rearrange("b s e -> (b s) e")
        ew = (ew_hi, ew_lo)
        rt_whole = whole(EH * S + EH * CW, 2 * EH * CW, "p (b k n) -> p b k n", b=2, k=EH)
        rt_lo = ew_lo[:, :, :].rearrange("p k n -> p (k n)")[:, EH * CW:3 * EH * CW].rearrange("p (b k n) -> p b k n", b=2, k=EH)
        mgt = rt[:, 0, :, :].rearrange("p k n -> p (k n)")
        rt_c = arena[:, EH * S:EH * S + EH * CW].rearrange("p (k n) -> p k n", k=EH)
        h_rows = hid[:, 0:2, :].rearrange("p f n -> p (f n)")
        h_t = hid[:, 2:4, :].rearrange("p f n -> p (f n)").rearrange("p (f n) -> p f n", f=FC)
        xn_t = hid[:, 4, 0:EH * P].rearrange("p (k n) -> p k n", k=EH)
        y_b = hid[:, 5, 0:E]
        ge = hid[:, 6, 0:SLOTS * NX].rearrange("p (n x) -> p n x", x=NX)
        b2 = rt[:, :, :, :].rearrange("p a k n -> p (a k n)").rearrange("p (x e) -> p x e", x=NX)
        in_n = [rows[:, 0, b, :] for b in range(2)]
        in_r = [rows[:, b, 2:4, :].rearrange("p t e -> p (t e)")[:, 0:PAY - E] for b in range(2)]
        res = [rows[:, 1, b, :] for b in range(2)]
        tok = [toki[:, b:b + 1] for b in range(2)]
        xc = x[:, :, :].rearrange("p (c t) e -> p c t e", t=CT)

        def after(eng, what, value):
            if not isinstance(value, int) or value > 0:
                eng.wait_ge(what, value)

        def slots(eng, step):
            for n in range(-1, 4):
                step(n, n % 2, n // 2)
            with eng.Fori(2, SLOTS // 2 - 1) as pair:
                for b in range(2):
                    step(2 * pair + b, b, pair)
            for n in range(SLOTS - 2, SLOTS + 1):
                step(n, n % 2, n // 2)

        block = ctx.enter_context(nc.Block())

        def load(eng, e, done):
            eng.dma_start(w1[:, e, :, :], d["L1_ffn_W1"][e].rearrange("(k p) f -> p k f", p=P)).then_inc(s[done], 16)
            eng.dma_start(w2[:, e, :, :], d["L1_ffn_W2"][e].rearrange("(k p) f -> p k f", p=P)).then_inc(s[done], 16)

        @block.sync
        def _(sp):
            for c in range(NC):
                sp.dma_start(x0[:, c], x_in[:, c]).then_inc(s[f"x0_in{c}"], 16)
            for i, (w, b) in enumerate((("L0_ffn_router_w", "L0_ffn_router_b"), ("L1_ffn_Wr", "L1_ffn_br"))):
                sp.dma_start(rw[:, i, :, :], d[w].rearrange("(k p) n -> p k n", p=P)).then_inc(s["rw_in"], 16)
                sp.dma_start(rb[:, i, :], d[b].partition_broadcast(P)).then_inc(s["rw_in"], 16)
            sp.dma_start(prio[:, :], d["c_prio"].partition_broadcast(P)).then_inc(s["rw_in"], 16)
            for k in range(EH):
                sp.dma_start(ew_whole[:, k, :].rearrange("p (x n) -> p x n", x=NX),
                             d["L0_ffn_expert_w"][:, k * P:(k + 1) * P, :].rearrange("x p n -> p x n")).then_inc(s["ew_in"], 16)
            sp.wait_ge(s["zero"], 1)
            for t in range(CT):
                sp.dma_start(eb[NX * t:NX * t + NX, t, :], d["L0_ffn_expert_b"]).then_inc(s["eb_in"], 16)
            for to, name in ((uv_whole[:, 0], "L1_attn_u_w"), (uv_whole[:, 1], "L1_attn_v_w"), (ow, "L1_attn_o_w")):
                sp.dma_start(to[:, :, :], d[name].rearrange("(k p) n -> p k n", p=P)).then_inc(s["at_in"], 16)
            for to, name in ((ub, "L1_attn_u_b"), (vb, "L1_attn_v_b")):
                sp.dma_start(to[:, :], d[name].rearrange("(k p) -> p k", p=P), allow_slow_non_contiguous=True).then_inc(s["at_in"], 16)
            heads = d["L1_attn_t_zero"].rearrange("(m h) o -> h (m o)", h=2)
            for h in range(2):
                sp.dma_start(tz[64 * h:64 * h + 64, :], heads[h].partition_broadcast(64), allow_slow_non_contiguous=True).then_inc(s["at_in"], 16)
            sp.dma_start(ob[:, :], d["L1_attn_o_b"].partition_broadcast(P)).then_inc(s["at_in"], 16)
            for i, name in enumerate(("L1_ffn_ln_g", "L1_ffn_ln_b")):
                sp.dma_start(lng[:, i, :], d[name].rearrange("(k p) -> p k", p=P), allow_slow_non_contiguous=True).then_inc(s["e2_in"], 16)
            sp.dma_start(b1[:, :, :], d["L1_ffn_b1"].rearrange("x (f p) -> p x f", p=P), allow_slow_non_contiguous=True).then_inc(s["e2_in"], 16)
            sp.dma_start(low[:, :], d["c_low"]).then_inc(s["const_in"], 16)
            sp.dma_start(slot_no[:, :], d["c_slot"].partition_broadcast(P)).then_inc(s["const_in"], 16)
            sp.dma_start(token[:, :], d["c_token"]).then_inc(s["const_in"], 16)
            sp.wait_ge(s["ex_pe"], NT)
            for e in range(NX // 2):
                if e == 2:
                    sp.wait_ge(s["o_pe"], NC)
                    sp.wait_ge(s["logits"], 2 * NC)
                load(sp, e, "w_in")
                sp.wait_ge(s["w_in"], 32 * (e + 1))
            sp.dma_start(b2, d["L1_ffn_b2"].rearrange("x e -> (x e)").partition_broadcast(P)).then_inc(s["b2_in"], 16)

            def fetch(n, b, first):
                if not first:
                    sp.wait_ge(s["xs_pe"], n - 1)
                    sp.sem_inc(s["held3"], 1)
                sp.dma_start(in_n[b], order[bass.ds(P * n, P), 0:E]).then_inc(s[f"n_in{b}"], 16)
                if not first:
                    sp.wait_ge(s["y_dve"], n - 1)
                    sp.sem_inc(s["held3"], 1)
                sp.dma_start(in_r[b], order[bass.ds(P * n, P), E:PAY]).then_inc(s[f"r_in{b}"], 16)

            sp.wait_ge(s["sent"], 16 * NT)
            fetch(0, 0, True)
            fetch(1, 1, True)
            with sp.Fori(1, SLOTS // 2) as pair:
                for b in range(2):
                    fetch(2 * pair + b, b, False)

        @block.tensor
        def _(pe):
            def turn(kind, c, of):
                pe.wait_ge(s["rows_" + kind], c + 1)
                before = {"a": [("a", c)], "b": [("a", NC), ("b", c), ("c", c - 3)],
                          "c": [("b", min(c + 4, NC)), ("c", c)]}[kind]
                for other, count in before:
                    after(pe, s["evac_" + other], count)
                for e in range(EH):
                    for t in range(CT):
                        mm = pe.transpose(bank[e][:, t * P:(t + 1) * P], of(t)[:, e * P:(e + 1) * P], ident[:, :])
                mm.then_inc(s["turned_" + kind], 1)

            def route(i, c, of):
                pe.wait_ge(s["evac_" + "ac"[i]], c + 1)
                for t in range(CT):
                    for k in range(EH):
                        mm = pe.matmul(bank[2 if i == 0 else 5][:, NX * (CT * c + t):NX * (CT * c + t + 1)],
                                       of[:, k, t * P:(t + 1) * P], rw[:, i, k, :], start=(k == 0), stop=(k == EH - 1))
                mm.then_inc(s["logits"], 1)

            def biases():
                pe.wait_ge(s["picked"], 1)
                for c in range(NC):
                    mm = pe.transpose(bank[c // 4][0:NX * CT, P * (c % 4):P * (c % 4 + 1)],
                                      mg[:, CT * c:CT * c + CT, :].rearrange("p t x -> p (t x)"), ident[:, :])
                mm.then_inc(s["mgt_pe"], 1)
                pe.wait_ge(s["mgt_act"], 1)
                for c in range(NC):
                    if c > 2:
                        pe.wait_ge(s["bias_dve"], c - 2)
                    for t in range(CT):
                        mm = pe.matmul(bank[2 + 2 * (c % 3) + t // 2][:, (t % 2) * E:(t % 2 + 1) * E],
                                       mgt[0:NX * CT, P * c:P * c + P], eb[0:NX * CT, t, :], start=True, stop=True)
                    mm.then_inc(s["bias_pe"], 1)

            pe.wait_ge(s["rw_in"], 16 * 5)
            for c in range(NC):
                turn("a", c, lambda t: rows[:, c % 2, t, :])
                if c:
                    route(0, c - 1, xt_whole[:, c - 1])
            route(0, NC - 1, xt_whole[:, NC - 1])
            pe.wait_ge(s["eb_in"], 16 * CT)
            biases()
            pe.wait_ge(s["ew_lo"], 1)
            pe.wait_ge(s["bias_dve"], NC)
            for i in range(NT):
                if i % CT == 0:
                    pe.wait_ge(s["xt_lo"], i // CT + 1)
                if i > 1:
                    pe.wait_ge(s["ex_dve"], i - 1)
                for q in range(4):
                    to, cols = bank[4 * (i % 2) + q][:, :], slice(512 * q, 512 * q + 512)
                    for k in range(EH):
                        a = [part[:, i // CT, k, P * (i % CT):P * (i % CT + 1)] for part in xt]
                        w = [part[:, k, cols] for part in ew]
                        pe.matmul(to, a[0], w[0], start=(k == 0), stop=False)
                        pe.matmul(to, a[0], w[1], start=False, stop=False)
                        mm = pe.matmul(to, a[1], w[0], start=False, stop=(k == EH - 1))
                mm.then_inc(s["ex_pe"], 1)
            pe.wait_ge(s["at_in"], 16 * 8)
            pe.wait_ge(s["uv_lo"], 1)
            pe.wait_ge(s["ex_dve"], NT)

            def project(c):
                pe.wait_ge(s["prod"], c + 1)
                if c:
                    pe.wait_ge(s["o_dve"], c)
                for t in range(CT):
                    for m in range(MC):
                        mm = pe.matmul(bank[6 + t // 2][:, (t % 2) * E:(t % 2 + 1) * E], su[:, m, t * P:(t + 1) * P],
                                       ow[:, m, :], start=(m == 0), stop=(m == MC - 1))
                mm.then_inc(s["o_pe"], 1)

            def route_c(c):
                turn("c", c, lambda t: pay[:, CT * c + t, 0:E])
                route(1, c, rt_c)

            for c in range(NC):
                turn("b", c, lambda t: rows[:, c % 2, t, :])
                if c:
                    project(c - 1)
                pe.wait_ge(s["rt_lo"], c + 1)
                for m in range(MC):
                    for j in range(2):
                        q = 2 * m + j
                        n = 8 * c + q
                        if n >= 3:
                            pe.wait_ge(s["u_act"], n - 2)
                        to = bank[2 + n % 3][:, :]
                        for k in range(EH):
                            w = [part[:, j, k, m * P:(m + 1) * P] for part in uv]
                            a = [part[:, c % 2, k, :] for part in (rt_hi, rt_lo)]
                            pe.matmul(to, w[0], a[0], start=(k == 0), stop=False)
                            pe.matmul(to, w[0], a[1], start=False, stop=False)
                            mm = pe.matmul(to, w[1], a[0], start=False, stop=(k == EH - 1))
                        mm.then_inc(s["u_pe"], 1)
                if c > 2:
                    route_c(c - 3)
            route_c(NC - 3)
            project(NC - 1)
            route_c(NC - 2)
            route_c(NC - 1)
            pe.wait_ge(s["picked"], 2)
            pe.wait_ge(s["const_in"], 48)
            pe.wait_ge(s["u_act"], 8 * NC)
            pe.wait_ge(s["o_dve"], NC)
            picked = pick[:, :, :].rearrange("p t x -> p (t x)")
            pe.matmul(bank[4][:, 0:NT * NX], low[:, :], picked, start=True, stop=True)
            pe.matmul(bank[3][:, 0:NT * NX], ones[:, :], picked, start=True, stop=True).then_inc(s["ranks_pe"], 1)

            def expert(n):
                return pe.value_load(owner_i[0:1, bass.ds(n, 1)], min_val=0, max_val=NX - 1)

            def step(n, b, pair):
                up = not isinstance(n, int) or 0 <= n < SLOTS
                down = not isinstance(n, int) or n > 0
                if up:
                    e = expert(n)
                if down:
                    e_down = expert(n - 1)
                if up:
                    after(pe, s["xs_act"], n + 1)
                    after(pe, s["w_in"], 32 * (e + 1))
                    after(pe, s["hr_dve"], n)
                    for q in range(2):
                        for k in range(EH):
                            mm = pe.matmul(bank[1 + q][:, :], xn_t[:, k, :],
                                           w1[:, bass.ds(e, 1), k, 512 * q:512 * q + 512].rearrange("p x f -> p (x f)"),
                                           start=(k == 0), stop=(k == EH - 1))
                    mm.then_inc(s["hr_pe"], 1)
                if not isinstance(n, int) or n + 1 < SLOTS:
                    after(pe, s[f"n_in{1 - b}"], 16 * (pair + (b + 1)))
                    after(pe, s["xs_act"], n + 1)
                    for k in range(EH):
                        mm = pe.transpose(bank[0][:, k * P:(k + 1) * P], in_n[1 - b][:, k * P:(k + 1) * P], ident[:, :])
                    mm.then_inc(s["xs_pe"], 1)
                if down:
                    after(pe, s["ht_act"], n)
                    after(pe, s["y_dve"], n - 1)
                    for f in range(FC):
                        mm = pe.matmul(bank[5][:, 0:E], h_t[:, f, :], w2[:, bass.ds(e_down, 1), f, :].rearrange("p x n -> p (x n)"),
                                       start=(f == 0), stop=(f == FC - 1))
                    mm.then_inc(s["y_pe"], 1)
                if up:
                    after(pe, s["hr_dve"], n + 1)
                    after(pe, s["ht_act"], n)
                    for f in range(FC):
                        mm = pe.transpose(bank[3 + f // 4][:, (f % 4) * P:(f % 4 + 1) * P], h_rows[:, f * P:(f + 1) * P], ident[:, :])
                    mm.then_inc(s["ht_pe"], 1)

            pe.wait_ge(s["owners"], 1)
            slots(pe, step)

        @block.scalar
        def _(act):
            def evac(kind, c, *to):
                act.wait_ge(s["turned_" + kind], c + 1)
                for e in range(EH):
                    for place in to:
                        ins = nc.scalar.activation(place[:, e, :], bank[e][:, :], ACT.Copy)
                ins.then_inc(s["evac_" + kind], 1)

            def softmax(i):
                act.wait_ge(s["expd"], 2 * i + 1)
                nc.scalar.activation(ex[:, :, :], lg[:, :, :], ACT.Exp).then_inc(s["expd"], 1)

            for c in range(NC):
                act.wait_ge(s["added"], c + 1)
                evac("a", c, xt_hi[:, c], xt_whole[:, c])
                if c == 3:
                    act.wait_ge(s["ew_in"], 32)
                    nc.scalar.activation(ew_hi[:, :, :], ew_whole, ACT.Copy).then_inc(s["ew_hi"], 1)
            softmax(0)
            act.wait_ge(s["mgt_pe"], 1)
            for b in range(2):
                ins = nc.scalar.activation(mgt[0:NX * CT, 512 * b:512 * b + 512], bank[b][0:NX * CT, :], ACT.Copy)
            ins.then_inc(s["mgt_act"], 1)
            act.wait_ge(s["at_in"], 16 * 8)
            act.wait_ge(s["added"], NC)
            nc.scalar.activation(uv_hi[:, :, :, :], uv_whole, ACT.Copy).then_inc(s["uv_hi"], 1)
            act.wait_ge(s["ex_pe"], NT)
            act.wait_ge(s["bias_pe"], NC)

            def evac_c(c):
                if c:
                    act.wait_ge(s["logits"], NC + c)
                evac("c", c, rt_c)

            for c in range(NC):
                if c > 1:
                    act.wait_ge(s["u_pe"], 8 * (c - 1))
                evac("b", c, rt_hi[:, c % 2], rt_whole[:, c % 2])
                for q in range(8):
                    if q == 0 and c:
                        act.wait_ge(s["o_pe"], c)
                    act.wait_ge(s["u_pe"], 8 * c + q + 1)
                    to, b = ((su, ub), (sv, vb))[q % 2]
                    nc.scalar.activation(to[:, q // 2, :], bank[2 + (8 * c + q) % 3][:, :], ACT.Silu,
                                         bias=b[:, q // 2:q // 2 + 1]).then_inc(s["u_act"], 1)
                if c > 2:
                    evac_c(c - 3)
            for c in range(NC - 3, NC):
                evac_c(c)
            act.wait_ge(s["e2_in"], 48)
            softmax(1)

            def step(n, b, pair):
                if not isinstance(n, int) or n + 1 < SLOTS:
                    after(act, s["xs_pe"], n + 2)
                    after(act, s["hr_pe"], n + 1)
                    for k in range(EH):
                        ins = nc.scalar.activation(xn_t[:, k, :], bank[0][:, k * P:(k + 1) * P], ACT.Identity,
                                                   bias=lng[:, 1, k:k + 1], scale=lng[:, 0, k:k + 1])
                    ins.then_inc(s["xs_act"], 1)
                if not isinstance(n, int) or 0 <= n < SLOTS:
                    e = act.value_load(owner_i[0:1, bass.ds(n, 1)], min_val=0, max_val=NX - 1)
                    after(act, s["ht_pe"], n + 1)
                    after(act, s["y_pe"], n)
                    for f in range(FC):
                        ins = nc.scalar.activation(h_t[:, f, :], bank[3 + f // 4][:, (f % 4) * P:(f % 4 + 1) * P], ACT.Relu,
                                                   bias=b1[:, bass.ds(e, 1), f])
                    ins.then_inc(s["ht_act"], 1)

            act.wait_ge(s["owners"], 1)
            act.wait_ge(s["o_pe"], NC)
            slots(act, step)

        @block.gpsimd
        def _(pool):
            k = s["pool2"]
            done_so_far = [0]

            def done(ins):
                ins.then_inc(k, 1)
                done_so_far[0] += 1
                pool.wait_ge(k, done_so_far[0])

            def power(o, a, which):
                done(nc.gpsimd.tensor_tensor(o, a, which, ALU.pow))

            def plus(o, a, v):
                done(nc.gpsimd.tensor_scalar(o, a, v, 0.0, ALU.add, ALU.add))

            def times(o, a, b):
                done(nc.gpsimd.tensor_tensor(o, a, b, ALU.mult))

            for i, v in enumerate((-0.5, 0.5, -1.0)):
                done(nc.gpsimd.memset(half[:, i, :], v))
            done(nc.gpsimd.memset(ones[:, :], 1.0))
            nc.gpsimd.memset(eb[:, :, :], 0.0).then_inc(s["zero"], 1)

            def add_in(c):
                pool.wait_ge(s[f"x0_in{c}"], 16)
                nc.gpsimd.tensor_tensor(xc[:, c], xc[:, c], x0[:, c], ALU.add).then_inc(s["added"], 1)

            def small(kind, c):
                now = slice(CT * c, CT * c + CT)
                var, mean = mv[:, now, 1], mv[:, now, 0]
                v = ve[:, now]
                rstd, t, a, b, ir = [q[:, now] for q in sc]
                pool.wait_ge(s["moments_" + kind], c + 1)
                plus(v, var, EPS)
                if kind == "a":
                    last = nc.gpsimd.tensor_tensor(rstd, v, half[:, 0, now], ALU.pow)
                elif kind == "b":
                    power(rstd, v, half[:, 0, now])
                    power(t, var, half[:, 1, now])
                    times(t, t, rstd)
                    plus(t, t, 1e-8)
                    power(t, t, half[:, 2, now])
                    times(t, t, rstd)
                    plus(a, rstd, 1.0)
                    times(b, rstd, mean)
                    last = nc.gpsimd.tensor_scalar(b, b, -1.0, 1.0, ALU.mult, ALU.mult)
                else:
                    power(rstd, v, half[:, 0, now])
                    times(v, rstd, rstd)
                    times(v, v, var)
                    plus(v, v, EPS)
                    power(t, v, half[:, 0, now])
                    times(t, t, rstd)
                    last = nc.gpsimd.tensor_tensor(ir, v, half[:, 1, now], ALU.pow)
                last.then_inc(s["small_" + kind], 1)

            def add_ob(c):
                pool.wait_ge(s["ahead"], c + 1)
                nc.gpsimd.tensor_tensor(xc[:, c], xc[:, c], ob[:, :].unsqueeze(1).broadcast_to([P, CT, E]),
                                        ALU.add).then_inc(s["ob_done"], 1)

            add_in(0)
            for c in range(NC):
                if c + 1 < NC:
                    add_in(c + 1)
                small("a", c)

            def rest(to, whole, first):
                return nc.gpsimd.tensor_tensor(to, whole, first, ALU.subtract)

            pool.wait_ge(s["ew_hi"], 1)
            rest(ew_lo[:, :, :], ew_whole, ew_hi[:, :, :].bitcast(F32)).then_inc(s["ew_lo"], 1)
            pool.wait_ge(s["uv_hi"], 1)
            rest(uv_lo[:, :, :, :], uv_whole, uv_hi[:, :, :, :].bitcast(F32)).then_inc(s["uv_lo"], 1)
            for c in range(NC):
                small("b", c)
            pool.wait_ge(s["at_in"], 16 * 8)
            add_ob(0)
            for c in range(NC):
                if c + 1 < NC:
                    add_ob(c + 1)
                small("c", c)
            pool.wait_ge(filled, 16 * SLOTS)
            pool.wait_ge(s["dest_done"], 1)
            for i in range(NT):
                nc.gpsimd.indirect_dma_start(order, bass.IndirectOffsetOnAxis(dest_i[:, i:i + 1], 0), pay[:, i, :], None,
                                             bounds_check=SLOTS * P - 1, oob_is_err=False).then_inc(s["sent"], 16)
            pool.wait_ge(s["sent"], 16 * NT)
            pool.wait_ge(s["w_in"], 32 * (NX // 2))
            for e in range(NX // 2, NX):
                load(pool, e, "w_late")
                pool.wait_ge(s["w_late"], 32 * (e - NX // 2 + 1))
                pool.sem_inc(s["w_in"], 32)

            def step(n, b, pair):
                if isinstance(n, int) and not 0 < n <= SLOTS:
                    return
                pool.wait_ge(s["y_dve"], n)
                if not isinstance(n, int):
                    pool.sem_inc(s["held3"], 1)
                nc.gpsimd.indirect_dma_start(out_rows, bass.IndirectOffsetOnAxis(tok[1 - b], 0), res[1 - b], None,
                                             bounds_check=S - 1, oob_is_err=False).then_inc(s[f"out{1 - b}"], 16)

            slots(pool, step)
            for b in range(2):
                pool.wait_ge(s[f"out{b}"], 16 * (SLOTS // 2))

        @block.vector
        def _(dve):
            V = nc.vector

            def stats(c, of=lambda i: x[:, i, :]):
                dve.drain()
                for t in range(CT):
                    V.bn_stats(stat[:, t, :], of(CT * c + t))
                dve.drain()
                for t in range(CT):
                    ins = V.bn_aggr(mv[:, CT * c + t, :], stat[:, t, :])
                return ins

            def norm(kind, c, scale):
                dve.wait_ge(s["small_" + kind], c + 1)
                if kind == "a":
                    after(dve, s["turned_a"], c - 1)
                else:
                    dve.wait_ge(s["turned_a"], NC)
                    after(dve, s["turned_b"], c - 1)
                for t in range(CT):
                    i = CT * c + t
                    ins = V.tensor_scalar(rows[:, c % 2, t, :], x[:, i, :], mv[:, i, 0:1], scale[:, i:i + 1],
                                          ALU.subtract, ALU.mult)
                ins.then_inc(s["rows_" + kind], 1)

            def choose(i):
                dve.wait_ge(s["logits"], NC * (i + 1))
                if i:
                    V.tensor_tensor(lg[:, :, :], bank[5][:, 0:NT * NX].rearrange("p (t x) -> p t x", x=NX),
                                    sc[4][:, :].unsqueeze(2).broadcast_to([P, NT, NX]), ALU.mult)
                    dve.drain()
                    V.tensor_tensor(lg[:, :, :], lg[:, :, :], rb[:, i, :].unsqueeze(1).broadcast_to([P, NT, NX]), ALU.add)
                else:
                    V.tensor_tensor(lg[:, :, :], bank[2][:, 0:NT * NX].rearrange("p (t x) -> p t x", x=NX),
                                    rb[:, i, :].unsqueeze(1).broadcast_to([P, NT, NX]), ALU.add)
                dve.drain()
                V.tensor_reduce(mx[:, :], lg[:, :, :], AX_X, ALU.max)
                dve.drain()
                V.tensor_tensor(lg[:, :, :], lg[:, :, :], mx[:, :].unsqueeze(2).broadcast_to([P, NT, NX]), ALU.subtract).then_inc(s["expd"], 1)
                dve.drain()
                V.tensor_scalar(pick[:, :, :], lg[:, :, :], 0.0, None, ALU.is_ge)
                dve.drain()
                V.tensor_tensor(pick[:, :, :], pick[:, :, :], prio[:, :].unsqueeze(1).broadcast_to([P, NT, NX]), ALU.mult)
                dve.drain()
                V.tensor_reduce(mx[:, :], pick[:, :, :], AX_X, ALU.max)
                dve.drain()
                V.tensor_tensor(pick[:, :, :], pick[:, :, :], mx[:, :].unsqueeze(2).broadcast_to([P, NT, NX]), ALU.is_equal)
                dve.wait_ge(s["expd"], 2 * i + 2)
                V.tensor_reduce(gate[:, :], ex[:, :, :], AX_X, ALU.add)
                dve.drain()
                V.reciprocal(gate[:, :], gate[:, :])
                dve.drain()
                V.tensor_tensor(mg[:, :, :], pick[:, :, :], gate[:, :].unsqueeze(2).broadcast_to([P, NT, NX]), ALU.mult).then_inc(s["picked"], 1)

            def add(c, b0):
                for b in range(2):
                    part = xc[:, c, 2 * b:2 * b + 2, :].rearrange("p t e -> p (t e)")
                    ins = V.tensor_tensor(part, part, bank[b0 + b][:, :], ALU.add)
                return ins

            def moments(c):
                dve.wait_ge(s["added"], c + 1)
                stats(c).then_inc(s["moments_a"], 1)

            moments(0)
            for c in range(NC):
                if c + 1 < NC:
                    moments(c + 1)
                norm("a", c, sc[0])
            dve.wait_ge(s["rw_in"], 80)
            choose(0)

            def split_rows(c):
                V.tensor_tensor(xt_lo[:, c], xt_whole[:, c], xt_hi[:, c].bitcast(F32), ALU.subtract).then_inc(s["xt_lo"], 1)

            split_rows(0)
            split_rows(1)
            for c in range(NC):
                dve.wait_ge(s["bias_pe"], c + 1)
                add(c, 2 + 2 * (c % 3)).then_inc(s["bias_dve"], 1)

            def norm_b(c):
                norm("b", c, sc[1])
                for t in range(CT):
                    i = CT * c + t
                    ins = V.tensor_scalar(x[:, i, :], x[:, i, :], sc[2][:, i:i + 1], sc[3][:, i:i + 1], ALU.mult, ALU.add)
                ins.then_inc(s["ahead"], 1)

            def gated(c):
                dve.wait_ge(s["u_act"], 8 * (c + 1))
                for m in range(MC):
                    ins = V.scalar_tensor_tensor(out=su[:, m, :], in0=sv[:, m, :], scalar=tz[:, m:m + 1], in1=su[:, m, :],
                                                 op0=ALU.mult, op1=ALU.mult)
                ins.then_inc(s["prod"], 1)

            def result(c):
                dve.wait_ge(s["ob_done"], c + 1)
                dve.wait_ge(s["o_pe"], c + 1)
                for b in range(2):
                    a = CT * c + 2 * b
                    ins = V.tensor_tensor(pay[:, a:a + 2, E:2 * E], x[:, a:a + 2, :],
                                          bank[6 + b][:, :].rearrange("p (t e) -> p t e", t=2), ALU.add)
                ins.then_inc(s["o_dve"], 1)
                stats(c, lambda i: pay[:, i, E:2 * E]).then_inc(s["moments_c"], 1)

            def norm_c(c):
                dve.wait_ge(s["small_c"], c + 1)
                for t in range(CT):
                    i = CT * c + t
                    ins = V.tensor_scalar(pay[:, i, 0:E], pay[:, i, E:2 * E], mv[:, i, 0:1], sc[1][:, i:i + 1],
                                          ALU.subtract, ALU.mult)
                ins.then_inc(s["rows_c"], 1)

            for i in range(NT):
                if i % CT == 0 and i // CT + 2 < NC:
                    split_rows(i // CT + 2)
                dve.wait_ge(s["ex_pe"], i + 1)
                for e in range(NX):
                    dve.drain()
                    ins = V.scalar_tensor_tensor(out=x[:, i, :], in0=bank[4 * (i % 2) + e // 2][:, (e % 2) * E:(e % 2 + 1) * E],
                                                 scalar=mg[:, i, e:e + 1], in1=x[:, i, :], op0=ALU.mult, op1=ALU.add)
                ins.then_inc(s["ex_dve"], 1)
                if i % CT == CT - 1:
                    stats(i // CT).then_inc(s["moments_b"], 1)
                if i == 2 * CT - 1:
                    norm_b(0)
            dve.wait_ge(s["at_in"], 16 * 8)

            for c in range(NC):
                dve.wait_ge(s["evac_b"], c + 1)
                V.tensor_tensor(rt_lo[:, c % 2], rt_whole[:, c % 2], rt_hi[:, c % 2].bitcast(F32), ALU.subtract).then_inc(s["rt_lo"], 1)
                if c + 1 < NC:
                    norm_b(c + 1)
                if c:
                    result(c - 1)
                if c > 1:
                    norm_c(c - 2)
                gated(c)
            result(NC - 1)
            norm_c(NC - 2)
            norm_c(NC - 1)
            choose(1)
            dve.wait_ge(s["const_in"], 48)
            V.tensor_copy(pay[:, :, 2 * E:2 * E + 1], gate[:, :].unsqueeze(2))
            V.tensor_copy(pay[:, :, 2 * E + 1:2 * E + 2], token[:, :].unsqueeze(2))
            V.memset(pay[:, :, 2 * E + 2:PAY], 0.0)
            dve.wait_ge(s["ranks_pe"], 1)
            per_tile = bank[3][:, 0:NT * NX].rearrange("p (t x) -> p t x", x=NX)
            V.memset(lg[:, 0:1, :], 0.0)
            V.tensor_copy(lg[:, 1:NT, :], per_tile[:, 0:NT - 1, :])
            dve.drain()
            a, b = lg, ex
            for sh in (1, 2, 4, 8, 16):
                V.tensor_copy(b[:, 0:sh, :], a[:, 0:sh, :])
                V.tensor_tensor(b[:, sh:NT, :], a[:, sh:NT, :], a[:, 0:NT - sh, :], ALU.add)
                dve.drain()
                a, b = b, a
            V.tensor_tensor(count[:, :], a[:, NT - 1, :], per_tile[:, NT - 1, :], ALU.add)
            V.tensor_tensor(b[:, :, :], a[:, :, :], bank[4][:, 0:NT * NX].rearrange("p (t x) -> p t x", x=NX), ALU.add)
            dve.drain()
            V.tensor_scalar(tiles[:, :], count[:, :], 1.0 / P, 0.5 - 1.0 / (2 * P), ALU.mult, ALU.add)
            dve.drain()
            V.tensor_scalar(tiles[:, :], tiles[:, :], ROUND, ROUND, ALU.add, ALU.subtract)
            dve.drain()
            u, v = tiles, ends[0]
            for sh in (1, 2, 4):
                V.tensor_copy(v[:, 0:sh], u[:, 0:sh])
                V.tensor_tensor(v[:, sh:NX], u[:, sh:NX], u[:, 0:NX - sh], ALU.add)
                dve.drain()
                u, v = v, (ends[1] if v is ends[0] else ends[0])
            end = u
            V.tensor_tensor(v[:, :], end[:, :], tiles[:, :], ALU.subtract)
            V.tensor_tensor(ge[:, :, :], slot_no[:, :].unsqueeze(2).broadcast_to([P, SLOTS, NX]),
                            end[:, :].unsqueeze(1).broadcast_to([P, SLOTS, NX]), ALU.is_ge)
            dve.drain()
            V.tensor_scalar(v[:, :], v[:, :], float(P), 0.0, ALU.mult, ALU.add)
            V.tensor_reduce(owner[:, :], ge[:, :, :], AX_X, ALU.add)
            dve.drain()
            V.tensor_scalar(owner[:, :], owner[:, :], float(NX - 1), None, ALU.min)
            V.tensor_tensor(b[:, :, :], b[:, :, :], v[:, :].unsqueeze(1).broadcast_to([P, NT, NX]), ALU.add)
            dve.drain()
            V.tensor_copy(owner_i[:, :], owner[0:1, :]).then_inc(s["owners"], 1)
            V.tensor_tensor(b[:, :, :], b[:, :, :], pick[:, :, :], ALU.mult)
            dve.drain()
            V.tensor_reduce(dest[:, :], b[:, :, :], AX_X, ALU.add)
            dve.drain()
            V.tensor_copy(dest_i[:, :], dest[:, :]).then_inc(s["dest_done"], 1)

            def step(n, b, pair):
                if not isinstance(n, int) or 0 <= n < SLOTS:
                    after(dve, s["hr_pe"], n + 1)
                    after(dve, s["ht_pe"], n)
                    for q in range(2):
                        ins = V.tensor_copy(h_rows[:, 512 * q:512 * q + 512], bank[1 + q][:, :])
                    ins.then_inc(s["hr_dve"], 1)
                if isinstance(n, int) and not 0 < n <= SLOTS:
                    return
                e = dve.value_load(owner_i[0:1, bass.ds(n - 1, 1)], min_val=0, max_val=NX - 1)
                b = 1 - b
                after(dve, s["y_pe"], n)
                V.tensor_tensor(y_b, bank[5][:, 0:E], b2[:, bass.ds(e, 1), :].rearrange("p x e -> p (x e)"), ALU.add)
                after(dve, s[f"r_in{b}"], 16 * (pair + (1 - b)))
                after(dve, s[f"out{b}"], 16 * (pair - b))
                V.tensor_copy(tok[b], in_r[b][:, E + 1:E + 2])
                dve.drain()
                V.scalar_tensor_tensor(out=res[b], in0=y_b, scalar=in_r[b][:, E:E + 1], in1=in_r[b][:, 0:E],
                                       op0=ALU.mult, op1=ALU.add).then_inc(s["y_dve"], 1)

            dve.wait_ge(s["b2_in"], 16)
            slots(dve, step)


def program(nc, d, out):
    with ExitStack() as ctx:
        x = ctx.enter_context(nc.sbuf_tensor("x", [P, NT, E], F32))
        ident = ctx.enter_context(nc.sbuf_tensor("ident", [P, P], F32))
        bank = [ctx.enter_context(nc.psum_tensor(f"bank{i}", [P, 512], F32)) for i in range(8)]
        order = nc.dram_tensor("order", [SLOTS * P, PAY], F32).ap()
        filled = ctx.enter_context(nc.semaphore("filled"))
        attention(nc, d, x, ident, bank, order, filled)
        tail(nc, d, out, x, ident, bank, order, filled)


_INS = ["L0_attn_x", "L0_attn_ln1_w", "L0_attn_ln1_b", "L0_attn_attn_w", "L0_attn_attn_b", "L0_attn_aproj_w",
        "L0_attn_aproj_b", "L0_attn_ln2_w", "L0_attn_ln2_b", "L0_attn_fc_w", "L0_attn_fc_b", "L0_attn_mproj_w",
        "L0_attn_mproj_b", "L0_ffn_router_w", "L0_ffn_router_b", "L0_ffn_expert_w", "L0_ffn_expert_b",
        "L1_attn_u_w", "L1_attn_u_b", "L1_attn_v_w", "L1_attn_v_b", "L1_attn_o_w", "L1_attn_o_b",
        "L1_attn_t_zero", "L1_ffn_Wr", "L1_ffn_br", "L1_ffn_ln_g", "L1_ffn_ln_b", "L1_ffn_W1", "L1_ffn_b1",
        "L1_ffn_W2", "L1_ffn_b2"]
_TURNED = ["L1_attn_u_w", "L1_attn_v_w", "L1_attn_o_w"]
_SHAPE = (1, S, E)


def kernel(**inputs):
    import numpy as _np
    import concourse.bacc as _bacc
    from concourse.bass_utils import run_bass_kernel_spmd as _run

    nc = _bacc.Bacc("TRN2", target_bir_lowering=False, num_devices=1)
    arrays, aps = {}, {}
    for name in _INS:
        a = _np.asarray(inputs[name])
        arrays[name] = _np.ascontiguousarray(a.T if name in _TURNED else a)
    arrays.update(shape_constants())
    for name, a in arrays.items():
        aps[name] = nc.dram_tensor(name, a.shape, mybir.dt.from_np(a.dtype), kind="ExternalInput").ap()
    out = nc.dram_tensor("out", _SHAPE, F32, kind="ExternalOutput").ap()
    program(nc, aps, out)
    r = _run(nc, [arrays], core_ids=[0])
    return r.results[0]["out"]
```
